# Optimizing a Trainium2 kernel written in Bass

```python
import numpy as np
import jax
import jax.numpy as jnp

def _softmax(x, axis=-1):
    return jax.nn.softmax(x, axis=axis)

def _gelu(x):
    return jax.nn.gelu(x, approximate=True)

def _silu(x):
    return jax.nn.silu(x)

def _sigmoid(x):
    return jax.nn.sigmoid(x)

def _layernorm(x, axis=-1, eps=1e-05):
    m = jnp.mean(x, axis=axis, keepdims=True)
    v = jnp.var(x, axis=axis, keepdims=True)
    return (x - m) / jnp.sqrt(v + eps)

def _scatter_add(tgt, idx, src, axis=0):
    return tgt.at[idx].add(src)

def _segment_sum(src, seg, n):
    return jax.ops.segment_sum(src, seg, n)
kernel_name = 'mk_xattn_ffn_d4_seqx_r8_ea377e'

def setup_inputs(seed: int=0):
    np.random.seed(seed)
    _w = jnp.asarray

    def _rec_inputs():
        import jax
        import jax.numpy as jnp
        _rk = jax.random.key(seed)
        x = -0.0002928 + 1 * jax.random.normal(jax.random.fold_in(_rk, 1), (8, 256, 128), jnp.float32)
        _lenS = 256 - jax.random.randint(jax.random.fold_in(_rk, 7), (8,), 0, max(1, 256 // 4) + 1, jnp.int32)
        _lenS2 = 64 - jax.random.randint(jax.random.fold_in(_rk, 8), (8,), 0, max(1, 64 // 4) + 1, jnp.int32)
        _ctx_1024P = jax.random.normal(jax.random.fold_in(_rk, 11), (8, 16, 128), jnp.float32)
        _ctx_1024c = jax.random.dirichlet(jax.random.fold_in(_rk, 511), 0.3 * jnp.ones((16,), jnp.float32), (8, 64))
        _ctx_1024t = jnp.einsum('bsk,bkd->bsd', _ctx_1024c, _ctx_1024P)
        _ctx_1024t = _ctx_1024t * jax.lax.rsqrt(jnp.mean(jnp.square(_ctx_1024t)) + 1e-12) * 0.953939
        ctx_1024 = -1.39393e-06 + 0.999914 * (_ctx_1024t + 0.3 * jax.random.normal(jax.random.fold_in(_rk, 611), (8, 64, 128), jnp.float32))
        _validS = jnp.arange(256)[None, :] < _lenS[:, None]
        _validS2 = jnp.arange(64)[None, :] < _lenS2[:, None]
        _causal = jnp.tril(jnp.ones((256, 256), dtype=bool))
        mask_1x1xSxS2_fk1 = jnp.where(jnp.broadcast_to(_validS2[0:1, None, None, :], (1, 1, 256, 64)), 1.0, 0.0).astype(jnp.float32)
        mask_BxSxS2_bk1 = jnp.broadcast_to(_validS2[:, None, :], (8, 256, 64))
        return (x, ctx_1024, mask_1x1xSxS2_fk1, mask_BxSxS2_bk1)
    x, ctx_1024, mask_1x1xSxS2_fk1, mask_BxSxS2_bk1 = _rec_inputs()

    def _L0_xattn_setup():
        import jax, jax.numpy as jnp
        import numpy as np
        D_MODEL = 128
        NUM_HEADS = 16
        DEPTH = D_MODEL // NUM_HEADS
        B, S = (2, 256)
        NEG = -1000000000.0

        def _split_heads(x):
            b, s, _ = x.shape
            return x.reshape(b, s, NUM_HEADS, DEPTH).transpose(0, 2, 1, 3)
        key = jax.random.key(seed)
        ks = jax.random.split(key, 12)
        sc = 1.0 / np.sqrt(D_MODEL)
        inp = {'query': jax.random.normal(ks[0], (B, S, D_MODEL), jnp.float32), 'key_in': jax.random.normal(ks[1], (B, S, D_MODEL), jnp.float32), 'value': jax.random.normal(ks[2], (B, S, D_MODEL), jnp.float32), 'mask': (1.0 - jnp.tril(jnp.ones((S, S), jnp.float32)))[None, None, :, :], 'wq': jax.random.normal(ks[3], (D_MODEL, D_MODEL), jnp.float32) * sc, 'bq': jnp.zeros((D_MODEL,), jnp.float32), 'wk': jax.random.normal(ks[4], (D_MODEL, D_MODEL), jnp.float32) * sc, 'bk': jnp.zeros((D_MODEL,), jnp.float32), 'wv': jax.random.normal(ks[5], (D_MODEL, D_MODEL), jnp.float32) * sc, 'bv': jnp.zeros((D_MODEL,), jnp.float32), 'wo': jax.random.normal(ks[6], (D_MODEL, D_MODEL), jnp.float32) * sc, 'bo': jnp.zeros((D_MODEL,), jnp.float32)}
        return inp
    _L0_xattn_all = _L0_xattn_setup()
    _L0_xattn_in = {k: v for k, v in _L0_xattn_all.items() if k in ('wq', 'bq', 'wk', 'bk', 'wv', 'bv', 'wo', 'bo')}
    del _L0_xattn_all

    def _L0_ffn_setup():
        import jax, jax.numpy as jnp
        import numpy as np
        DIM = 128
        HEADS = 16
        HD = DIM // HEADS
        M = 32
        E = 4
        K = 2
        HID = 256
        MID = 256
        LB = 0.01
        EPS = 1.1920929e-07

        def _rms(x, w):
            return x * jax.lax.rsqrt(jnp.mean(x * x, axis=-1, keepdims=True) + EPS) * w

        def _gelu(x):
            return jax.nn.gelu(x, approximate=False)
        key = jax.random.key(seed)
        ks = jax.random.split(key, 20)
        d = DIM
        w = lambda k, s: jax.random.normal(k, s, jnp.float32) * 0.02
        return {'x': jax.random.normal(ks[0], (4, 128, d), jnp.float32), 'n1_w': jnp.ones((d,), jnp.float32), 'n2_w': jnp.ones((d,), jnp.float32), 'wq': w(ks[1], (d, d)), 'wk': w(ks[2], (d, d)), 'wv': w(ks[3], (d, d)), 'wo': w(ks[4], (d, d)), 'qn_w': jnp.ones((HD,), jnp.float32), 'kn_w': jnp.ones((HD,), jnp.float32), 'gate_w': w(ks[5], (E, d)), 'e0_up': w(ks[6], (HID, d)), 'e0_down': w(ks[7], (d, HID)), 'e1_w1': w(ks[8], (HID, d)), 'e1_w2': w(ks[9], (HID, d)), 'e1_down': w(ks[10], (d, HID)), 'e2_l1': w(ks[11], (MID, d)), 'e2_l2': w(ks[12], (HID, MID)), 'e2_l3': w(ks[13], (MID, HID)), 'e2_l4': w(ks[14], (d, MID)), 'e3_down': w(ks[15], (d, d)), 'e3_up': w(ks[16], (HID, d)), 'e3_out': w(ks[17], (d, HID))}
    _L0_ffn_all = _L0_ffn_setup()
    _L0_ffn_in = {k: v for k, v in _L0_ffn_all.items() if k in ('n1_w', 'n2_w', 'wq', 'wk', 'wv', 'wo', 'qn_w', 'kn_w', 'gate_w', 'e0_up', 'e0_down', 'e1_w1', 'e1_w2', 'e1_down', 'e2_l1', 'e2_l2', 'e2_l3', 'e2_l4', 'e3_down', 'e3_up', 'e3_out')}
    del _L0_ffn_all

    def _L1_xattn_setup():
        import jax, jax.numpy as jnp
        import numpy as np
        HIDDEN = 128
        NUM_HEADS = 16
        DK = 64
        DV = 64
        NEG_INF = -1000000000.0
        key = jax.random.key(seed)
        ks = jax.random.split(key, 12)
        B, S = (4, 256)
        scale = 0.02
        return {'q_hidden_inputs': jax.random.normal(ks[0], (B, S, HIDDEN), dtype=jnp.float32), 'k_hidden_inputs': jax.random.normal(ks[1], (B, S, HIDDEN), dtype=jnp.float32), 'v_hidden_inputs': jax.random.normal(ks[2], (B, S, HIDDEN), dtype=jnp.float32), 'mask': jax.random.randint(ks[3], (B, S, S), 0, 2) > 0, 'wq': jax.random.normal(ks[4], (NUM_HEADS, HIDDEN, DK), dtype=jnp.float32) * scale, 'bq': jax.random.normal(ks[5], (NUM_HEADS, DK), dtype=jnp.float32) * scale, 'wk': jax.random.normal(ks[6], (NUM_HEADS, HIDDEN, DK), dtype=jnp.float32) * scale, 'bk': jax.random.normal(ks[7], (NUM_HEADS, DK), dtype=jnp.float32) * scale, 'wv': jax.random.normal(ks[8], (NUM_HEADS, HIDDEN, DV), dtype=jnp.float32) * scale, 'bv': jax.random.normal(ks[9], (NUM_HEADS, DV), dtype=jnp.float32) * scale, 'wo': jax.random.normal(ks[10], (NUM_HEADS * DV, HIDDEN), dtype=jnp.float32) * scale, 'bo': jax.random.normal(ks[11], (HIDDEN,), dtype=jnp.float32) * scale}
    _L1_xattn_all = _L1_xattn_setup()
    _L1_xattn_in = {k: v for k, v in _L1_xattn_all.items() if k in ('wq', 'bq', 'wk', 'bk', 'wv', 'bv', 'wo', 'bo')}
    del _L1_xattn_all

    def _L1_ffn_setup():
        import jax, jax.numpy as jnp
        import numpy as np
        TOP_K = 2
        key = jax.random.key(seed)
        ks = jax.random.split(key, 5)
        B, T, D, F, E = (4, 256, 128, 512, 8)
        s = 0.02
        return {'x': jax.random.normal(ks[0], (B, T, D), jnp.float32), 'gate_w': jax.random.normal(ks[1], (D, E), jnp.float32) * s, 'w1': jax.random.normal(ks[2], (E, D, F), jnp.float32) * s, 'w3': jax.random.normal(ks[3], (E, D, F), jnp.float32) * s, 'w2': jax.random.normal(ks[4], (E, F, D), jnp.float32) * s}
    _L1_ffn_all = _L1_ffn_setup()
    _L1_ffn_in = {k: v for k, v in _L1_ffn_all.items() if k in ('gate_w', 'w1', 'w3', 'w2')}
    del _L1_ffn_all

    def _L2_xattn_setup():
        import jax, jax.numpy as jnp
        import numpy as np
        HIDDEN = 128
        NUM_HEADS = 16
        HEAD_DIM = HIDDEN // NUM_HEADS
        SCALE = 1.0 / float(np.sqrt(HEAD_DIM))
        key = jax.random.key(seed)
        ks = jax.random.split(key, 10)
        B, SQ, SKV = (2, 256, 512)
        init = 0.02
        return {'query_states': jax.random.normal(ks[0], (B, SQ, HIDDEN), dtype=jnp.float32), 'key_value_states': jax.random.normal(ks[1], (B, SKV, HIDDEN), dtype=jnp.float32), 'Wq': jax.random.normal(ks[2], (HIDDEN, HIDDEN), dtype=jnp.float32) * init, 'bq': jnp.zeros((HIDDEN,), dtype=jnp.float32), 'Wk': jax.random.normal(ks[3], (HIDDEN, HIDDEN), dtype=jnp.float32) * init, 'bk': jnp.zeros((HIDDEN,), dtype=jnp.float32), 'Wv': jax.random.normal(ks[4], (HIDDEN, HIDDEN), dtype=jnp.float32) * init, 'bv': jnp.zeros((HIDDEN,), dtype=jnp.float32), 'Wo': jax.random.normal(ks[5], (HIDDEN, HIDDEN), dtype=jnp.float32) * init, 'bo': jnp.zeros((HIDDEN,), dtype=jnp.float32)}
    _L2_xattn_all = _L2_xattn_setup()
    _L2_xattn_in = {k: v for k, v in _L2_xattn_all.items() if k in ('Wq', 'bq', 'Wk', 'bk', 'Wv', 'bv', 'Wo', 'bo')}
    del _L2_xattn_all

    def _L2_ffn_setup():
        import jax, jax.numpy as jnp
        import numpy as np
        B, S, D = (4, 128, 128)
        E, K = (8, 2)
        H = 2 * D
        key = jax.random.key(seed)
        ks = jax.random.split(key, 5)
        x = jax.random.normal(ks[0], (B, S, D), dtype=jnp.float32)
        Wg = jax.random.normal(ks[1], (E, D), dtype=jnp.float32) * 0.02
        W1 = jax.random.normal(ks[2], (E, H, D), dtype=jnp.float32) * 0.02
        W2 = jax.random.normal(ks[3], (E, H, D), dtype=jnp.float32) * 0.02
        W3 = jax.random.normal(ks[4], (E, D, H), dtype=jnp.float32) * 0.02
        return {'x': x, 'Wg': Wg, 'W1': W1, 'W2': W2, 'W3': W3}
    _L2_ffn_all = _L2_ffn_setup()
    _L2_ffn_in = {k: v for k, v in _L2_ffn_all.items() if k in ('Wg', 'W1', 'W2', 'W3')}
    del _L2_ffn_all

    def _L3_xattn_setup():
        import jax, jax.numpy as jnp
        import numpy as np
        B, C_LEN, Q_LEN, D = (8, 256, 64, 128)
        key = jax.random.key(seed)
        ks = jax.random.split(key, 10)
        scale = 1.0 / np.sqrt(D)
        return {'c': jax.random.normal(ks[0], (B, C_LEN, D), dtype=jnp.float32), 'q': jax.random.normal(ks[1], (B, Q_LEN, D), dtype=jnp.float32), 'w_cq': jax.random.normal(ks[2], (D,), dtype=jnp.float32) * scale, 'b_cq': jax.random.normal(ks[3], (), dtype=jnp.float32) * scale, 'w_c': jax.random.normal(ks[4], (D,), dtype=jnp.float32) * scale, 'b_c': jax.random.normal(ks[5], (), dtype=jnp.float32) * scale, 'w_q': jax.random.normal(ks[6], (D,), dtype=jnp.float32) * scale, 'b_q': jax.random.normal(ks[7], (), dtype=jnp.float32) * scale, 'W_l': jax.random.normal(ks[8], (D, 4 * D), dtype=jnp.float32) * (1.0 / np.sqrt(4 * D)), 'b_l': jax.random.normal(ks[9], (D,), dtype=jnp.float32) * (1.0 / np.sqrt(4 * D))}
    _L3_xattn_all = _L3_xattn_setup()
    _L3_xattn_in = {k: v for k, v in _L3_xattn_all.items() if k in ('w_cq', 'b_cq', 'w_c', 'b_c', 'w_q', 'b_q', 'W_l', 'b_l')}
    del _L3_xattn_all

    def _L3_ffn_setup():
        import jax, jax.numpy as jnp
        import numpy as np
        from jax import lax
        HIDDEN = 128
        INTER = 64
        E = 64
        K = 6
        G = 8
        TG = 4
        NSH = 2
        ISH = INTER * NSH

        def _moe_forward(hidden_states, gate_w, gate_bias, eg_w, eu_w, ed_w, sg_w, su_w, sd_w):
            B, S, H = hidden_states.shape
            x = hidden_states.reshape(-1, H)
            T = x.shape[0]
            shared = jax.nn.silu(x @ sg_w.T) * (x @ su_w.T) @ sd_w.T
            logits = x @ gate_w.T
            scores = jax.nn.sigmoid(logits) + gate_bias
            group_scores = scores.reshape(T, G, E // G).max(axis=-1)
            _, sel_groups = lax.top_k(group_scores, TG)
            group_mask = jnp.zeros((T, G), scores.dtype).at[jnp.arange(T)[:, None], sel_groups].set(1.0)
            mask = jnp.repeat(group_mask, E // G, axis=1)
            masked_scores = scores * mask
            topk_w, topk_i = lax.top_k(masked_scores, K)
            topk_w = topk_w / (topk_w.sum(axis=-1, keepdims=True) + 1e-08)
            comb = jnp.zeros((T, E), x.dtype).at[jnp.arange(T)[:, None], topk_i].add(topk_w)
            h = jax.nn.silu(jnp.einsum('th,eih->eti', x, eg_w)) * jnp.einsum('th,eih->eti', x, eu_w)
            routed = jnp.einsum('eti,ehi,te->th', h, ed_w, comb)
            return (shared + routed).reshape(B, S, H)
        key = jax.random.key(seed)
        ks = jax.random.split(key, 9)
        s = 0.02
        return {'hidden_states': jax.random.normal(ks[0], (1, 128, HIDDEN), jnp.float32), 'gate_w': jax.random.normal(ks[1], (E, HIDDEN), jnp.float32) * s, 'gate_bias': jnp.zeros((E,), jnp.float32), 'eg_w': jax.random.normal(ks[2], (E, INTER, HIDDEN), jnp.float32) * s, 'eu_w': jax.random.normal(ks[3], (E, INTER, HIDDEN), jnp.float32) * s, 'ed_w': jax.random.normal(ks[4], (E, HIDDEN, INTER), jnp.float32) * s, 'sg_w': jax.random.normal(ks[5], (ISH, HIDDEN), jnp.float32) * s, 'su_w': jax.random.normal(ks[6], (ISH, HIDDEN), jnp.float32) * s, 'sd_w': jax.random.normal(ks[7], (HIDDEN, ISH), jnp.float32) * s}
    _L3_ffn_all = _L3_ffn_setup()
    _L3_ffn_in = {k: v for k, v in _L3_ffn_all.items() if k in ('gate_w', 'gate_bias', 'eg_w', 'eu_w', 'ed_w', 'sg_w', 'su_w', 'sd_w')}
    del _L3_ffn_all
    return {'x': x, 'ctx_1024': ctx_1024, 'mask_1x1xSxS2_fk1': mask_1x1xSxS2_fk1, 'mask_BxSxS2_bk1': mask_BxSxS2_bk1, 'L0_xattn_wq': _L0_xattn_in['wq'], 'L0_xattn_bq': _L0_xattn_in['bq'], 'L0_xattn_wk': _L0_xattn_in['wk'], 'L0_xattn_bk': _L0_xattn_in['bk'], 'L0_xattn_wv': _L0_xattn_in['wv'], 'L0_xattn_bv': _L0_xattn_in['bv'], 'L0_xattn_wo': _L0_xattn_in['wo'], 'L0_xattn_bo': _L0_xattn_in['bo'], 'L0_ffn_n1_w': _L0_ffn_in['n1_w'], 'L0_ffn_n2_w': _L0_ffn_in['n2_w'], 'L0_ffn_wq': _L0_ffn_in['wq'], 'L0_ffn_wk': _L0_ffn_in['wk'], 'L0_ffn_wv': _L0_ffn_in['wv'], 'L0_ffn_wo': _L0_ffn_in['wo'], 'L0_ffn_qn_w': _L0_ffn_in['qn_w'], 'L0_ffn_kn_w': _L0_ffn_in['kn_w'], 'L0_ffn_gate_w': _L0_ffn_in['gate_w'], 'L0_ffn_e0_up': _L0_ffn_in['e0_up'], 'L0_ffn_e0_down': _L0_ffn_in['e0_down'], 'L0_ffn_e1_w1': _L0_ffn_in['e1_w1'], 'L0_ffn_e1_w2': _L0_ffn_in['e1_w2'], 'L0_ffn_e1_down': _L0_ffn_in['e1_down'], 'L0_ffn_e2_l1': _L0_ffn_in['e2_l1'], 'L0_ffn_e2_l2': _L0_ffn_in['e2_l2'], 'L0_ffn_e2_l3': _L0_ffn_in['e2_l3'], 'L0_ffn_e2_l4': _L0_ffn_in['e2_l4'], 'L0_ffn_e3_down': _L0_ffn_in['e3_down'], 'L0_ffn_e3_up': _L0_ffn_in['e3_up'], 'L0_ffn_e3_out': _L0_ffn_in['e3_out'], 'L1_xattn_wq': _L1_xattn_in['wq'], 'L1_xattn_bq': _L1_xattn_in['bq'], 'L1_xattn_wk': _L1_xattn_in['wk'], 'L1_xattn_bk': _L1_xattn_in['bk'], 'L1_xattn_wv': _L1_xattn_in['wv'], 'L1_xattn_bv': _L1_xattn_in['bv'], 'L1_xattn_wo': _L1_xattn_in['wo'], 'L1_xattn_bo': _L1_xattn_in['bo'], 'L1_ffn_gate_w': _L1_ffn_in['gate_w'], 'L1_ffn_w1': _L1_ffn_in['w1'], 'L1_ffn_w3': _L1_ffn_in['w3'], 'L1_ffn_w2': _L1_ffn_in['w2'], 'L2_xattn_Wq': _L2_xattn_in['Wq'], 'L2_xattn_bq': _L2_xattn_in['bq'], 'L2_xattn_Wk': _L2_xattn_in['Wk'], 'L2_xattn_bk': _L2_xattn_in['bk'], 'L2_xattn_Wv': _L2_xattn_in['Wv'], 'L2_xattn_bv': _L2_xattn_in['bv'], 'L2_xattn_Wo': _L2_xattn_in['Wo'], 'L2_xattn_bo': _L2_xattn_in['bo'], 'L2_ffn_Wg': _L2_ffn_in['Wg'], 'L2_ffn_W1': _L2_ffn_in['W1'], 'L2_ffn_W2': _L2_ffn_in['W2'], 'L2_ffn_W3': _L2_ffn_in['W3'], 'L3_xattn_w_cq': _L3_xattn_in['w_cq'], 'L3_xattn_b_cq': _L3_xattn_in['b_cq'], 'L3_xattn_w_c': _L3_xattn_in['w_c'], 'L3_xattn_b_c': _L3_xattn_in['b_c'], 'L3_xattn_w_q': _L3_xattn_in['w_q'], 'L3_xattn_b_q': _L3_xattn_in['b_q'], 'L3_xattn_W_l': _L3_xattn_in['W_l'], 'L3_xattn_b_l': _L3_xattn_in['b_l'], 'L3_ffn_gate_w': _L3_ffn_in['gate_w'], 'L3_ffn_gate_bias': _L3_ffn_in['gate_bias'], 'L3_ffn_eg_w': _L3_ffn_in['eg_w'], 'L3_ffn_eu_w': _L3_ffn_in['eu_w'], 'L3_ffn_ed_w': _L3_ffn_in['ed_w'], 'L3_ffn_sg_w': _L3_ffn_in['sg_w'], 'L3_ffn_su_w': _L3_ffn_in['su_w'], 'L3_ffn_sd_w': _L3_ffn_in['sd_w']}

def reference(x, ctx_1024, mask_1x1xSxS2_fk1, mask_BxSxS2_bk1, L0_xattn_wq, L0_xattn_bq, L0_xattn_wk, L0_xattn_bk, L0_xattn_wv, L0_xattn_bv, L0_xattn_wo, L0_xattn_bo, L0_ffn_n1_w, L0_ffn_n2_w, L0_ffn_wq, L0_ffn_wk, L0_ffn_wv, L0_ffn_wo, L0_ffn_qn_w, L0_ffn_kn_w, L0_ffn_gate_w, L0_ffn_e0_up, L0_ffn_e0_down, L0_ffn_e1_w1, L0_ffn_e1_w2, L0_ffn_e1_down, L0_ffn_e2_l1, L0_ffn_e2_l2, L0_ffn_e2_l3, L0_ffn_e2_l4, L0_ffn_e3_down, L0_ffn_e3_up, L0_ffn_e3_out, L1_xattn_wq, L1_xattn_bq, L1_xattn_wk, L1_xattn_bk, L1_xattn_wv, L1_xattn_bv, L1_xattn_wo, L1_xattn_bo, L1_ffn_gate_w, L1_ffn_w1, L1_ffn_w3, L1_ffn_w2, L2_xattn_Wq, L2_xattn_bq, L2_xattn_Wk, L2_xattn_bk, L2_xattn_Wv, L2_xattn_bv, L2_xattn_Wo, L2_xattn_bo, L2_ffn_Wg, L2_ffn_W1, L2_ffn_W2, L2_ffn_W3, L3_xattn_w_cq, L3_xattn_b_cq, L3_xattn_w_c, L3_xattn_b_c, L3_xattn_w_q, L3_xattn_b_q, L3_xattn_W_l, L3_xattn_b_l, L3_ffn_gate_w, L3_ffn_gate_bias, L3_ffn_eg_w, L3_ffn_eu_w, L3_ffn_ed_w, L3_ffn_sg_w, L3_ffn_su_w, L3_ffn_sd_w):
    import jax
    import jax.numpy as jnp

    def _L0_xattn_ref(query, key_in, value, mask, wq, bq, wk, bk, wv, bv, wo, bo):
        import jax, jax.numpy as jnp
        import numpy as np
        D_MODEL = 128
        NUM_HEADS = 16
        DEPTH = D_MODEL // NUM_HEADS
        B, S = (2, 256)
        NEG = -1000000000.0

        def _split_heads(x):
            b, s, _ = x.shape
            return x.reshape(b, s, NUM_HEADS, DEPTH).transpose(0, 2, 1, 3)
        q = _split_heads(query @ wq + bq)
        k = _split_heads(key_in @ wk + bk)
        v = _split_heads(value @ wv + bv)
        scale = 1.0 / jnp.sqrt(jnp.asarray(DEPTH, jnp.float32))
        logits = jnp.einsum('bhqd,bhkd->bhqk', q, k) * scale + mask * NEG
        attn = jax.nn.softmax(logits, axis=-1)
        out = jnp.einsum('bhqk,bhkd->bhqd', attn, v)
        out = out.transpose(0, 2, 1, 3).reshape(query.shape[0], -1, D_MODEL)
        return out @ wo + bo

    def _L0_ffn_ref(x, n1_w, n2_w, wq, wk, wv, wo, qn_w, kn_w, gate_w, e0_up, e0_down, e1_w1, e1_w2, e1_down, e2_l1, e2_l2, e2_l3, e2_l4, e3_down, e3_up, e3_out):
        import jax, jax.numpy as jnp
        import numpy as np
        DIM = 128
        HEADS = 16
        HD = DIM // HEADS
        M = 32
        E = 4
        K = 2
        HID = 256
        MID = 256
        LB = 0.01
        EPS = 1.1920929e-07

        def _rms(x, w):
            return x * jax.lax.rsqrt(jnp.mean(x * x, axis=-1, keepdims=True) + EPS) * w

        def _gelu(x):
            return jax.nn.gelu(x, approximate=False)
        B, T, C = x.shape
        h = _rms(x, n1_w)
        heads = lambda w_: (h @ w_.T).reshape(B, T, HEADS, HD).transpose(0, 2, 1, 3)
        q = _rms(heads(wq), qn_w)
        k = _rms(heads(wk), kn_w)
        v = heads(wv)
        scores = jnp.einsum('bhqd,bhkd->bhqk', q, k) * HD ** (-0.5)
        causal = jnp.tril(jnp.ones((T, T), bool))
        scores = jnp.where(causal[None, None], scores, -jnp.inf)
        attn = jax.nn.softmax(scores, axis=-1)
        ao = jnp.einsum('bhqk,bhkd->bhqd', attn, v).transpose(0, 2, 1, 3).reshape(B, T, C) @ wo.T
        ao = ao.at[:, :, :M].set(0.0)
        x = x + ao
        xf = _rms(x, n2_w).reshape(-1, C)
        N = xf.shape[0]
        logits = jnp.nan_to_num(xf @ gate_w.T)
        probs = jax.nn.softmax(logits, axis=-1)
        topv, topi = jax.lax.top_k(probs, K)
        topv = topv / (topv.sum(-1, keepdims=True) + 1e-08)
        wts = jnp.zeros((N, E), x.dtype).at[jnp.arange(N)[:, None], topi].add(topv)
        o0 = _gelu(xf @ e0_up.T) @ e0_down.T
        o1 = jax.nn.silu(xf @ e1_w1.T) * (xf @ e1_w2.T) @ e1_down.T
        o2 = _gelu(_gelu(_gelu(xf @ e2_l1.T) @ e2_l2.T) @ e2_l3.T) @ e2_l4.T
        o3 = _gelu(_gelu(xf @ e3_down.T) @ e3_up.T) @ e3_out.T
        moe = wts[:, 0:1] * o0 + wts[:, 1:2] * o1 + wts[:, 2:3] * o2 + wts[:, 3:4] * o3
        moe = moe.reshape(B, T, C).at[:, :, :M].set(0.0)
        return x + moe

    def _L1_xattn_ref(q_hidden_inputs, k_hidden_inputs, v_hidden_inputs, mask, wq, bq, wk, bk, wv, bv, wo, bo):
        import jax, jax.numpy as jnp
        import numpy as np
        HIDDEN = 128
        NUM_HEADS = 16
        DK = 64
        DV = 64
        NEG_INF = -1000000000.0
        q = jnp.einsum('bsd,hdk->bhsk', q_hidden_inputs, wq) + bq[None, :, None, :]
        k = jnp.einsum('bsd,hdk->bhsk', k_hidden_inputs, wk) + bk[None, :, None, :]
        v = jnp.einsum('bsd,hdv->bhsv', v_hidden_inputs, wv) + bv[None, :, None, :]
        scores = jnp.einsum('bhsk,bhtk->bhst', q, k) / jnp.sqrt(jnp.float32(DK))
        scores = jnp.where(mask[:, None, :, :], scores, NEG_INF)
        attn = jax.nn.softmax(scores, axis=-1)
        out = jnp.einsum('bhst,bhtv->bhsv', attn, v)
        B, H, Sq, Dv = out.shape
        out = jnp.transpose(out, (0, 2, 1, 3)).reshape(B, Sq, H * Dv)
        return out @ wo + bo

    def _L1_ffn_ref(x, gate_w, w1, w3, w2):
        import jax, jax.numpy as jnp
        import numpy as np
        TOP_K = 2
        logits = jnp.einsum('btd,de->bte', x, gate_w)
        probs = jax.nn.softmax(logits, axis=-1)
        expert_weights, expert_indices = jax.lax.top_k(probs, TOP_K)
        expert_weights = expert_weights / expert_weights.sum(-1, keepdims=True)
        E = w1.shape[0]
        out = jnp.zeros_like(x)
        for i in range(E):
            wi = jnp.where(expert_indices == i, expert_weights, 0.0).sum(-1)
            h = jax.nn.silu(jnp.einsum('btd,df->btf', x, w1[i])) * jnp.einsum('btd,df->btf', x, w3[i])
            out = out + jnp.einsum('btf,fd->btd', h, w2[i]) * wi[..., None]
        return out

    def _L2_xattn_ref(query_states, key_value_states, Wq, bq, Wk, bk, Wv, bv, Wo, bo):
        import jax, jax.numpy as jnp
        import numpy as np
        HIDDEN = 128
        NUM_HEADS = 16
        HEAD_DIM = HIDDEN // NUM_HEADS
        SCALE = 1.0 / float(np.sqrt(HEAD_DIM))
        B, SQ, _ = query_states.shape
        _, SKV, _ = key_value_states.shape
        q = query_states @ Wq.T + bq
        k = key_value_states @ Wk.T + bk
        v = key_value_states @ Wv.T + bv
        q = q.reshape(B, SQ, NUM_HEADS, HEAD_DIM).transpose(0, 2, 1, 3) * SCALE
        k = k.reshape(B, SKV, NUM_HEADS, HEAD_DIM).transpose(0, 2, 1, 3)
        v = v.reshape(B, SKV, NUM_HEADS, HEAD_DIM).transpose(0, 2, 1, 3)
        scores = jnp.einsum('bhqd,bhkd->bhqk', q, k)
        attn = jax.nn.softmax(scores, axis=-1)
        ctx = jnp.einsum('bhqk,bhkd->bhqd', attn, v)
        ctx = ctx.transpose(0, 2, 1, 3).reshape(B, SQ, HIDDEN)
        return ctx @ Wo.T + bo

    def _L2_ffn_ref(x, Wg, W1, W2, W3):
        import jax, jax.numpy as jnp
        import numpy as np
        B, S, D = (4, 128, 128)
        E, K = (8, 2)
        H = 2 * D
        gate_out = jnp.einsum('bsd,ed->bse', x, Wg)
        top_v, top_i = jax.lax.top_k(gate_out, K)
        probs = jax.nn.softmax(top_v, axis=-1)
        out = jnp.zeros_like(x)
        for e in range(E):
            w_e = jnp.sum(probs * (top_i == e), axis=-1)
            h1 = jnp.einsum('bsd,hd->bsh', x, W1[e])
            h2 = jnp.einsum('bsd,hd->bsh', x, W2[e])
            g = h1 * jax.nn.sigmoid(h1) * h2
            y = jnp.einsum('bsh,dh->bsd', g, W3[e])
            out = out + y * w_e[..., None]
        return out

    def _L3_xattn_ref(c, q, w_cq, b_cq, w_c, b_c, w_q, b_q, W_l, b_l):
        import jax, jax.numpy as jnp
        import numpy as np
        B, C_LEN, Q_LEN, D = (8, 256, 64, 128)
        cq = jnp.einsum('bcd,bqd,d->bcq', c, q, w_cq) + b_cq
        s = (c @ w_c + b_c)[:, :, None] + (q @ w_q + b_q)[:, None, :] + cq
        a = jax.nn.softmax(s, axis=2)
        c2q_att = jnp.einsum('bcq,bqd->bcd', a, q)
        b_att = jax.nn.softmax(jnp.max(s, axis=2), axis=1)
        q2c_att = jnp.einsum('bc,bcd->bd', b_att, c)[:, None, :]
        x = jnp.concatenate([c, c2q_att, c * c2q_att, c * q2c_att], axis=-1)
        z = x @ W_l.T + b_l
        return z

    def _L3_ffn_ref(hidden_states, gate_w, gate_bias, eg_w, eu_w, ed_w, sg_w, su_w, sd_w):
        import jax, jax.numpy as jnp
        import numpy as np
        from jax import lax
        HIDDEN = 128
        INTER = 64
        E = 64
        K = 6
        G = 8
        TG = 4
        NSH = 2
        ISH = INTER * NSH

        def _moe_forward(hidden_states, gate_w, gate_bias, eg_w, eu_w, ed_w, sg_w, su_w, sd_w):
            B, S, H = hidden_states.shape
            x = hidden_states.reshape(-1, H)
            T = x.shape[0]
            shared = jax.nn.silu(x @ sg_w.T) * (x @ su_w.T) @ sd_w.T
            logits = x @ gate_w.T
            scores = jax.nn.sigmoid(logits) + gate_bias
            group_scores = scores.reshape(T, G, E // G).max(axis=-1)
            _, sel_groups = lax.top_k(group_scores, TG)
            group_mask = jnp.zeros((T, G), scores.dtype).at[jnp.arange(T)[:, None], sel_groups].set(1.0)
            mask = jnp.repeat(group_mask, E // G, axis=1)
            masked_scores = scores * mask
            topk_w, topk_i = lax.top_k(masked_scores, K)
            topk_w = topk_w / (topk_w.sum(axis=-1, keepdims=True) + 1e-08)
            comb = jnp.zeros((T, E), x.dtype).at[jnp.arange(T)[:, None], topk_i].add(topk_w)
            h = jax.nn.silu(jnp.einsum('th,eih->eti', x, eg_w)) * jnp.einsum('th,eih->eti', x, eu_w)
            routed = jnp.einsum('eti,ehi,te->th', h, ed_w, comb)
            return (shared + routed).reshape(B, S, H)
        return _moe_forward(hidden_states, gate_w, gate_bias, eg_w, eu_w, ed_w, sg_w, su_w, sd_w)
    x = x + _L0_xattn_ref(_layernorm(x, axis=-1), ctx_1024, ctx_1024, mask_1x1xSxS2_fk1, L0_xattn_wq, L0_xattn_bq, L0_xattn_wk, L0_xattn_bk, L0_xattn_wv, L0_xattn_bv, L0_xattn_wo, L0_xattn_bo)
    x = x + _L0_ffn_ref(_layernorm(x, axis=-1), L0_ffn_n1_w, L0_ffn_n2_w, L0_ffn_wq, L0_ffn_wk, L0_ffn_wv, L0_ffn_wo, L0_ffn_qn_w, L0_ffn_kn_w, L0_ffn_gate_w, L0_ffn_e0_up, L0_ffn_e0_down, L0_ffn_e1_w1, L0_ffn_e1_w2, L0_ffn_e1_down, L0_ffn_e2_l1, L0_ffn_e2_l2, L0_ffn_e2_l3, L0_ffn_e2_l4, L0_ffn_e3_down, L0_ffn_e3_up, L0_ffn_e3_out)
    x = x + _L1_xattn_ref(_layernorm(x, axis=-1), ctx_1024, ctx_1024, mask_BxSxS2_bk1, L1_xattn_wq, L1_xattn_bq, L1_xattn_wk, L1_xattn_bk, L1_xattn_wv, L1_xattn_bv, L1_xattn_wo, L1_xattn_bo)
    x = x + _L1_ffn_ref(_layernorm(x, axis=-1), L1_ffn_gate_w, L1_ffn_w1, L1_ffn_w3, L1_ffn_w2)
    x = x + _L2_xattn_ref(_layernorm(x, axis=-1), ctx_1024, L2_xattn_Wq, L2_xattn_bq, L2_xattn_Wk, L2_xattn_bk, L2_xattn_Wv, L2_xattn_bv, L2_xattn_Wo, L2_xattn_bo)
    x = x + _L2_ffn_ref(_layernorm(x, axis=-1), L2_ffn_Wg, L2_ffn_W1, L2_ffn_W2, L2_ffn_W3)
    x = x + _L3_xattn_ref(_layernorm(x, axis=-1), ctx_1024, L3_xattn_w_cq, L3_xattn_b_cq, L3_xattn_w_c, L3_xattn_b_c, L3_xattn_w_q, L3_xattn_b_q, L3_xattn_W_l, L3_xattn_b_l)
    x = x + _L3_ffn_ref(_layernorm(x, axis=-1), L3_ffn_gate_w, L3_ffn_gate_bias, L3_ffn_eg_w, L3_ffn_eu_w, L3_ffn_ed_w, L3_ffn_sg_w, L3_ffn_su_w, L3_ffn_sd_w)
    return x

_drawn_inputs = setup_inputs


def setup_inputs(seed=0):
    import zlib

    import numpy as np

    out = dict(_drawn_inputs(seed))
    spreads = {'L0_xattn_bq': (0.0, 0.276),
     'L0_xattn_bk': (0.0, 2.0),
     'L0_xattn_bv': (0.0, 0.1),
     'L0_xattn_bo': (0.0, 0.1),
     'L0_ffn_n1_w': (1.0, 0.6),
     'L0_ffn_n2_w': (1.0, 0.6),
     'L0_ffn_qn_w': (1.0, 0.6),
     'L0_ffn_kn_w': (1.0, 0.6),
     'L2_xattn_bq': (0.0, 0.8),
     'L2_xattn_bk': (0.0, 2.0),
     'L2_xattn_bv': (0.0, 0.794),
     'L2_xattn_bo': (0.0, 0.1),
     'L3_ffn_gate_bias': (0.0, 0.8)}
    factors = {'L0_ffn_wq': 8.0,
     'L0_ffn_wk': 8.0,
     'L0_ffn_wv': 4.984,
     'L0_ffn_wo': 5.183,
     'L0_ffn_gate_w': 8.0,
     'L0_ffn_e0_up': 8.0,
     'L0_ffn_e0_down': 8.0,
     'L0_ffn_e1_w1': 8.0,
     'L0_ffn_e1_w2': 8.0,
     'L0_ffn_e1_down': 8.0,
     'L0_ffn_e2_l1': 8.0,
     'L0_ffn_e2_l2': 8.0,
     'L0_ffn_e2_l3': 8.0,
     'L0_ffn_e2_l4': 8.0,
     'L0_ffn_e3_down': 8.0,
     'L0_ffn_e3_up': 8.0,
     'L0_ffn_e3_out': 8.0,
     'L1_xattn_wq': 8.0,
     'L1_xattn_bq': 8.0,
     'L1_xattn_wk': 8.0,
     'L1_xattn_bk': 200.0,
     'L1_xattn_bv': 8.0,
     'L1_xattn_bo': 5.574,
     'L1_ffn_gate_w': 8.0,
     'L1_ffn_w1': 8.0,
     'L1_ffn_w3': 8.0,
     'L1_ffn_w2': 8.0,
     'L2_xattn_Wq': 8.0,
     'L2_xattn_Wk': 8.0,
     'L2_xattn_Wv': 4.437,
     'L2_xattn_Wo': 3.391,
     'L2_ffn_Wg': 8.0,
     'L2_ffn_W1': 8.0,
     'L2_ffn_W2': 8.0,
     'L2_ffn_W3': 8.0,
     'L3_xattn_w_c': 2.833,
     'L3_ffn_gate_w': 8.0,
     'L3_ffn_eg_w': 8.0,
     'L3_ffn_eu_w': 8.0,
     'L3_ffn_ed_w': 8.0,
     'L3_ffn_sg_w': 8.0,
     'L3_ffn_su_w': 8.0,
     'L3_ffn_sd_w': 8.0,
     'L3_xattn_b_l': 8.0,
     'L3_xattn_w_cq': 2.69}
    for name, (base, spread) in spreads.items():
        noise = np.random.default_rng([zlib.crc32(name.encode()), seed]).standard_normal(out[name].shape)
        drawn = base * np.exp(spread * noise) if base else spread * noise
        out[name] = jnp.asarray(drawn.astype(out[name].dtype))
    for name, factor in factors.items():
        out[name] = (out[name] * factor).astype(out[name].dtype)
    return out
```

```python
from contextlib import ExitStack

import concourse.bass as bass
from concourse import mybir

F32 = mybir.dt.float32
BF16 = mybir.dt.bfloat16
U8 = mybir.dt.uint8
ALU = mybir.AluOpType
ACT = mybir.ActivationFunctionType
X = mybir.AxisListType.X

P = 128
B, S, D = 8, 256, 128
KEYS = 64
TILES = B * S // P
TPB = S // P
HEADS = 16
HD = D // HEADS
GROUP = 4
GROUPS = TILES // GROUP
BIG = 1.0e30
KEEP = 32


def wait(eng, sem, value):
    if not isinstance(value, int) or value > 0:
        eng.wait_ge(sem, value)


def ds(i, n):
    return bass.ds(i * n, n)


class Memory:

    def __init__(self, nc, stack, tag=""):
        self.nc, self.stack, self.tag = nc, stack, tag

    def sb(self, name, shape, dt=F32):
        return self.stack.enter_context(self.nc.sbuf_tensor(self.tag + name, shape, dt))

    def ps(self, name, cols=512):
        return self.stack.enter_context(self.nc.psum_tensor(self.tag + name, [P, cols], F32))

    def sem(self, name):
        handle = self.stack.enter_context(self.nc.semaphore(self.tag + name))
        if self.tag:
            SPENT.append(handle.num)
        return handle


SPENT = []


def clear_spent(nc):
    with nc.Block() as block:
        @block.gpsimd
        def _(pool):
            nums = sorted(set(SPENT))
            while nums:
                n = 1
                while n < len(nums) and nums[n] == nums[0] + n:
                    n += 1
                pool.sem_clear(range(nums[0], nums[0] + n))
                nums = nums[n:]
    SPENT.clear()



def normalise(nc, tag, src, ident, eps, center, out_natural=None, out_T=None, channel_scale=None,
              gate_w=None, logits=None, eps_tile=None, after=None):
    with ExitStack() as stack:
        m = Memory(nc, stack, tag)
        stats = m.sb("stats", [P, TILES, 6])
        tmp = m.sb("tmp", [P, 5, TILES])
        var = m.sb("var", [P, TILES])
        std = m.sb("std", [P, TILES])
        rstd = m.sb("rstd", [P, TILES])
        zn = m.sb("zn", [P, GROUP, D])
        zs = m.sb("zs", [P, GROUP * P])
        ps_t = m.ps("ps_t")
        ps_g = m.ps("ps_g")
        var_ready, std_ready = m.sem("var_ready"), m.sem("std_ready")
        normed, turned = m.sem("normed"), m.sem("turned")
        evacuated, logits_done, logits_out = m.sem("evacuated"), m.sem("logits_done"), m.sem("logits_out")
        block = stack.enter_context(nc.Block())
        E = gate_w.shape[1] if gate_w is not None else 0
        sum2, dif, ssq, mean, dif2 = (tmp[:, k, :] for k in range(5))

        @block.vector
        def _(dve):
            with dve.Fori(0, TILES) as t:
                nc.vector.bn_stats(stats[:, bass.ds(t, 1), :].rearrange("p a b -> p (a b)"),
                                   src[:, bass.ds(t, 1), :].rearrange("p a b -> p (a b)"))
            dve.drain()
            nc.vector.tensor_tensor(sum2, stats[:, :, 1], stats[:, :, 4], ALU.add)
            nc.vector.tensor_tensor(dif, stats[:, :, 1], stats[:, :, 4], ALU.subtract)
            nc.vector.tensor_tensor(ssq, stats[:, :, 2], stats[:, :, 5], ALU.add)
            dve.drain()
            nc.vector.tensor_scalar(mean, sum2, 0.5, None, ALU.mult)
            nc.vector.scalar_tensor_tensor(out=dif2, in0=dif, scalar=0.25, in1=dif, op0=ALU.mult, op1=ALU.mult)
            dve.drain()
            last = nc.vector.scalar_tensor_tensor(out=var[:, :], in0=ssq, scalar=1.0 / D, in1=dif2,
                                                  op0=ALU.mult, op1=ALU.add)
            if not center:
                dve.drain()
                nc.vector.tensor_tensor(dif2, mean, mean, ALU.mult)
                dve.drain()
                last = nc.vector.tensor_tensor(var[:, :], var[:, :], dif2, ALU.add)
            last.then_inc(var_ready, 1)
            dve.wait_ge(std_ready, 1)
            nc.vector.reciprocal(rstd[:, :], std[:, :])
            dve.drain()
            with dve.Fori(0, GROUPS) as g:
                if out_T is not None:
                    dve.wait_ge(turned, g)
                for j in range(GROUP):
                    t = g * GROUP + j
                    one = bass.ds(t, 1)
                    row = src[:, one, :].rearrange("p a b -> p (a b)")
                    dst = zn[:, j, :] if out_T is not None else out_natural[:, one, :].rearrange("p a b -> p (a b)")
                    if center:
                        last = nc.vector.tensor_scalar(dst, row, mean[:, one], rstd[:, one],
                                                       ALU.subtract, ALU.mult)
                    else:
                        last = nc.vector.tensor_scalar(dst, row, rstd[:, one], None, ALU.mult)
                last.then_inc(normed, 1)
                if gate_w is not None:
                    dve.wait_ge(logits_done, g + 1)
                    nc.vector.tensor_copy(logits[:, bass.ds(g * GROUP, GROUP), :],
                                          ps_g[:, 0:GROUP * E].rearrange("p (a b) -> p a b", b=E))\
                        .then_inc(logits_out, 1)

        @block.scalar
        def _(act):
            act.wait_ge(var_ready, 1)
            nc.scalar.activation(std[:, :], var[:, :], ACT.Sqrt, bias=eps_tile).then_inc(std_ready, 1)
            scale = 1.0 if channel_scale is None else channel_scale
            if out_T is not None:
                with act.Fori(0, GROUPS) as g:
                    act.wait_ge(turned, g + 1)
                    if gate_w is not None:
                        act.wait_ge(logits_done, g)
                        nc.scalar.activation(zs[:, :], ps_t[:, :], ACT.Copy, scale=scale)
                    nc.scalar.activation(out_T[:, ds(g, GROUP * P)], ps_t[:, :], ACT.Copy, scale=scale)\
                        .then_inc(evacuated, 1)

        if out_T is not None:
            @block.tensor
            def _(pe):
                with pe.Fori(0, GROUPS) as g:
                    pe.wait_ge(normed, g + 1)
                    pe.wait_ge(evacuated, g)
                    for j in range(GROUP):
                        last = nc.tensor.transpose(ps_t[:, j * P:(j + 1) * P], zn[:, j, :], ident)
                    last.then_inc(turned, 1)
                    if gate_w is not None:
                        pe.wait_ge(evacuated, g + 1)
                        pe.wait_ge(logits_out, g)
                        for j in range(GROUP):
                            last = nc.tensor.matmul(ps_g[:, j * E:(j + 1) * E], zs[:, j * P:(j + 1) * P],
                                                    gate_w[:, :], start=True, stop=True)
                        last.then_inc(logits_done, 1)

        if after is not None:
            @block.gpsimd
            def _(pool):
                pool.wait_ge(normed, GROUPS)
                x3, row = after
                nc.gpsimd.tensor_tensor(x3, x3, row.unsqueeze(1).broadcast_to([P, TILES, D]), ALU.add)


LAGS = 4


def rotate(eng, step, lags=LAGS):
    for t in range(4):
        step(t, t, t // TPB)
    with eng.Fori(1, TILES // 4) as i:
        for r in range(4):
            step(i * 4 + r, r, i * 2 + r // TPB)
    for t in range(TILES, TILES + lags):
        step(t, t % 4, t // TPB)


def live(t, lag):
    return not isinstance(t, int) or 0 <= t - lag < TILES



def project_small(nc, tag, w, zT, ctx2T, ident, qT_all, kT_all, v2_all):
    with ExitStack() as stack:
        m = Memory(nc, stack, tag)
        pq = [m.ps(f"pq{i}") for i in range(2)]
        pk = m.ps("pk")
        pv = m.ps("pv", 1024)
        q_done, q_out, k_done, v_done = m.sem("q_done"), m.sem("q_out"), m.sem("k_done"), m.sem("v_done")
        block = stack.enter_context(nc.Block())

        @block.tensor
        def _(pe):
            nc.tensor.matmul(pk[:, :].rearrange("p (b k) -> p b k", k=KEYS), w["wk"][:, :], ctx2T[:, :, 0, :],
                             start=True, stop=True).then_inc(k_done, 1)
            for b in range(B):
                last = nc.tensor.matmul(pv[:, b * D:(b + 1) * D],
                                        ctx2T[:, b, :, :].rearrange("p a k -> p (a k)"),
                                        w["wv"][:, :], start=True, stop=True)
            last.then_inc(v_done, 1)
            for g in range(GROUPS):
                if g >= 2:
                    pe.wait_ge(q_out, g - 1)
                nc.tensor.matmul(pq[g % 2][:, :], w["wq"][:, :], zT[:, g * 512:(g + 1) * 512],
                                 start=True, stop=True).then_inc(q_done, 1)

        @block.scalar
        def _(act):
            act.wait_ge(k_done, 1)
            nc.scalar.activation(kT_all[:, :], pk[:, :], ACT.Identity, bias=w["bk"][:, 0:1])
            for g in range(GROUPS):
                act.wait_ge(q_done, g + 1)
                nc.scalar.activation(qT_all[:, g * 512:(g + 1) * 512], pq[g % 2][:, :], ACT.Identity,
                                     bias=w["bq"][:, 0:1]).then_inc(q_out, 1)

        @block.vector
        def _(dve):
            dve.wait_ge(v_done, 1)
            nc.vector.tensor_tensor(v2_all[:, :, :], pv[:, :].rearrange("p (b d) -> p b d", d=D),
                                    w["bv"][:, :].unsqueeze(1).broadcast_to([P, B, D]), ALU.add)


def attend_small(nc, tag, x, w, qT_all, kT_all, v2_all, ident, headmask, scale, neg=None):
    with ExitStack() as stack:
        m = Memory(nc, stack, tag)
        qs = [m.sb(f"qs{i}", [P, P]) for i in range(2)]
        kbd = [m.sb(f"kbd{i}", [P, HEADS, KEYS]) for i in range(2)]
        NA = D + HEADS
        vaug = [m.sb(f"vaug{i}", [P, 8 * (NA + 16)]) for i in range(2)]
        sm = [m.sb(f"sm{i}", [P, HEADS, KEYS]) for i in range(2)]
        mx = [m.sb(f"mx{i}", [P, HEADS]) for i in range(2)]
        pT = [m.sb(f"pT{i}", [P, 8, P]) for i in range(2)]
        rden = m.sb("rden", [P, HEADS])
        on = [m.sb(f"on{i}", [P, D]) for i in range(2)]
        onT = [m.sb(f"onT{i}", [P, P]) for i in range(2)]
        ps_s = [m.ps(f"ps_s{i}", 1024) for i in range(2)]
        ps_t = m.ps("ps_t", 1024)
        ps_o = m.ps("ps_o")
        ps_w = m.ps("ps_w")
        (k_ready, v_ready, q_ready, s_done, s_used, sub_done, p_ready, t_done, pT_ready, o_done, on_ready,
         ot_done, onT_ready, w_done, x_done, zeroed) = (m.sem(n) for n in (
             "k_ready", "v_ready", "q_ready", "s_done", "s_used", "sub_done", "p_ready", "t_done", "pT_ready", "o_done",
             "on_ready", "ot_done", "onT_ready", "w_done", "x_done", "zeroed"))
        block = stack.enter_context(nc.Block())
        @block.gpsimd
        def _(pool):
            def step(t, r, b):
                if not live(t, 0):
                    return
                if r % 2 == 0:
                    b2 = r // 2
                    wait(pool, s_done, t - 2)
                    nc.gpsimd.tensor_tensor(kbd[b2][:, :, :],
                                            kT_all[:, ds(b, KEYS)].unsqueeze(1).broadcast_to([P, HEADS, KEYS]),
                                            headmask.unsqueeze(2).broadcast_to([P, HEADS, KEYS]), ALU.mult)\
                        .then_inc(k_ready, 1)
                wait(pool, s_done, t - 1)
                nc.gpsimd.tensor_copy(qs[r % 2][:, :], qT_all[:, ds(t, P)]).then_inc(q_ready, 1)

            rotate(pool, step, 0)

        @block.tensor
        def _(pe):
            def step(t, r, b):
                p = r % 2
                if live(t, 3):
                    pe.wait_ge(on_ready, t - 2)
                    nc.tensor.transpose(ps_o[:, 2 * P:3 * P], on[1 - p][:, :], ident).then_inc(ot_done, 1)
                if live(t, 0):
                    pe.wait_ge(q_ready, t + 1)
                    if r % 2 == 0:
                        pe.wait_ge(k_ready, b + 1)
                    wait(pe, s_used if neg is not None else sub_done, t - 1)
                    for h in range(2):
                        last = nc.tensor.matmul(ps_s[p][:, h * 512:(h + 1) * 512], qs[p][:, :],
                                                kbd[r // 2][:, 8 * h:8 * h + 8, :].rearrange("p a b -> p (a b)"),
                                                start=True, stop=True)
                    last.then_inc(s_done, 1)
                if live(t, 1):
                    pe.wait_ge(p_ready, t)
                    wait(pe, pT_ready, t - 1)
                    for j in range(8):
                        last = nc.tensor.transpose(ps_t[:, j * P:(j + 1) * P],
                                                   sm[1 - p][:, 2 * j:2 * j + 2, :].rearrange("p a b -> p (a b)"), ident)
                    last.then_inc(t_done, 1)
                if live(t, 2):
                    pe.wait_ge(pT_ready, t - 1)
                    wait(pe, onT_ready, t - 2)
                    vb = ((r - 2) % 4) // 2
                    if r % 2 == 0:
                        pe.wait_ge(v_ready, b)
                    for j in range(8):
                        last = nc.tensor.matmul(ps_o[:, 0:NA], pT[p][:, j, :],
                                                vaug[vb][:, j * NA:(j + 1) * NA], start=j == 0, stop=j == 7)
                    last.then_inc(o_done, 1)
                if live(t, 4):
                    pe.wait_ge(onT_ready, t - 3)
                    wait(pe, x_done, t - 4)
                    nc.tensor.matmul(ps_w[:, 0:P], onT[p][:, :], w["wo"][:, :],
                                     start=True, stop=True).then_inc(w_done, 1)

            rotate(pe, step)

        @block.scalar
        def _(act):
            act.wait_ge(zeroed, 1)

            def step(t, r, b):
                p = r % 2
                if live(t, 0) and p == 0:
                    wait(act, o_done, t - 2)
                    for half in range(2):
                        rows = slice(64 * half, 64 * half + 64)
                        out = vaug[r // 2][rows, :].rearrange("p (j c) -> p j c", c=NA + 16)
                        src = v2_all[rows, bass.ds(b, 1), :].rearrange("p a (j e d) -> p (a j) e d", e=2, d=HD)
                        last = nc.scalar.activation(out[:, :, HD * half:HD * half + HD], src[:, :, half, :], ACT.Copy)
                    last.then_inc(v_ready, 1)
                if live(t, 0):
                    act.wait_ge(sub_done, t + 1)
                    flat = sm[p][:, :, :].rearrange("p a b -> p (a b)")
                    nc.scalar.activation(flat, flat, ACT.Exp, scale=1.0 if neg is not None else scale)\
                        .then_inc(p_ready, 1)
                if live(t, 1):
                    act.wait_ge(t_done, t)
                    wait(act, o_done, t - 2)
                    nc.scalar.activation(pT[1 - p][:, :, :].rearrange("p a b -> p (a b)"), ps_t[:, :], ACT.Copy)\
                        .then_inc(pT_ready, 1)
                if live(t, 3):
                    act.wait_ge(ot_done, t - 2)
                    wait(act, w_done, t - 4)
                    nc.scalar.activation(onT[1 - p][:, :], ps_o[:, 2 * P:3 * P], ACT.Copy).then_inc(onT_ready, 1)

            rotate(act, step)

        @block.vector
        def _(dve):
            for i in range(2):
                nc.vector.memset(vaug[i][:, :], 0.0)
            dve.drain()
            for i in range(2):
                for half in range(2):
                    rows = slice(64 * half, 64 * half + 64)
                    for j in range(8):
                        c = j * NA + D + 2 * j + half
                        last = nc.vector.memset(vaug[i][rows, c:c + 1], 1.0)
            last.then_inc(zeroed, 1)

            def step(t, r, b):
                p = r % 2
                if live(t, 0):
                    dve.wait_ge(s_done, t + 1)
                    wait(dve, t_done, t - 1)
                    s3 = ps_s[p][:, :].rearrange("p (h k) -> p h k", k=KEYS)
                    if neg is not None:
                        tile = neg[:, bass.ds(t, 1), :] if neg.shape[1] == TILES else neg[:, r % 2:r % 2 + 1, :]
                        nc.vector.scalar_tensor_tensor(out=sm[p][:, :, :], in0=s3, scalar=scale,
                                                       in1=tile.broadcast_to([P, HEADS, KEYS]),
                                                       op0=ALU.mult, op1=ALU.add).then_inc(s_used, 1)
                        s3 = sm[p][:, :, :]
                        dve.drain()
                    nc.vector.tensor_reduce(mx[p][:, :], s3, X, ALU.max)
                    dve.drain()
                    last = nc.vector.tensor_tensor(sm[p][:, :, :], s3,
                                                   mx[p][:, :].unsqueeze(2).broadcast_to([P, HEADS, KEYS]), ALU.subtract)
                    last.then_inc(sub_done, 1)
                if live(t, 2):
                    dve.wait_ge(o_done, t - 1)
                    wait(dve, ot_done, t - 3)
                    nc.vector.reciprocal(rden[:, :], ps_o[:, D:NA])
                    dve.drain()
                    nc.vector.tensor_tensor(on[p][:, :].rearrange("p (h d) -> p h d", d=HD),
                                            ps_o[:, 0:D].rearrange("p (h d) -> p h d", d=HD),
                                            rden[:, :].unsqueeze(2).broadcast_to([P, HEADS, HD]), ALU.mult)\
                        .then_inc(on_ready, 1)
                if live(t, 4):
                    dve.wait_ge(w_done, t - 3)
                    row = x[:, bass.ds(t - 4, 1), :].rearrange("p a b -> p (a b)")
                    nc.vector.tensor_tensor(row, row, ps_w[:, 0:P], ALU.add).then_inc(x_done, 1)

            rotate(dve, step)



def project_wide(nc, tag, w, ctxT, kT_all, vT_all):
    with ExitStack() as stack:
        m = Memory(nc, stack, tag)
        pb = [m.ps(f"pb{i}") for i in range(4)]
        done, out = m.sem("done"), m.sem("out")
        block = stack.enter_context(nc.Block())

        @block.tensor
        def _(pe):
            n = 0
            for name in ("wk", "wv"):
                for j in range(8):
                    if n >= 4:
                        pe.wait_ge(out, n - 3)
                    nc.tensor.matmul(pb[n % 4][:, :], w[name][:, j * P:(j + 1) * P], ctxT[:, :],
                                     start=True, stop=True).then_inc(done, 1)
                    n += 1

        @block.scalar
        def _(act):
            n = 0
            for bias, dst in (("bk", kT_all), ("bv", vT_all)):
                for j in range(8):
                    act.wait_ge(done, n + 1)
                    nc.scalar.activation(dst[:, j, :], pb[n % 4][:, :], ACT.Identity,
                                         bias=w[bias][:, j:j + 1]).then_inc(out, 1)
                    n += 1


def attend_wide(nc, tag, x, w, zT, kT_all, vT_all, ident, neg):
    scale = 0.125
    with ExitStack() as stack:
        m = Memory(nc, stack, tag)
        qT = [m.sb(f"qT{i}", [P, 8, P]) for i in range(2)]
        kbd = [m.sb(f"kbd{i}", [P, 8, 2, KEYS]) for i in range(2)]
        vbd = m.sb("vbd", [P, 8, 2, KEYS])
        vw = [m.sb(f"vw{i}", [P, 8, D]) for i in range(2)]
        sm = [m.sb(f"sm{i}", [P, HEADS, KEYS]) for i in range(2)]
        mx = [m.sb(f"mx{i}", [P, HEADS]) for i in range(2)]
        den = [m.sb(f"den{i}", [P, HEADS]) for i in range(2)]
        pT = [m.sb(f"pT{i}", [P, 8, P]) for i in range(2)]
        ps_q = m.ps("ps_q", 1024)
        ps_s = m.ps("ps_s", 1024)
        ps_t = m.ps("ps_t", 1024)
        ps_v = m.ps("ps_v", 512)
        ps_o = m.ps("ps_o", 512)
        (zeroed, k_ready, v_ready, vw_done, vw_ready, q_done, qT_ready, s_done, s_used, sub_done, exp_done,
         den_ready, p_ready, t_done, pT_ready, o_done, x_done) = (m.sem(n) for n in (
             "zeroed", "k_ready", "v_ready", "vw_done", "vw_ready", "q_done", "qT_ready", "s_done", "s_used",
             "sub_done", "exp_done", "den_ready", "p_ready", "t_done", "pT_ready", "o_done", "x_done"))
        block = stack.enter_context(nc.Block())

        @block.gpsimd
        def _(pool):
            nc.gpsimd.memset(vbd[:, :, :, :], 0.0)
            for i in range(2):
                last = nc.gpsimd.memset(kbd[i][:, :, :, :], 0.0)
            last.then_inc(zeroed, 1)

            def step(t, r, b):
                if live(t, 1):
                    pool.wait_ge(den_ready, t)
                    tile = sm[(r - 1) % 2][:, :, :]
                    nc.gpsimd.tensor_tensor(tile, tile, den[(r - 1) % 2][:, :].unsqueeze(2)
                                            .broadcast_to([P, HEADS, KEYS]), ALU.mult).then_inc(p_ready, 1)

            rotate(pool, step, 1)

        @block.tensor
        def _(pe):
            def step(t, r, b):
                p = r % 2
                if live(t, 0):
                    wait(pe, qT_ready, t)
                    for j in range(8):
                        last = nc.tensor.matmul(ps_q[:, j * P:(j + 1) * P], w["wq"][:, j * P:(j + 1) * P],
                                                zT[:, ds(t, P)], start=True, stop=True)
                    last.then_inc(q_done, 1)
                if live(t, 1):
                    pe.wait_ge(p_ready, t)
                    wait(pe, pT_ready, t - 1)
                    for j in range(8):
                        last = nc.tensor.transpose(ps_t[:, j * P:(j + 1) * P],
                                                   sm[1 - p][:, 2 * j:2 * j + 2, :].rearrange("p a b -> p (a b)"), ident)
                    last.then_inc(t_done, 1)
                if live(t, 0):
                    pe.wait_ge(qT_ready, t + 1)
                    pe.wait_ge(k_ready, b + 1)
                    wait(pe, s_used, t)
                    for j in range(8):
                        last = nc.tensor.matmul(ps_s[:, j * P:(j + 1) * P], qT[p][:, j, :],
                                                kbd[r // 2][:, j, :, :].rearrange("p a b -> p (a b)"),
                                                start=True, stop=True)
                    last.then_inc(s_done, 1)
                if live(t, 2):
                    pe.wait_ge(pT_ready, t - 1)
                    wait(pe, x_done, t - 2)
                    vb = ((r - 2) % 4) // 2
                    for j in range(8):
                        last = nc.tensor.matmul(ps_o[:, 0:D], pT[p][:, j, :], vw[vb][:, j, :],
                                                start=j == 0, stop=j == 7)
                    last.then_inc(o_done, 1)
                if live(t, 0) and p == 0:
                    pe.wait_ge(v_ready, b + 1)
                    for half in range(2):
                        wait(pe, vw_ready, b * 2 + half)
                        for j in range(4 * half, 4 * half + 4):
                            last = nc.tensor.matmul(ps_v[:, (j % 4) * P:(j % 4 + 1) * P],
                                                    vbd[:, j, :, :].rearrange("p a b -> p (a b)"), w["wo"][:, j, :],
                                                    start=True, stop=True)
                        last.then_inc(vw_done, 1)

            rotate(pe, step, 2)

        @block.scalar
        def _(act):
            act.wait_ge(zeroed, 1)

            def step(t, r, b):
                p = r % 2
                if live(t, 0) and p == 0:
                    wait(act, s_done, t - 2)
                    for half in range(2):
                        rows = slice(64 * half, 64 * half + 64)
                        last = nc.scalar.activation(kbd[r // 2][rows, :, half, :], kT_all[rows, :, ds(b, KEYS)], ACT.Copy)
                    last.then_inc(k_ready, 1)
                    wait(act, vw_done, b * 2)
                    for half in range(2):
                        rows = slice(64 * half, 64 * half + 64)
                        last = nc.scalar.activation(vbd[rows, :, half, :], vT_all[rows, :, ds(b, KEYS)], ACT.Copy)
                    last.then_inc(v_ready, 1)
                if live(t, 1):
                    act.wait_ge(t_done, t)
                    wait(act, o_done, t - 2)
                    nc.scalar.activation(pT[1 - p][:, :, :].rearrange("p a b -> p (a b)"), ps_t[:, :], ACT.Copy)\
                        .then_inc(pT_ready, 1)
                if live(t, 0):
                    act.wait_ge(sub_done, t + 1)
                    flat = sm[p][:, :, :].rearrange("p a b -> p (a b)")
                    nc.scalar.activation(flat, flat, ACT.Exp).then_inc(exp_done, 1)
                    if p == 0:
                        wait(act, o_done, t - 2)
                        for half in range(2):
                            act.wait_ge(vw_done, b * 2 + half + 1)
                            nc.scalar.activation(vw[r // 2][:, 4 * half:4 * half + 4, :].rearrange("p a b -> p (a b)"),
                                                 ps_v[:, :], ACT.Copy).then_inc(vw_ready, 1)

            rotate(act, step, 1)

        @block.vector
        def _(dve):
            def step(t, r, b):
                p = r % 2
                if live(t, 0):
                    dve.wait_ge(q_done, t + 1)
                    wait(dve, s_done, t - 1)
                    nc.vector.tensor_tensor(qT[p][:, :, :], ps_q[:, :].rearrange("p (j q) -> p j q", q=P),
                                            w["bq"][:, :].unsqueeze(2).broadcast_to([P, 8, P]), ALU.add)\
                        .then_inc(qT_ready, 1)
                    dve.wait_ge(s_done, t + 1)
                    wait(dve, t_done, t - 1)
                    tile = neg[:, bass.ds(t, 1), :]
                    nc.vector.scalar_tensor_tensor(out=sm[p][:, :, :], in0=ps_s[:, :].rearrange("p (h k) -> p h k", k=KEYS),
                                                   scalar=scale, in1=tile.broadcast_to([P, HEADS, KEYS]),
                                                   op0=ALU.mult, op1=ALU.add).then_inc(s_used, 1)
                    dve.drain()
                    nc.vector.tensor_reduce(mx[p][:, :], sm[p][:, :, :], X, ALU.max)
                    dve.drain()
                    nc.vector.tensor_tensor(sm[p][:, :, :], sm[p][:, :, :],
                                            mx[p][:, :].unsqueeze(2).broadcast_to([P, HEADS, KEYS]), ALU.subtract)\
                        .then_inc(sub_done, 1)
                if live(t, 2):
                    dve.wait_ge(o_done, t - 1)
                    row = x[:, bass.ds(t - 2, 1), :].rearrange("p a b -> p (a b)")
                    nc.vector.tensor_tensor(row, row, ps_o[:, 0:D], ALU.add).then_inc(x_done, 1)
                if live(t, 0):
                    dve.wait_ge(exp_done, t + 1)
                    wait(dve, p_ready, t - 1)
                    nc.vector.reduce_sum(den[p][:, :], sm[p][:, :, :], X)
                    dve.drain()
                    nc.vector.reciprocal(den[p][:, :], den[p][:, :]).then_inc(den_ready, 1)

            rotate(dve, step, 2)



def project_self(nc, tag, w, zT, ident, qT_all, kT_all, v_all, eps_tile):
    with ExitStack() as stack:
        m = Memory(nc, stack, tag)
        zs = [m.sb(f"zs{i}", [P, P]) for i in range(2)]
        qk = m.sb("qk", [P, TILES, 2 * D])
        sq = [m.sb(f"sq{i}", [P, 2 * D]) for i in range(2)]
        ms = m.sb("ms", [P, TILES, 2 * HEADS])
        ps_p = [m.ps(f"ps_p{i}") for i in range(2)]
        ps_t = [m.ps(f"ps_t{i}") for i in range(2)]
        (z_ready, p_done, sq_ready, ms_ready, root_ready, n_ready, t_done, t_used) = (m.sem(n) for n in (
            "z_ready", "p_done", "sq_ready", "ms_ready", "root_ready", "n_ready", "t_done", "t_used"))
        block = stack.enter_context(nc.Block())
        msf = ms[:, :, :].rearrange("p a b -> p (a b)")

        @block.gpsimd
        def _(pool):
            with pool.Fori(0, TILES // 2) as i:
                for r in range(2):
                    t = i * 2 + r
                    pool.wait_ge(p_done, i * 2)
                    nc.gpsimd.tensor_copy(zs[r][:, :], zT[:, ds(t, P)]).then_inc(z_ready, 1)

        @block.tensor
        def _(pe):
            with pe.Fori(0, TILES // 2) as i:
                for r in range(2):
                    t = i * 2 + r
                    pe.wait_ge(z_ready, t + 1)
                    pe.wait_ge(ms_ready, i * 2)
                    nc.tensor.matmul(ps_p[r][:, 0:3 * D], zs[r][:, :], w["wqkv"][:, :],
                                     start=True, stop=True).then_inc(p_done, 1)
            for t in range(TILES):
                pe.wait_ge(n_ready, t + 1)
                if t >= 2:
                    pe.wait_ge(t_used, t - 1)
                for half in range(2):
                    last = nc.tensor.transpose(ps_t[t % 2][:, half * P:(half + 1) * P],
                                               qk[:, t, half * D:(half + 1) * D], ident)
                last.then_inc(t_done, 1)

        @block.scalar
        def _(act):
            with act.Fori(0, TILES // 2) as i:
                for r in range(2):
                    t = i * 2 + r
                    act.wait_ge(p_done, t + 1)
                    act.wait_ge(ms_ready, i * 2)
                    nc.scalar.activation(sq[r][:, :], ps_p[r][:, 0:2 * D], ACT.Square).then_inc(sq_ready, 1)
            act.wait_ge(ms_ready, TILES)
            nc.scalar.activation(msf, msf, ACT.Sqrt, bias=eps_tile, scale=1.0 / HD).then_inc(root_ready, 1)

        @block.vector
        def _(dve):
            with dve.Fori(0, TILES // 2) as i:
                for r in range(2):
                    t = i * 2 + r
                    dve.wait_ge(sq_ready, t + 1)
                    nc.vector.tensor_copy(qk[:, bass.ds(t, 1), :].rearrange("p a b -> p (a b)"), ps_p[r][:, 0:2 * D])
                    nc.vector.tensor_copy(v_all[:, bass.ds(t, 1), :].rearrange("p a b -> p (a b)"), ps_p[r][:, 2 * D:3 * D])
                    nc.vector.reduce_sum(ms[:, bass.ds(t, 1), :].rearrange("p a b -> p (a b)"),
                                         sq[r][:, :].rearrange("p (h d) -> p h d", d=HD), X).then_inc(ms_ready, 1)
            dve.wait_ge(root_ready, 1)
            nc.vector.reciprocal(msf, msf)
            dve.drain()
            with dve.Fori(0, TILES) as t:
                tile = qk[:, bass.ds(t, 1), :].rearrange("p a (h d) -> p (a h) d", d=HD)
                scale = ms[:, bass.ds(t, 1), :].rearrange("p a h -> p (a h)").unsqueeze(2).broadcast_to([P, 2 * HEADS, HD])
                nc.vector.tensor_tensor(tile, tile, scale, ALU.mult).then_inc(n_ready, 1)
            for t in range(TILES):
                dve.wait_ge(t_done, t + 1)
                nc.vector.tensor_scalar(qT_all[:, t * P:(t + 1) * P], ps_t[t % 2][:, 0:P], w["qn"][:, 0:1], None, ALU.mult)
                nc.vector.tensor_scalar(kT_all[:, t * P:(t + 1) * P], ps_t[t % 2][:, P:2 * P], w["kn"][:, 0:1], None,
                                        ALU.mult).then_inc(t_used, 1)


def attend_self(nc, tag, x2, w, qT_all, kT_all, v_all, ident, headmask, causal, ident_b):
    scale = float(HD) ** -0.5
    NA = D + HEADS
    CH = 12
    with ExitStack() as stack:
        m = Memory(nc, stack, tag)
        qs = [m.sb(f"qs{i}", [P, P]) for i in range(2)]
        keys = m.sb("keys", [P, S])
        kbd = m.sb("kbd", [P, HEADS, S])
        vaug = [m.sb(f"vaug{i}", [P, HEADS * (NA + HD)]) for i in range(2)]
        sm = [m.sb(f"sm{i}", [P, 512]) for i in range(3)]
        mx = [m.sb(f"mx{i}", [P, 4]) for i in range(2)]
        pT = [m.sb(f"pT{i}", [P, 4, P]) for i in range(2)]
        rden = m.sb("rden", [P, HEADS])
        on = m.sb("on", [P, D])
        onT = m.sb("onT", [P, P])
        ps_s = [m.ps(f"ps_s{i}") for i in range(2)]
        ps_t = [m.ps(f"ps_t{i}") for i in range(2)]
        ps_o = [m.ps(f"ps_o{i}") for i in range(2)]
        ps_w = m.ps("ps_w")
        (zeroed, q_ready, k_ready, v_ready, s_done, sub_done, p_ready, t_done, pT_ready, pv_done, on_ready,
         ot_done, onT_ready, w_done, x_done) = (m.sem(n) for n in (
             "zeroed", "q_ready", "k_ready", "v_ready", "s_done", "sub_done", "p_ready", "t_done", "pT_ready",
             "pv_done", "on_ready", "ot_done", "onT_ready", "w_done", "x_done"))
        block = stack.enter_context(nc.Block())

        def rotate_chunks(eng, step, lags):
            for r in range(CH):
                step(r, r, 0)
            with eng.Fori(1, B) as b:
                for r in range(CH):
                    step(b * CH + r, r, b)
            for r in range(lags):
                step(B * CH + r, r, B)

        def alive(n, lag):
            return not isinstance(n, int) or 0 <= n - lag < B * CH

        def blocks(r):
            if r < 4:
                return [(4 * r + i, 0, 128 * i) for i in range(4)]
            return [(2 * (r - 4) + i // 2, i % 2, 128 * i) for i in range(4)]

        NORMALISE = {7: 0, 15: 1}
        TURN = {8: 0, 16: 1}
        PROJECT = {10: 0, 18: 1}
        ADD = {11: 0, 19: 1}

        def finishing(table, r, b):
            for at, par in table.items():
                if at == r and not (isinstance(b, int) and b >= B):
                    return par, b * 2 + par
                if at == r + CH and not (isinstance(b, int) and b == 0):
                    return par, (b - 1) * 2 + par
            return None

        @block.gpsimd
        def _(pool):
            def fill(b):
                def q_copy(par):
                    nc.gpsimd.tensor_copy(qs[par][:, :], qT_all[:, ds(b * 2 + par, P)]).then_inc(q_ready, 1)
                wait(pool, s_done, b * CH - CH + 4)
                q_copy(0)
                nc.gpsimd.tensor_copy(keys[:, :], kT_all[:, ds(b, S)])
                pool.drain()
                for g in range(4):
                    wait(pool, s_done, b * CH - CH + 6 + 2 * g)
                    hs = slice(4 * g, 4 * g + 4)
                    nc.gpsimd.tensor_tensor(kbd[:, hs, :],
                                            keys[:, :].unsqueeze(1).broadcast_to([P, 4, S]),
                                            headmask[:, hs].unsqueeze(2).broadcast_to([P, 4, S]),
                                            ALU.mult).then_inc(k_ready, 1)
                q_copy(1)
                wait(pool, pv_done, b * CH)
                for kb in range(2):
                    out = vaug[kb][:, :].rearrange("p (h c) -> p h c", c=NA + HD)[:, :, 0:HD]
                    src = v_all[:, bass.ds(b * 2 + kb, 1), :].rearrange("p a (h d) -> p (a h) d", d=HD)
                    nc.gpsimd.tensor_copy(out, src).then_inc(v_ready, 1)

            pool.wait_ge(zeroed, 1)
            fill(0)
            with pool.Fori(1, B) as b:
                fill(b)

        @block.tensor
        def _(pe):
            def step(n, r, b):
                if alive(n, 0):
                    if r in (0, 4):
                        pe.wait_ge(q_ready, b * 2 + 1 + r // 4)
                    if r < 4:
                        pe.wait_ge(k_ready, b * 4 + r + 1)
                    wait(pe, sub_done, n - 1)
                    out = ps_s[r % 2]
                    if r < 4:
                        keys = kbd[:, 4 * r:4 * r + 4, 0:P]
                        out3 = out[:, :].rearrange("p (h k) -> p h k", k=P)
                        diag, heads = out3, 4
                    else:
                        keys = kbd[:, 2 * (r - 4):2 * (r - 4) + 2, :]
                        out3 = out[:, :].rearrange("p (h k) -> p h k", k=S)
                        diag, heads = out3[:, :, P:S], 2
                    nc.tensor.matmul(out3, qs[r // 4 if r < 4 else 1][:, :], keys, start=True, stop=False)
                    nc.tensor.matmul(diag, ident_b, causal.unsqueeze(1).broadcast_to([P, heads, P]),
                                     start=False, stop=True).then_inc(s_done, 1)
                if alive(n, 2):
                    pe.wait_ge(p_ready, n - 1)
                    wait(pe, pT_ready, n - 3)
                    for i in range(4):
                        last = nc.tensor.transpose(ps_t[r % 2][:, i * P:(i + 1) * P],
                                                   sm[(r + 1) % 3][:, i * P:(i + 1) * P], ident)
                    last.then_inc(t_done, 1)
                if alive(n, 3):
                    pe.wait_ge(pT_ready, n - 2)
                    c = (r - 3) % CH
                    par = 0 if c < 4 else 1
                    if c in (0, 4):
                        pe.wait_ge(v_ready, b * 2 + par + 1)
                        wait(pe, on_ready, b * 2 + par - 1)
                    for i, (h, kb, col) in enumerate(blocks(c)):
                        last = nc.tensor.matmul(ps_o[par][:, 0:NA], pT[(r - 3) % 2][:, i, :],
                                                vaug[kb][:, h * NA:(h + 1) * NA],
                                                start=c in (0, 4) and i == 0, stop=c in (3, 11) and i == 3)
                    last.then_inc(pv_done, 1)
                if found := finishing(TURN, r, b):
                    par, tile = found
                    pe.wait_ge(on_ready, tile + 1)
                    wait(pe, x_done, tile)
                    nc.tensor.transpose(ps_w[:, 0:P], on[:, :], ident).then_inc(ot_done, 1)
                if found := finishing(PROJECT, r, b):
                    par, tile = found
                    pe.wait_ge(onT_ready, tile + 1)
                    nc.tensor.matmul(ps_w[:, P:2 * P], onT[:, :], w["wo"][:, :], start=True, stop=True)\
                        .then_inc(w_done, 1)

            rotate_chunks(pe, step, 8)

        @block.scalar
        def _(act):
            def step(n, r, b):
                if alive(n, 2):
                    act.wait_ge(t_done, n - 1)
                    wait(act, pv_done, n - 3)
                    nc.scalar.activation(pT[r % 2][:, :, :].rearrange("p a b -> p (a b)"), ps_t[r % 2][:, :],
                                         ACT.Copy).then_inc(pT_ready, 1)
                if alive(n, 0):
                    act.wait_ge(sub_done, n + 1)
                    nc.scalar.activation(sm[r % 3][:, :], sm[r % 3][:, :], ACT.Exp, scale=scale).then_inc(p_ready, 1)
                if found := finishing(TURN, r, b):
                    par, tile = found
                    act.wait_ge(ot_done, tile + 1)
                    wait(act, w_done, tile)
                    nc.scalar.activation(onT[:, :], ps_w[:, 0:P], ACT.Copy).then_inc(onT_ready, 1)

            rotate_chunks(act, step, 8)

        @block.vector
        def _(dve):
            for kb in range(2):
                nc.vector.memset(vaug[kb][:, :], 0.0)
            dve.drain()
            for kb in range(2):
                ones = vaug[kb][:, 0:HEADS * (NA + 1)].rearrange("p (h c) -> p h c", c=NA + 1)[:, :, D:D + 1]
                last = nc.vector.memset(ones, 1.0)
            last.then_inc(zeroed, 1)

            def step(n, r, b):
                if alive(n, 0):
                    heads = 4 if r < 4 else 2
                    dve.wait_ge(s_done, n + 1)
                    wait(dve, t_done, n - 2)
                    s3 = ps_s[r % 2][:, :].rearrange("p (h k) -> p h k", h=heads)
                    nc.vector.tensor_reduce(mx[r % 2][:, 0:heads], s3, X, ALU.max)
                    dve.drain()
                    nc.vector.tensor_tensor(sm[r % 3][:, :].rearrange("p (h k) -> p h k", h=heads), s3,
                                            mx[r % 2][:, 0:heads].unsqueeze(2).broadcast_to([P, heads, 512 // heads]),
                                            ALU.subtract).then_inc(sub_done, 1)
                if found := finishing(NORMALISE, r, b):
                    par, tile = found
                    dve.wait_ge(pv_done, (b if r == 7 else b - 1) * CH + (4 if par == 0 else CH))
                    wait(dve, ot_done, tile)
                    nc.vector.reciprocal(rden[:, :], ps_o[par][:, D:NA])
                    dve.drain()
                    nc.vector.tensor_tensor(on[:, :].rearrange("p (h d) -> p h d", d=HD),
                                            ps_o[par][:, 0:D].rearrange("p (h d) -> p h d", d=HD),
                                            rden[:, :].unsqueeze(2).broadcast_to([P, HEADS, HD]), ALU.mult)\
                        .then_inc(on_ready, 1)
                if found := finishing(ADD, r, b):
                    par, tile = found
                    dve.wait_ge(w_done, tile + 1)
                    row = x2[:, bass.ds(tile, 1), KEEP:D].rearrange("p a b -> p (a b)")
                    nc.vector.tensor_tensor(row, row, ps_w[:, P + KEEP:2 * P], ALU.add).then_inc(x_done, 1)

            rotate_chunks(dve, step, 8)



def attend_two_way(nc, tag, x, w, zT, ctxT, ctx_nat, ident, ones):
    with ExitStack() as stack:
        m = Memory(nc, stack, tag)
        R = m.sb("R", [P, B * KEYS + KEYS])
        qrow = m.sb("qrow", [P, B * KEYS])
        wq_bc = m.sb("wq_bc", [P, P])
        const = m.sb("const", [P, 1])
        two = range(2)
        zs = [m.sb(f"zs{i}", [P, S]) for i in two]
        cn = [m.sb(f"cn{i}", [KEYS, D]) for i in two]
        a = [m.sb(f"a{i}", [P, TPB, KEYS]) for i in two]
        mx = [m.sb(f"mx{i}", [P, TPB]) for i in two]
        rs = [m.sb(f"rs{i}", [P, TPB]) for i in two]
        aT = [m.sb(f"aT{i}", [KEYS, S]) for i in two]
        row = [m.sb(f"row{i}", [1, S]) for i in two]
        one = [m.sb(f"one{i}", [1, 2]) for i in two]
        c2q = [m.sb(f"c2q{i}", [P, S]) for i in two]
        prod = [m.sb(f"prod{i}", [P, S]) for i in two]
        tmp = [m.sb(f"tmp{i}", [P, S]) for i in two]
        q2c = [m.sb(f"q2c{i}", [P, 1]) for i in two]
        w14 = [m.sb(f"w14{i}", [P, D]) for i in two]
        ps_s = [m.ps(f"ps_s{i}") for i in two]
        ps_a = [m.ps(f"ps_a{i}") for i in two]
        ps_c = [m.ps(f"ps_c{i}") for i in two]
        ps_q = m.ps("ps_q")
        (wq_ready, qrow_done, set_up, slots_ready, s_done, sub_done, exp_done, a_ready, a_turned, aT_ready,
         row_sub, row_exp, row_ready, c_done, c2q_ready, ready, o_done, x_done) = (m.sem(n) for n in (
             "wq_ready", "qrow_done", "set_up", "slots_ready", "s_done", "sub_done", "exp_done", "a_ready",
             "a_turned", "aT_ready", "row_sub", "row_exp", "row_ready", "c_done", "c2q_ready", "ready",
             "o_done", "x_done"))
        block = stack.enter_context(nc.Block())

        @block.gpsimd
        def _(pool):
            with pool.Fori(0, B // 2) as i:
                pool.wait_ge(x_done, i * 2)
                for r in two:
                    nc.gpsimd.tensor_copy(zs[r][:, :], zT[:, ds(i * 2 + r, S)])
                    nc.gpsimd.tensor_copy(cn[r][:, :], ctx_nat[:, bass.ds(i * 2 + r, 1), :]
                                          .rearrange("p a b -> p (a b)")).then_inc(slots_ready, 1)

        @block.tensor
        def _(pe):
            pe.wait_ge(wq_ready, 1)
            nc.tensor.matmul(ps_q[:, :], wq_bc[:, :], ctxT[:, :], start=True, stop=True).then_inc(qrow_done, 1)
            pe.wait_ge(set_up, 1)
            with pe.Fori(0, B // 2) as i:
                for r in two:
                    pe.wait_ge(slots_ready, i * 2 + r + 1)
                    for j in range(TPB):
                        last = nc.tensor.matmul(ps_s[r][:, j * P:(j + 1) * P], zs[r][:, j * P:(j + 1) * P],
                                                R[:, bass.ds((i * 2 + r) * KEYS, 2 * KEYS)], start=True, stop=True)
                    last.then_inc(s_done, 1)
                for r in two:
                    pe.wait_ge(a_ready, i * 2 + r + 1)
                    for j in range(TPB):
                        nc.tensor.transpose(ps_a[r][0:1, S + j * P:S + (j + 1) * P], mx[r][:, j:j + 1], ident)
                    for j in range(TPB):
                        last = nc.tensor.transpose(ps_a[r][0:KEYS, j * P:(j + 1) * P], a[r][:, j, :], ident)
                    last.then_inc(a_turned, 1)
                for r in two:
                    pe.wait_ge(aT_ready, i * 2 + r + 1)
                    nc.tensor.matmul(ps_c[r][:, 0:S], cn[r][:, :], aT[r][:, :], start=True, stop=True)
                    pe.wait_ge(row_ready, i * 2 + r + 1)
                    nc.tensor.matmul(ps_c[r][:, S:2 * S], ones, row[r][:, :], start=True, stop=True)\
                        .then_inc(c_done, 1)
                for r in two:
                    pe.wait_ge(ready, i * 2 + r + 1)
                    for j in range(TPB):
                        cols = slice(j * P, (j + 1) * P)
                        out = ps_s[r][:, S + j * P:S + (j + 1) * P]
                        nc.tensor.matmul(out, zs[r][:, cols], w14[r][:, :], start=True, stop=False)
                        nc.tensor.matmul(out, c2q[r][:, cols], w["wl"][:, 1, :], start=False, stop=False)
                        last = nc.tensor.matmul(out, prod[r][:, cols], w["wl"][:, 2, :], start=False, stop=True)
                    last.then_inc(o_done, 1)

        @block.scalar
        def _(act):
            with act.Fori(0, B // 2) as i:
                for r in two:
                    act.wait_ge(sub_done, i * 2 + r + 1)
                    flat = a[r][:, :, :].rearrange("p a b -> p (a b)")
                    nc.scalar.activation(flat, flat, ACT.Exp).then_inc(exp_done, 1)
                for r in two:
                    act.wait_ge(a_turned, i * 2 + r + 1)
                    nc.scalar.activation(aT[r][:, :], ps_a[r][0:KEYS, 0:S], ACT.Copy).then_inc(aT_ready, 1)
                    act.wait_ge(row_sub, i * 2 + r + 1)
                    nc.scalar.activation(row[r][:, :], row[r][:, :], ACT.Exp).then_inc(row_exp, 1)
                for r in two:
                    act.wait_ge(c_done, i * 2 + r + 1)
                    nc.scalar.activation(c2q[r][:, :], ps_c[r][:, 0:S], ACT.Copy).then_inc(c2q_ready, 1)

        @block.vector
        def _(dve):
            nc.vector.tensor_copy(wq_bc[:, :], w["w_q"][:, 0:1].broadcast_to([P, P]))
            nc.vector.tensor_tensor(const[:, :], w["b_q"][:, 0:1], w["b_c"][:, 0:1], ALU.add).then_inc(wq_ready, 1)
            nc.vector.tensor_scalar(R[:, 0:B * KEYS], ctxT[:, :], w["w_cq"][:, 0:1], w["w_c"][:, 0:1],
                                    ALU.mult, ALU.add)
            nc.vector.memset(R[:, B * KEYS:], 0.0)
            dve.drain()
            nc.vector.tensor_tensor(const[:, :], const[:, :], w["b_cq"][:, 0:1], ALU.add)
            dve.drain()
            dve.wait_ge(qrow_done, 1)
            nc.vector.tensor_scalar(qrow[:, :], ps_q[:, :], const[:, 0:1], None, ALU.add).then_inc(set_up, 1)
            dve.drain()
            with dve.Fori(0, B // 2) as i:
                for r in two:
                    dve.wait_ge(s_done, i * 2 + r + 1)
                    nc.vector.tensor_tensor(a[r][:, :, :],
                                            ps_s[r][:, 0:S].rearrange("p (j k) -> p j k", k=P)[:, :, 0:KEYS],
                                            qrow[:, ds(i * 2 + r, KEYS)].unsqueeze(1).broadcast_to([P, TPB, KEYS]),
                                            ALU.add)
                    dve.drain()
                    nc.vector.tensor_reduce(mx[r][:, :], a[r][:, :, :], X, ALU.max)
                    dve.drain()
                    nc.vector.tensor_tensor(a[r][:, :, :], a[r][:, :, :],
                                            mx[r][:, :].unsqueeze(2).broadcast_to([P, TPB, KEYS]), ALU.subtract)\
                        .then_inc(sub_done, 1)
                for r in two:
                    dve.wait_ge(exp_done, i * 2 + r + 1)
                    nc.vector.reduce_sum(rs[r][:, :], a[r][:, :, :], X)
                    dve.drain()
                    nc.vector.reciprocal(rs[r][:, :], rs[r][:, :])
                    dve.drain()
                    nc.vector.tensor_tensor(a[r][:, :, :], a[r][:, :, :],
                                            rs[r][:, :].unsqueeze(2).broadcast_to([P, TPB, KEYS]), ALU.mult)\
                        .then_inc(a_ready, 1)
                for r in two:
                    dve.wait_ge(aT_ready, i * 2 + r + 1)
                    nc.vector.tensor_reduce(one[r][:, 0:1], ps_a[r][0:1, S:2 * S], X, ALU.max)
                    dve.drain()
                    nc.vector.tensor_scalar(row[r][:, :], ps_a[r][0:1, S:2 * S], one[r][:, 0:1], None, ALU.subtract)\
                        .then_inc(row_sub, 1)
                for r in two:
                    dve.wait_ge(row_exp, i * 2 + r + 1)
                    nc.vector.reduce_sum(one[r][:, 1:2], row[r][:, :], X)
                    dve.drain()
                    nc.vector.reciprocal(one[r][:, 1:2], one[r][:, 1:2])
                    dve.drain()
                    nc.vector.tensor_scalar(row[r][:, :], row[r][:, :], one[r][:, 1:2], None, ALU.mult)\
                        .then_inc(row_ready, 1)
                for r in two:
                    dve.wait_ge(c2q_ready, i * 2 + r + 1)
                    nc.vector.tensor_tensor(tmp[r][:, :], zs[r][:, :], ps_c[r][:, S:2 * S], ALU.mult)
                    dve.drain()
                    nc.vector.reduce_sum(q2c[r][:, :], tmp[r][:, :], X)
                    dve.drain()
                    nc.vector.scalar_tensor_tensor(out=w14[r][:, :], in0=w["wl"][:, 3, :], scalar=q2c[r][:, 0:1],
                                                   in1=w["wl"][:, 0, :], op0=ALU.mult, op1=ALU.add)
                    nc.vector.tensor_tensor(prod[r][:, :], zs[r][:, :], c2q[r][:, :], ALU.mult).then_inc(ready, 1)
                for r in two:
                    dve.wait_ge(o_done, i * 2 + r + 1)
                    xs = x[:, bass.ds((i * 2 + r) * TPB, TPB), :]
                    nc.vector.tensor_tensor(xs, xs, ps_s[r][:, S:2 * S].rearrange("p (j d) -> p j d", d=D), ALU.add)\
                        .then_inc(x_done, 1)



def top2_gates(nc, m, dve, act_sem, dve_sem, L, e, G, E, rank, eps):
    sh = [P, TILES, E]
    sel, pick = m.sb("g_sel", sh), m.sb("g_pick", sh)
    rest, key = m.sb("g_rest", sh), m.sb("g_key", sh)
    mx, s1, s2 = m.sb("g_mx", [P, TILES]), m.sb("g_s1", [P, TILES]), m.sb("g_s2", [P, TILES])
    wide = lambda t: t[:, :].unsqueeze(2).broadcast_to(sh)
    ranks = rank[:, 0:E].unsqueeze(1).broadcast_to(sh)

    def first_of_max(values, out):
        nc.vector.tensor_reduce(mx[:, :], values, X, ALU.max)
        dve.drain()
        nc.vector.tensor_tensor(key[:, :, :], values, wide(mx), ALU.is_equal)
        dve.drain()
        nc.vector.tensor_tensor(key[:, :, :], key[:, :, :], ranks, ALU.mult)
        dve.drain()
        nc.vector.tensor_reduce(s1[:, :], key[:, :, :], X, ALU.max)
        dve.drain()
        nc.vector.tensor_tensor(out, key[:, :, :], wide(s1), ALU.is_equal)

    nc.vector.tensor_reduce(mx[:, :], L[:, :, :], X, ALU.max)
    dve.drain()
    nc.vector.tensor_tensor(e[:, :, :], L[:, :, :], wide(mx), ALU.subtract).then_inc(dve_sem, 1)
    dve.drain()
    first_of_max(L[:, :, :], sel[:, :, :])
    dve.drain()
    nc.vector.scalar_tensor_tensor(out=rest[:, :, :], in0=sel[:, :, :], scalar=-3.0e38, in1=L[:, :, :],
                                   op0=ALU.mult, op1=ALU.add)
    dve.drain()
    first_of_max(rest[:, :, :], pick[:, :, :])
    dve.drain()
    nc.vector.tensor_tensor(sel[:, :, :], sel[:, :, :], pick[:, :, :], ALU.add)
    dve.wait_ge(act_sem, 1)
    dve.drain()
    nc.vector.tensor_tensor(sel[:, :, :], sel[:, :, :], e[:, :, :], ALU.mult)
    nc.vector.reduce_sum(s1[:, :], e[:, :, :], X)
    dve.drain()
    nc.vector.reduce_sum(s2[:, :], sel[:, :, :], X)
    dve.drain()
    nc.vector.scalar_tensor_tensor(out=s2[:, :], in0=s1[:, :], scalar=eps, in1=s2[:, :], op0=ALU.mult, op1=ALU.add)
    dve.drain()
    nc.vector.reciprocal(s2[:, :], s2[:, :])
    dve.drain()
    nc.vector.tensor_tensor(G[:, :, :], sel[:, :, :], wide(s2), ALU.mult)
    dve.drain()



def experts_gated(nc, tag, x, zT, L, rank, E, NF, w1, w3, w2):
    U = 2 * GROUPS * NF
    K = 2 * GROUPS
    with ExitStack() as stack:
        m = Memory(nc, stack, tag)
        W1 = [m.sb(f"W1_{i}", [P, NF * P]) for i in range(2)]
        W3 = [m.sb(f"W3_{i}", [P, NF * P]) for i in range(2)]
        W2 = [m.sb(f"W2_{i}", [P, NF, D]) for i in range(2)]
        s = [m.sb(f"s{i}", [P, 512]) for i in range(2)]
        h = [m.sb(f"h{i}", [P, NF, 512]) for i in range(2)]
        G = m.sb("G", [P, TILES, E])
        gate_exp = m.sb("gate_exp", [P, TILES, E])
        ps_a = [m.ps(f"ps_a{i}") for i in range(2)]
        ps_b = [m.ps(f"ps_b{i}") for i in range(2)]
        ps_y = [m.ps(f"ps_y{i}") for i in range(2)]
        w_loaded = [m.sem(f"w_loaded{i}") for i in range(2)]
        logits_shifted, gates_exp = m.sem("logits_shifted"), m.sem("gates_exp")
        up_done, s_ready, h_ready, down_done, added = (m.sem(n) for n in (
            "up_done", "s_ready", "h_ready", "down_done", "added"))
        block = stack.enter_context(nc.Block())

        @block.sync
        def _(sp):
            def load(p, e):
                for dst, src in ((W1[e][:, :], w1), (W3[e][:, :], w3),
                                 (W2[e][:, :, :].rearrange("p a b -> p (a b)"), w2)):
                    sp.dma_start(dst, src[bass.ds(p * 2 + e, 1)].rearrange("a p n -> p (a n)"))\
                        .then_inc(w_loaded[e], 16)

            for e in range(2):
                load(0, e)
            with sp.Fori(1, E // 2) as p:
                for e in range(2):
                    sp.wait_ge(down_done, p * K - K + (e + 1) * GROUPS)
                    load(p, e)

        @block.tensor
        def _(pe):
            with pe.Fori(0, E // 2) as p:
                def down(k, f):
                    if f == 0:
                        pe.wait_ge(added, p * K + (k - 1 if k >= 2 else 0))
                    pe.wait_ge(h_ready, p * U + k * NF + f + 1)
                    for j in range(GROUP):
                        last = nc.tensor.matmul(ps_y[k % 2][:, j * D:(j + 1) * D], h[k % 2][:, f, j * P:(j + 1) * P],
                                                W2[k // GROUPS][:, f, :], start=f == 0 and j == 0, stop=f == NF - 1,
                                                skip_group_check=True)
                    if f == NF - 1:
                        last.then_inc(down_done, 1)

                for k in range(K):
                    e, g = k // GROUPS, k % GROUPS
                    if g == 0:
                        pe.wait_ge(w_loaded[e], p * 48 + 48)
                    for f in range(NF):
                        u = k * NF + f
                        if u >= 2:
                            pe.wait_ge(h_ready, p * U + u - 1)
                        rhs = zT[:, g * 512:(g + 1) * 512]
                        nc.tensor.matmul(ps_a[u % 2][:, :], W1[e][:, f * P:(f + 1) * P], rhs,
                                         start=True, stop=True).then_inc(up_done, 1)
                        nc.tensor.matmul(ps_b[u % 2][:, :], W3[e][:, f * P:(f + 1) * P], rhs,
                                         start=True, stop=True).then_inc(up_done, 1)
                        if k > 0:
                            down(k - 1, f)
                for f in range(NF):
                    down(K - 1, f)

        @block.scalar
        def _(act):
            act.wait_ge(logits_shifted, 1)
            e_flat = gate_exp[:, :, :].rearrange("p a b -> p (a b)")
            nc.scalar.activation(e_flat, e_flat, ACT.Exp).then_inc(gates_exp, 1)
            with act.Fori(0, E // 2) as p:
                for u in range(U):
                    act.wait_ge(up_done, p * 2 * U + 2 * u + 1)
                    if u >= 2:
                        act.wait_ge(h_ready, p * U + u - 1)
                    nc.scalar.activation(s[u % 2][:, :], ps_a[u % 2][:, :], ACT.Silu).then_inc(s_ready, 1)

        @block.vector
        def _(dve):
            top2_gates(nc, m, dve, gates_exp, logits_shifted, L, gate_exp, G, E, rank, 0.0)
            with dve.Fori(0, E // 2) as p:
                def add(k):
                    dve.wait_ge(down_done, p * K + k + 1)
                    for j in range(GROUP):
                        t = (k % GROUPS) * GROUP + j
                        last = nc.vector.scalar_tensor_tensor(
                            out=x[:, t, :], in0=ps_y[k % 2][:, j * D:(j + 1) * D],
                            scalar=G[:, t, bass.ds(p * 2 + k // GROUPS, 1)], in1=x[:, t, :],
                            op0=ALU.mult, op1=ALU.add)
                    last.then_inc(added, 1)

                for k in range(K):
                    for f in range(NF):
                        u = k * NF + f
                        dve.wait_ge(s_ready, p * U + u + 1)
                        dve.wait_ge(up_done, p * 2 * U + 2 * u + 2)
                        if k >= 2 and f == 0:
                            dve.wait_ge(down_done, p * K + k - 1)
                        nc.vector.tensor_tensor(h[k % 2][:, f, :], s[u % 2][:, :], ps_b[u % 2][:, :], ALU.mult)\
                            .then_inc(h_ready, 1)
                    if k > 0:
                        add(k - 1)
                add(K - 1)



def experts_mixed(nc, tag, x, x2, w, zT, L, rank):
    HID = ("a0", "a1", "u0", "u1", "b0", "b1", "g0", "v0", "g1", "v1", "c0", "c1", "d0", "p0", "p1")
    ORDER = HID[:13] + ("y0", "p0", "p1", "y1", "y2", "y3")
    ACT_OPS = ("a0", "a1", "u0", "u1", "b0", "b1", "g0", "g1", "c0", "c1", "d0", "p0", "p1")
    NB = 5
    DOWN = {"y0": (("u0", "u1"), "e0_down", 0), "y1": (("m0", "m1"), "e1_down", 1),
            "y2": (("c0", "c1"), "e2_l4", 2), "y3": (("p0", "p1"), "e3_out", 3)}
    UP = {"a": ("e2_l1", None), "u": ("e0_up", None), "g": ("e1_w1", None), "v": ("e1_w2", None),
          "b": ("e2_l2", ("a0", "a1")), "c": ("e2_l3", ("b0", "b1")), "d": ("e3_down", None), "p": ("e3_up", ("d0",))}
    with ExitStack() as stack:
        m = Memory(nc, stack, tag)
        h = {n: m.sb("h_" + n, [P, 512]) for n in ACT_OPS + ("m0", "m1")}
        G = m.sb("G", [P, TILES, 4])
        gate_exp = m.sb("gate_exp", [P, TILES, 4])
        ps_h = [m.ps(f"ps_h{i}") for i in range(NB)]
        ps_y = [m.ps(f"ps_y{i}") for i in range(2)]
        logits_shifted, gates_exp = m.sem("logits_shifted"), m.sem("gates_exp")
        block_done, act_done, gated_done, down_done, added = (m.sem(n) for n in (
            "block_done", "act_done", "gated_done", "down_done", "added"))
        block = stack.enter_context(nc.Block())
        bank = {n: ps_h[i % NB] for i, n in enumerate(HID)}

        def wait_for(eng, names, g):
            gated = [int(n[1]) + 1 for n in names if n[0] == "m"]
            acts = [ACT_OPS.index(n) + 1 for n in names if n[0] != "m"]
            if gated:
                eng.wait_ge(gated_done, g * 2 + max(gated))
            if acts:
                eng.wait_ge(act_done, g * len(ACT_OPS) + max(acts))

        @block.tensor
        def _(pe):
            with pe.Fori(0, GROUPS) as g:
                for name in ORDER:
                    if name in DOWN:
                        inputs, wn, e = DOWN[name]
                        pe.wait_ge(added, g * 4 + max(0, e - 1))
                        wait_for(pe, inputs, g)
                        for j in range(GROUP):
                            for i, inp in enumerate(inputs):
                                last = nc.tensor.matmul(ps_y[e % 2][:, j * D:(j + 1) * D], h[inp][:, j * P:(j + 1) * P],
                                                        w[wn][:, i, :], start=i == 0, stop=i == 1)
                        last.then_inc(down_done, 1)
                        continue
                    n = HID.index(name)
                    wn, inputs = UP[name[0]]
                    needed = list(inputs or ())
                    if n >= NB:
                        old = HID[n - NB]
                        needed.append("m" + old[1] if old[0] in "gv" else old)
                    wait_for(pe, needed, g)
                    cols = slice(int(name[1]) * P, int(name[1]) * P + P)
                    if inputs is None:
                        last = nc.tensor.matmul(bank[name][:, :], w[wn][:, 0, cols], zT[:, ds(g, 512)],
                                                start=True, stop=True)
                    else:
                        for i, inp in enumerate(inputs):
                            last = nc.tensor.matmul(bank[name][:, :], w[wn][:, i, cols], h[inp][:, :],
                                                    start=i == 0, stop=i == len(inputs) - 1)
                    last.then_inc(block_done, 1)

        @block.scalar
        def _(act):
            act.wait_ge(logits_shifted, 1)
            e_flat = gate_exp[:, :, :].rearrange("p a b -> p (a b)")
            nc.scalar.activation(e_flat, e_flat, ACT.Exp).then_inc(gates_exp, 1)
            with act.Fori(0, GROUPS) as g:
                for name in ACT_OPS:
                    act.wait_ge(block_done, g * len(HID) + HID.index(name) + 1)
                    gate = name[0] == "g"
                    nc.scalar.activation(h[name][:, :], bank[name][:, :], ACT.Tanh if gate else ACT.Gelu,
                                         scale=0.5 if gate else 1.0).then_inc(act_done, 1)

        @block.vector
        def _(dve):
            top2_gates(nc, m, dve, gates_exp, logits_shifted, L, gate_exp, G, 4, rank, 1.0e-8)
            with dve.Fori(0, GROUPS) as g:
                for k in range(2):
                    wait_for(dve, (f"g{k}",), g)
                    tanh, out = h[f"g{k}"][:, :], h[f"m{k}"][:, :]
                    nc.vector.scalar_tensor_tensor(out=tanh, in0=tanh, scalar=1.0, in1=bank[f"g{k}"][:, :],
                                                   op0=ALU.add, op1=ALU.mult)
                    dve.drain()
                    dve.wait_ge(block_done, g * len(HID) + HID.index(f"v{k}") + 1)
                    nc.vector.scalar_tensor_tensor(out=out, in0=tanh, scalar=0.5, in1=bank[f"v{k}"][:, :],
                                                   op0=ALU.mult, op1=ALU.mult).then_inc(gated_done, 1)
                for e in range(4):
                    dve.wait_ge(down_done, g * 4 + e + 1)
                    for j in range(GROUP):
                        row = x2[:, bass.ds(g * GROUP + j, 1), KEEP:D].rearrange("p a b -> p (a b)")
                        last = nc.vector.scalar_tensor_tensor(
                            out=row, in0=ps_y[e % 2][:, j * D + KEEP:(j + 1) * D],
                            scalar=G[:, bass.ds(g * GROUP + j, 1), e], in1=row, op0=ALU.mult, op1=ALU.add)
                    last.then_inc(added, 1)
                    dve.drain()
            nc.vector.tensor_tensor(x[:, :, :], x[:, :, :], x2[:, :, :], ALU.add)



def experts_many(nc, tag, x, zT, L, bias, eg, eu, ed, ident):
    E, W, GRP = 64, 64, 8
    ALL = E + 2
    CE = 6
    CH = ALL // CE
    NC = CE * W
    NBK = NC // P
    SENTINEL = 3.0e38
    with ExitStack() as stack:
        m = Memory(nc, stack, tag)
        zs = m.sb("zs", [P, P])
        s = [m.sb(f"s{i}", [P, NC]) for i in range(3)]
        h = [m.sb(f"h{i}", [P, NC]) for i in range(3)]
        hT = [m.sb(f"hT{i}", [P, NC]) for i in range(3)]
        G = m.sb("G", [P, TILES, ALL])
        grp = m.sb("grp", [P, TILES, 12])
        grp_rest = m.sb("grp_rest", [P, TILES, 12])
        cand = m.sb("cand", [P, TILES, ALL])
        rest = m.sb("rest", [P, TILES, ALL])
        top = m.sb("top", [P, TILES, 8])
        den = m.sb("den", [P, TILES])
        ps_a = [m.ps(f"ps_a{i}") for i in range(3)]
        ps_b = [m.ps(f"ps_b{i}") for i in range(3)]
        ps_t = m.ps("ps_t")
        ps_y = m.ps("ps_y")
        (scores_ready, gates_ready, z_ready, a_done, b_done, s_ready, h_ready, g_ready, t_done, hT_ready,
         down_done, added) = (m.sem(n) for n in (
             "scores_ready", "gates_ready", "z_ready", "a_done", "b_done", "s_ready", "h_ready", "g_ready",
             "t_done", "hT_ready", "down_done", "added"))
        block = stack.enter_context(nc.Block())

        def rotate_chunks(eng, step, lags):
            for c in range(CH):
                step(c, c, 0)
            with eng.Fori(1, TILES) as t:
                for c in range(CH):
                    step(t * CH + c, c, t)
            for c in range(lags):
                step(TILES * CH + c, c, TILES)

        def alive(n, lag):
            return not isinstance(n, int) or 0 <= n - lag < TILES * CH

        def back(c, lag):
            return (c - lag) % CH

        @block.tensor
        def _(pe):
            def step(n, c, t):
                if alive(n, 2):
                    k = back(c, 2)
                    pe.wait_ge(g_ready, n - 1)
                    wait(pe, hT_ready, n - 2)
                    for i in range(NBK):
                        last = nc.tensor.transpose(ps_t[:, i * P:(i + 1) * P], h[k % 3][:, i * P:(i + 1) * P], ident)
                    last.then_inc(t_done, 1)
                if alive(n, 0):
                    if c == 0:
                        pe.wait_ge(z_ready, t + 1)
                    wait(pe, h_ready, n - 1 if c < 2 else n - 2)
                    cols = slice(c * NC, (c + 1) * NC)
                    nc.tensor.matmul(ps_a[c % 3][:, 0:NC], zs[:, :], eg[:, cols], start=True, stop=True)\
                        .then_inc(a_done, 1)
                    nc.tensor.matmul(ps_b[c % 3][:, 0:NC], zs[:, :], eu[:, cols], start=True, stop=True)\
                        .then_inc(b_done, 1)
                if alive(n, 3):
                    k = back(c, 3)
                    pe.wait_ge(hT_ready, n - 2)
                    if k == 0:
                        wait(pe, added, t)
                    for i in range(NBK):
                        last = nc.tensor.matmul(ps_y[:, 0:D], hT[k % 3][:, i * P:(i + 1) * P], ed[:, NBK * k + i, :],
                                                start=k == 0 and i == 0, stop=k == CH - 1 and i == NBK - 1)
                    last.then_inc(down_done, 1)

            rotate_chunks(pe, step, 3)

        @block.scalar
        def _(act):
            act_in = L[:, :, :].rearrange("p a b -> p (a b)")
            nc.scalar.activation(act_in, act_in, ACT.Sigmoid).then_inc(scores_ready, 1)

            def step(n, c, t):
                if alive(n, 0):
                    act.wait_ge(a_done, n + 1)
                    wait(act, h_ready, n - 1 if c < 2 else n - 2)
                    nc.scalar.activation(s[c % 3][:, :], ps_a[c % 3][:, 0:NC], ACT.Silu).then_inc(s_ready, 1)
                if alive(n, 2):
                    act.wait_ge(t_done, n - 1)
                    k = back(c, 2)
                    wait(act, down_done, n - 3 if k < 2 else n - 4)
                    nc.scalar.activation(hT[k % 3][:, :], ps_t[:, 0:NC], ACT.Copy).then_inc(hT_ready, 1)

            rotate_chunks(act, step, 3)

        @block.gpsimd
        def _(pool):
            pool.wait_ge(gates_ready, 1)

            def step(n, c, t):
                if not alive(n, 0):
                    return
                if c == 0:
                    wait(pool, b_done, n)
                    nc.gpsimd.tensor_copy(zs[:, :], zT[:, ds(t, P)]).then_inc(z_ready, 1)
                pool.wait_ge(h_ready, n + 1)
                h3 = h[c % 3][:, :].rearrange("p (e i) -> p e i", i=W)
                gate = G[:, bass.ds(t, 1), c * CE:(c + 1) * CE].rearrange("p a b -> p (a b)")
                nc.gpsimd.tensor_tensor(h3, h3, gate.unsqueeze(2).broadcast_to([P, CE, W]), ALU.mult)\
                    .then_inc(g_ready, 1)

            rotate_chunks(pool, step, 0)

        @block.vector
        def _(dve):
            flat = lambda a: a.rearrange("p a b -> p (a b)")
            dve.wait_ge(scores_ready, 1)
            nc.vector.tensor_tensor(L[:, :, :], L[:, :, :], bias.unsqueeze(1).broadcast_to([P, TILES, E]), ALU.add)
            nc.vector.memset(grp[:, :, GRP:12], SENTINEL)
            nc.vector.memset(cand[:, :, E:ALL], SENTINEL)
            dve.drain()
            nc.vector.tensor_reduce(grp[:, :, 0:GRP], L[:, :, :].rearrange("p t (g e) -> p t g e", e=GRP), X, ALU.max)
            dve.drain()
            for t in range(TILES):
                nc.vector.max(top[:, t, :], grp[:, t, :])
            dve.drain()
            for t in range(TILES):
                nc.vector.match_replace(grp_rest[:, t, :], top[:, t, :], grp[:, t, :], -SENTINEL)
            dve.drain()
            nc.vector.tensor_tensor(grp[:, :, 0:GRP], grp[:, :, 0:GRP], grp_rest[:, :, 0:GRP], ALU.not_equal)
            dve.drain()
            for t in range(TILES):
                nc.vector.tensor_tensor(cand[:, t, 0:E].rearrange("p (g e) -> p g e", e=GRP),
                                        L[:, t, :].rearrange("p (g e) -> p g e", e=GRP),
                                        grp[:, t, 0:GRP].unsqueeze(2).broadcast_to([P, GRP, GRP]), ALU.mult)
            dve.drain()
            for t in range(TILES):
                nc.vector.max(top[:, t, :], cand[:, t, :])
            dve.drain()
            for t in range(TILES):
                nc.vector.match_replace(rest[:, t, :], top[:, t, :], cand[:, t, :], -SENTINEL)
            nc.vector.reduce_sum(den[:, :], top[:, :, 2:8], X)
            dve.drain()
            nc.vector.tensor_tensor(rest[:, :, 0:E], rest[:, :, 0:E], cand[:, :, 0:E], ALU.not_equal)
            nc.vector.tensor_scalar(den[:, :], den[:, :], 1.0e-8, None, ALU.add)
            dve.drain()
            nc.vector.tensor_tensor(rest[:, :, 0:E], rest[:, :, 0:E], cand[:, :, 0:E], ALU.mult)
            nc.vector.reciprocal(den[:, :], den[:, :])
            dve.drain()
            nc.vector.tensor_tensor(G[:, :, 0:E], rest[:, :, 0:E],
                                    den[:, :].unsqueeze(2).broadcast_to([P, TILES, E]), ALU.mult)
            nc.vector.memset(G[:, :, E:ALL], 1.0).then_inc(gates_ready, 1)

            def step(n, c, t):
                if alive(n, 0):
                    dve.wait_ge(s_ready, n + 1)
                    dve.wait_ge(b_done, n + 1)
                    wait(dve, t_done, n - 1 if c < 2 else n - 2)
                    nc.vector.tensor_tensor(h[c % 3][:, :], s[c % 3][:, :], ps_b[c % 3][:, 0:NC], ALU.mult)\
                        .then_inc(h_ready, 1)
                if alive(n, 3) and back(c, 3) == CH - 1:
                    dve.wait_ge(down_done, n - 2)
                    row = x[:, bass.ds(t - 1, 1), :].rearrange("p a b -> p (a b)")
                    nc.vector.tensor_tensor(row, row, ps_y[:, 0:D], ALU.add).then_inc(added, 1)

            rotate_chunks(dve, step, 3)



def arrive(nc, sem, value):
    with nc.Block() as block:
        @block.sync
        def _(sp):
            sp.wait_ge(sem, value)


def build(nc, A, out):
    with ExitStack() as top:
        m = Memory(nc, top)
        x = m.sb("x", [P, TILES, D])
        zT = m.sb("zT", [P, TILES * P])
        ident = m.sb("ident", [P, P])
        headmask = m.sb("headmask", [P, HEADS])
        rank = m.sb("rank", [P, 8])
        ones = m.sb("ones", [1, P])
        eps = m.sb("eps", [P, 2])
        logits = {E: m.sb(f"logits{E}", [P, TILES, E]) for E in (4, 8, 64)}
        ctxT = m.sb("ctxT", [P, B * KEYS])
        ctx2T = m.sb("ctx2T", [P, B, 2, KEYS])
        ctx_nat = m.sb("ctx_nat", [KEYS, B, D])
        small2 = {n: m.sb("L2" + n, sh) for n, sh in (
            ("wq", [P, D]), ("wk", [P, D]), ("wv", [P, D]), ("wo", [P, D]), ("bq", [P, 1]), ("bk", [P, 1]),
            ("bv", [P, D]), ("bo", [P, D]))}
        two_way = {n: m.sb("L3" + n, sh) for n, sh in (
            ("w_cq", [P, 1]), ("w_c", [P, 1]), ("w_q", [P, 1]), ("b_cq", [P, 1]), ("b_c", [P, 1]), ("b_q", [P, 1]),
            ("wl", [P, 4, D]), ("b_l", [P, D]))}
        gate2 = m.sb("gate2", [P, 8])
        gate3 = m.sb("gate3", [P, 64])
        bias3 = m.sb("bias3", [P, 64])
        x_loaded, consts_loaded, early_loaded, late_loaded = (m.sem(n) for n in (
            "x_loaded", "consts_loaded", "early_loaded", "late_loaded"))
        stored = m.sem("stored")
        eps_ln, eps_rms = eps[:, 0:1], eps[:, 1:2]

        early = ExitStack()
        me = Memory(nc, early)
        self_w = {n: me.sb("L0f" + n, sh) for n, sh in (
            ("wqkv", [P, 3 * D]), ("wo", [P, D]), ("qn", [P, 1]), ("kn", [P, 1]), ("n1", [P, 1]), ("n2", [P, 1]),
            ("gate", [P, 4]), ("e0_up", [P, 1, 256]), ("e0_down", [P, 2, D]), ("e1_w1", [P, 1, 256]),
            ("e1_w2", [P, 1, 256]), ("e1_down", [P, 2, D]), ("e2_l1", [P, 1, 256]), ("e2_l2", [P, 2, 256]),
            ("e2_l3", [P, 2, 256]), ("e2_l4", [P, 2, D]), ("e3_down", [P, 1, D]), ("e3_up", [P, 1, 256]),
            ("e3_out", [P, 2, D]))}
        small0 = {n: me.sb("L0" + n, sh) for n, sh in (
            ("wq", [P, D]), ("wk", [P, D]), ("wv", [P, D]), ("wo", [P, D]), ("bq", [P, 1]), ("bk", [P, 1]),
            ("bv", [P, D]), ("bo", [P, D]))}
        wide1 = {n: me.sb("L1" + n, sh) for n, sh in (
            ("wq", [P, 1024]), ("wk", [P, 1024]), ("wv", [P, 1024]), ("wo", [P, 8, D]), ("bq", [P, 8]), ("bk", [P, 8]),
            ("bv", [P, 8]), ("bo", [P, D]))}
        gate1 = me.sb("gate1", [P, 8])
        mask0 = me.sb("mask0", [P, TPB, KEYS])
        mask1 = me.sb("mask1", [P, TILES, KEYS], U8)
        neg1 = me.sb("neg1", [P, TILES, KEYS])
        causal = me.sb("causal", [P, P])
        causal_b = me.sb("causal_b", [P, P], BF16)
        ident_b = me.sb("ident_b", [P, P], BF16)

        with ExitStack() as stack:
            ms = Memory(nc, stack, "su_")
            ctx_rows = ms.sb("ctx_rows", [P, B * KEYS // P, D])
            ps_c = ms.ps("ps_c")
            turned, made = ms.sem("turned"), ms.sem("made")
            block = stack.enter_context(nc.Block())
            n_const = []

            @block.sync
            def _(sp):
                sp.dma_start(x[:, :, :], A["x"].rearrange("(t p) d -> p t d", p=P)).then_inc(x_loaded, 16)
                for dst, name in ((self_w, "L0f"), (wide1, "L1")):
                    for key, tile in dst.items():
                        sp.dma_start(tile[tuple(slice(None) for _ in tile.shape)], A[name + key])\
                            .then_inc(early_loaded, 16)
                sp.dma_start(gate1[:, :], A["gate1"]).then_inc(early_loaded, 16)
                for dst, name in ((small2, "L2"), (two_way, "L3")):
                    for key, tile in dst.items():
                        sp.dma_start(tile[tuple(slice(None) for _ in tile.shape)], A[name + key])\
                            .then_inc(late_loaded, 16)
                for tile, key in ((gate2, "gate2"), (gate3, "gate3"), (bias3, "bias3")):
                    sp.dma_start(tile[:, :], A[key]).then_inc(late_loaded, 16)

            @block.scalar
            def _(act):
                loads = [(ctx_rows[:, :, :], A["ctx"].rearrange("(t p) d -> p t d", p=P)),
                         (ctx_nat[:, :, :], A["ctx"].rearrange("(b k) d -> k b d", k=KEYS)),
                         (ident[:, :], A["ident"]), (headmask[:, :], A["headmask"]), (rank[:, :], A["rank"]),
                         (causal[:, :], A["causal"]), (mask0[:, :, :], A["mask0"].rearrange("(t p) k -> p t k", p=P)),
                         (mask1[:, :, :], A["mask1"].rearrange("(t p) k -> p t k", p=P))]
                loads += [(t[tuple(slice(None) for _ in t.shape)], A["L0" + k]) for k, t in small0.items()]
                for dst, src in loads:
                    act.dma_start(dst, src).then_inc(consts_loaded, 16)
                n_const.append(16 * len(loads))

            @block.tensor
            def _(pe):
                pe.wait_ge(consts_loaded, n_const[0])
                for i in range(B * KEYS // P):
                    last = nc.tensor.transpose(ps_c[:, i * P:(i + 1) * P], ctx_rows[:, i, :], ident[:, :])
                last.then_inc(turned, 1)

            @block.vector
            def _(dve):
                nc.vector.memset(eps[:, 0:1], 1.0e-5)
                nc.vector.memset(eps[:, 1:2], 1.1920929e-07)
                nc.vector.memset(ones[:, :], 1.0)
                dve.wait_ge(consts_loaded, n_const[0])
                nc.vector.tensor_copy(ident_b[:, :], ident[:, :])
                nc.vector.tensor_scalar(causal_b[:, :], causal[:, :], BIG, -BIG, ALU.mult, ALU.add)
                nc.vector.tensor_scalar(mask0[:, :, :], mask0[:, :, :], -1.0e9, None, ALU.mult)
                nc.vector.tensor_scalar(neg1[:, :, :], mask1[:, :, :], BIG, -BIG, ALU.mult, ALU.add)
                dve.wait_ge(turned, 1)
                nc.vector.tensor_copy(ctxT[:, :], ps_c[:, :])
                for i in range(2):
                    nc.vector.tensor_copy(ctx2T[:, :, i, :], ps_c[:, :].rearrange("p (b k) -> p b k", k=KEYS))

            @block.gpsimd
            def _(pool):
                pool.wait_ge(x_loaded, 16)

        n_early = 16 * (len(self_w) + len(wide1) + 1)
        n_late = 16 * (len(small2) + len(two_way) + 3)
        idn, hm = ident[:, :], headmask[:, :]

        def finish():
            with nc.Block() as block:
                @block.sync
                def _(sp):
                    sp.dma_start(out.rearrange("(t p) d -> p t d", p=P), x[:, :, :]).then_inc(stored, 16)
                    sp.wait_ge(stored, 16)

        normalise(nc, "n0_", x, idn, 1e-5, True, out_T=zT, eps_tile=eps_ln, after=(x[:, :, :], small0["bo"][:, :]))
        with ExitStack() as stack:
            ml = Memory(nc, stack, "a0_")
            qT_all, kT_all, v2_all = ml.sb("qT", [P, TILES * P]), ml.sb("kT", [P, B * KEYS]), ml.sb("v2", [P, B, D])
            project_small(nc, "p0_", small0, zT, ctx2T, idn, qT_all, kT_all, v2_all)
            attend_small(nc, "t0_", x, small0, qT_all, kT_all, v2_all, idn, hm, HD ** -0.5, neg=mask0)
        if True:
            arrive(nc, early_loaded, n_early)
            with ExitStack() as stack:
                ml = Memory(nc, stack, "f0_")
                x2 = ml.sb("x2", [P, TILES, D])
                normalise(nc, "n1_", x, idn, 1e-5, True, out_natural=x2, eps_tile=eps_ln)
                normalise(nc, "n2_", x2, idn, 1e-7, False, out_T=zT, eps_tile=eps_rms, channel_scale=self_w["n1"][:, 0:1])
                with ExitStack() as inner:
                    mi = Memory(nc, inner, "s0_")
                    qT_all, kT_all = mi.sb("qT", [P, TILES * P]), mi.sb("kT", [P, TILES * P])
                    v_all = mi.sb("v", [P, TILES, D])
                    project_self(nc, "q0_", self_w, zT, idn, qT_all, kT_all, v_all, eps_rms)
                    attend_self(nc, "u0_", x2, self_w, qT_all, kT_all, v_all, idn, hm, causal_b[:, :], ident_b[:, :])
                normalise(nc, "n3_", x2, idn, 1e-7, False, out_T=zT, eps_tile=eps_rms, channel_scale=self_w["n2"][:, 0:1],
                          gate_w=self_w["gate"], logits=logits[4])
                experts_mixed(nc, "e0_", x, x2, self_w, zT, logits[4], rank)
        clear_spent(nc)
        if True:
            normalise(nc, "n4_", x, idn, 1e-5, True, out_T=zT, eps_tile=eps_ln, after=(x[:, :, :], wide1["bo"][:, :]))
            with ExitStack() as stack:
                ml = Memory(nc, stack, "a1_")
                kT_all, vT_all = ml.sb("kT", [P, 8, B * KEYS]), ml.sb("vT", [P, 8, B * KEYS])
                project_wide(nc, "p1_", wide1, ctxT, kT_all, vT_all)
                attend_wide(nc, "t1_", x, wide1, zT, kT_all, vT_all, idn, neg1)
        if True:
            normalise(nc, "n5_", x, idn, 1e-5, True, out_T=zT, eps_tile=eps_ln, gate_w=gate1, logits=logits[8])
            experts_gated(nc, "e1_", x, zT, logits[8], rank, 8, 4, A["L1w1"], A["L1w3"], A["L1w2"])
        early.close()
        clear_spent(nc)
        eg, eu = m.sb("eg", [P, 66 * 64]), m.sb("eu", [P, 66 * 64])
        ed = m.sb("ed", [P, 33, D])
        if True:
            with nc.Block() as block:
                @block.sync
                def _(sp):
                    sp.wait_ge(late_loaded, n_late)
                    for dst, src in ((eg[:, 0:4096], "L3eg"), (eg[:, 4096:], "L3sg"), (eu[:, 0:4096], "L3eu"),
                                     (eu[:, 4096:], "L3su"),
                                     (ed[:, 0:32, :].rearrange("p a b -> p (a b)"), "L3ed"), (ed[:, 32, :], "L3sd")):
                        sp.dma_start(dst, A[src]).then_inc(late_loaded, 16)
            normalise(nc, "n6_", x, idn, 1e-5, True, out_T=zT, eps_tile=eps_ln, after=(x[:, :, :], small2["bo"][:, :]))
            with ExitStack() as stack:
                ml = Memory(nc, stack, "a2_")
                qT_all, kT_all, v2_all = ml.sb("qT", [P, TILES * P]), ml.sb("kT", [P, B * KEYS]), ml.sb("v2", [P, B, D])
                project_small(nc, "p2_", small2, zT, ctx2T, idn, qT_all, kT_all, v2_all)
                attend_small(nc, "t2_", x, small2, qT_all, kT_all, v2_all, idn, hm, HD ** -0.5)
        if True:
            normalise(nc, "n7_", x, idn, 1e-5, True, out_T=zT, eps_tile=eps_ln, gate_w=gate2, logits=logits[8])
            experts_gated(nc, "e2_", x, zT, logits[8], rank, 8, 2, A["L2w1"], A["L2w3"], A["L2w2"])
        clear_spent(nc)
        if True:
            normalise(nc, "n8_", x, idn, 1e-5, True, out_T=zT, eps_tile=eps_ln, after=(x[:, :, :], two_way["b_l"][:, :]))
            attend_two_way(nc, "t3_", x, two_way, zT, ctxT, ctx_nat, idn, ones[:, :])
        if True:
            arrive(nc, late_loaded, n_late + 6 * 16)
            normalise(nc, "n9_", x, idn, 1e-5, True, out_T=zT, eps_tile=eps_ln, gate_w=gate3, logits=logits[64])
            experts_many(nc, "e3_", x, zT, logits[64], bias3[:, :], eg, eu, ed, idn)
        finish()


def lay_out(i):
    import numpy as np

    c = lambda a: np.ascontiguousarray(a)
    rows = lambda v: c(np.broadcast_to(v.reshape(1, -1), (P, v.size)))
    col = lambda v: c(v.reshape(-1, 1))
    split = lambda a: c(a.reshape(-1, P, a.shape[-1]).transpose(1, 0, 2))
    f = {k: np.asarray(v) for k, v in i.items()}
    a = {"x": f["x"].reshape(-1, D), "ctx": f["ctx_1024"].reshape(-1, D),
         "mask0": f["mask_1x1xSxS2_fk1"].reshape(S, KEYS),
         "mask1": f["mask_BxSxS2_bk1"].reshape(B * S, KEYS),
         "ident": np.eye(P, dtype=np.float32),
         "headmask": np.repeat(np.eye(HEADS, dtype=np.float32), HD, axis=0),
         "rank": np.tile(np.arange(8, 0, -1, dtype=np.float32), (P, 1)),
         "causal": np.tril(np.ones((P, P), np.float32))}
    for n, b in (("q", "q"), ("k", "k")):
        a["L0w" + n], a["L0b" + b] = f["L0_xattn_w" + n], col(f["L0_xattn_b" + b])
        a["L2w" + n], a["L2b" + b] = c(f["L2_xattn_W" + n].T), col(f["L2_xattn_b" + b])
    for n in "vo":
        a["L0w" + n], a["L0b" + n] = f["L0_xattn_w" + n], rows(f["L0_xattn_b" + n])
        a["L2w" + n], a["L2b" + n] = c(f["L2_xattn_W" + n].T), rows(f["L2_xattn_b" + n])
    g = lambda n: f["L0_ffn_" + n]
    a["L0fwqkv"] = c(np.concatenate([g("wq").T, g("wk").T, g("wv").T], axis=1))
    a["L0fwo"] = c(g("wo").T)
    a["L0fqn"], a["L0fkn"] = col(np.tile(g("qn_w"), HEADS)), col(np.tile(g("kn_w"), HEADS))
    a["L0fn1"], a["L0fn2"] = col(g("n1_w")), col(g("n2_w"))
    a["L0fgate"] = c(g("gate_w").T)
    for n in ("e0_up", "e0_down", "e1_w1", "e1_w2", "e1_down", "e2_l1", "e2_l2", "e2_l3", "e2_l4", "e3_down",
              "e3_up", "e3_out"):
        a["L0f" + n] = split(g(n).T)
    for n in "qkv":
        a["L1w" + n] = c(f["L1_xattn_w" + n].transpose(1, 0, 2).reshape(D, 1024))
        a["L1b" + n] = c(f["L1_xattn_b" + n].reshape(8, P).T)
    a["L1wo"], a["L1bo"] = split(f["L1_xattn_wo"]), rows(f["L1_xattn_bo"])
    a["gate1"], a["gate2"] = f["L1_ffn_gate_w"], c(f["L2_ffn_Wg"].T)
    down = lambda w: c(w.reshape(8, -1, P, D).transpose(0, 2, 1, 3).reshape(8, P, -1))
    a["L1w1"], a["L1w3"], a["L1w2"] = f["L1_ffn_w1"], f["L1_ffn_w3"], down(f["L1_ffn_w2"])
    a["L2w1"], a["L2w3"] = c(f["L2_ffn_W1"].transpose(0, 2, 1)), c(f["L2_ffn_W2"].transpose(0, 2, 1))
    a["L2w2"] = down(f["L2_ffn_W3"].transpose(0, 2, 1))
    for n in ("w_cq", "w_c", "w_q"):
        a["L3" + n] = col(f["L3_xattn_" + n])
    for n in ("b_cq", "b_c", "b_q"):
        a["L3" + n] = c(np.broadcast_to(f["L3_xattn_" + n].reshape(1, 1), (P, 1)))
    a["L3wl"], a["L3b_l"] = split(f["L3_xattn_W_l"].T), rows(f["L3_xattn_b_l"])
    a["gate3"], a["bias3"] = c(f["L3_ffn_gate_w"].T), rows(f["L3_ffn_gate_bias"])
    for n in ("eg", "eu"):
        a["L3" + n] = c(f[f"L3_ffn_{n}_w"].transpose(2, 0, 1).reshape(D, -1))
    a["L3sg"], a["L3su"] = c(f["L3_ffn_sg_w"].T), c(f["L3_ffn_su_w"].T)
    a["L3ed"] = c(f["L3_ffn_ed_w"].transpose(0, 2, 1).reshape(32, P, D).transpose(1, 0, 2).reshape(P, -1))
    a["L3sd"] = c(f["L3_ffn_sd_w"].T)
    return a


def kernel(**inputs):
    import numpy as np
    import concourse.bacc as bacc
    from concourse.bass_utils import run_bass_kernel_spmd

    nc = bacc.Bacc("TRN2", target_bir_lowering=False, num_devices=1)
    arrays = {f"in_{n}": np.ascontiguousarray(a) for n, a in lay_out(inputs).items()}
    aps = {n[3:]: nc.dram_tensor(n, a.shape, mybir.dt.from_np(a.dtype), kind="ExternalInput").ap()
           for n, a in arrays.items()}
    out = nc.dram_tensor("out", (B * S, D), F32, kind="ExternalOutput").ap()
    build(nc, aps, out)
    r = run_bass_kernel_spmd(nc, [arrays], core_ids=[0])
    return r.results[0]["out"].reshape(B, S, D)
```

```python
from contextlib import ExitStack

import concourse.bass as bass
from concourse import mybir

F32 = mybir.dt.float32
BF16 = mybir.dt.bfloat16
U8 = mybir.dt.uint8
ALU = mybir.AluOpType
ACT = mybir.ActivationFunctionType
X = mybir.AxisListType.X

P = 128
B, S, D = 8, 256, 128
KEYS = 64
TILES = B * S // P
TPB = S // P
HEADS = 16
HD = D // HEADS
GROUP = 4
GROUPS = TILES // GROUP
BIG = 1.0e30
EPS_LN, EPS_RMS = 1.0e-5, 1.1920929e-07
KEEP = 32


def wait(eng, sem, value):
    if not isinstance(value, int) or value > 0:
        eng.wait_ge(sem, value)


def ds(i, n):
    return bass.ds(i * n, n)


class Memory:

    def __init__(self, nc, stack, tag=""):
        self.nc, self.stack, self.tag = nc, stack, tag

    def sb(self, name, shape, dt=F32):
        return self.stack.enter_context(self.nc.sbuf_tensor(self.tag + name, shape, dt))

    def ps(self, name, cols=512):
        return self.stack.enter_context(self.nc.psum_tensor(self.tag + name, [P, cols], F32))

    def sem(self, name):
        handle = self.stack.enter_context(self.nc.semaphore(self.tag + name))
        if self.tag:
            SPENT.append(handle.num)
        return handle


SPENT = []


def clear_spent(nc):
    with nc.Block() as block:
        @block.gpsimd
        def _(pool):
            nums = sorted(set(SPENT))
            while nums:
                n = 1
                while n < len(nums) and nums[n] == nums[0] + n:
                    n += 1
                pool.sem_clear(range(nums[0], nums[0] + n))
                nums = nums[n:]
    SPENT.clear()



def normalise(nc, tag, src, ident, root, out_T, center=True, second=None, out_natural=None, channel_scale=1.0,
              gate_w=None, logits=None, arrived=None, ident_loaded=None, then=None, loads=None):
    HALF = TILES // 2
    with ExitStack() as stack:
        m = Memory(nc, stack, tag)
        stats = m.sb("stats", [P, TILES, 6])
        sum2, dif, ssq, mean, dif2, var, std, rstd, std2, rstd2 = (m.sb(n, [P, TILES]) for n in (
            "sum2", "dif", "ssq", "mean", "dif2", "var", "std", "rstd", "std2", "rstd2"))
        scratch = m.sb("scratch", [P, 1])
        zn = [m.sb(f"zn{i}", [P, GROUP, D]) for i in range(2)]
        ps_t = [m.ps(f"ps_t{i}") for i in range(2)]
        E = gate_w.shape[1] if gate_w is not None else 0
        ps_g = m.ps("ps_g", max(512, TILES * E)) if gate_w is not None else None
        var_ready, std_ready, rstd2_ready = m.sem("var_ready"), m.sem("std_ready"), m.sem("rstd2_ready")
        normed, turned = m.sem("normed"), m.sem("turned")
        evacuated, logits_done = m.sem("evacuated"), m.sem("logits_done")
        block = stack.enter_context(nc.Block())

        if loads is not None:
            block.sync(loads)

        @block.vector
        def _(dve):
            for half in range(2):
                h = slice(half * HALF, (half + 1) * HALF)
                for t in range(half * HALF, (half + 1) * HALF):
                    if arrived is not None and t % GROUP == 0:
                        dve.wait_ge(arrived[t // GROUP], 16)
                    nc.vector.bn_stats(stats[:, t, :], src[:, t, :])
                dve.drain()
                nc.vector.tensor_tensor(sum2[:, h], stats[:, h, 1], stats[:, h, 4], ALU.add)
                nc.vector.tensor_tensor(dif[:, h], stats[:, h, 1], stats[:, h, 4], ALU.subtract)
                nc.vector.tensor_tensor(ssq[:, h], stats[:, h, 2], stats[:, h, 5], ALU.add)
                dve.drain()
                nc.vector.tensor_scalar(mean[:, h], sum2[:, h], 0.5, None, ALU.mult)
                nc.vector.scalar_tensor_tensor(out=dif2[:, h], in0=dif[:, h], scalar=0.25, in1=dif[:, h],
                                               op0=ALU.mult, op1=ALU.mult)
                dve.drain()
                last = nc.vector.scalar_tensor_tensor(out=var[:, h], in0=ssq[:, h], scalar=1.0 / D, in1=dif2[:, h],
                                                      op0=ALU.mult, op1=ALU.add)
                if not center:
                    dve.drain()
                    nc.vector.tensor_tensor(dif2[:, h], mean[:, h], mean[:, h], ALU.mult)
                    dve.drain()
                    last = nc.vector.tensor_tensor(var[:, h], var[:, h], dif2[:, h], ALU.add)
                last.then_inc(var_ready, 1)
            for g in range(GROUPS):
                if g % 2 == 0:
                    half = g // 2
                    h = slice(half * HALF, (half + 1) * HALF)
                    dve.wait_ge(std_ready, half + 1)
                    nc.vector.reciprocal(rstd[:, h], std[:, h])
                    if out_natural is not None:
                        nc.vector.reciprocal(rstd2[:, h], std2[:, h]).then_inc(rstd2_ready, 1)
                    dve.drain()
                if g >= 2:
                    dve.wait_ge(turned, g - 1)
                for j in range(GROUP):
                    t = g * GROUP + j
                    if center:
                        last = nc.vector.tensor_scalar(zn[g % 2][:, j, :], src[:, t, :], mean[:, t:t + 1],
                                                       rstd[:, t:t + 1], ALU.subtract, ALU.mult)
                    else:
                        last = nc.vector.tensor_scalar(zn[g % 2][:, j, :], src[:, t, :], rstd[:, t:t + 1], None,
                                                       ALU.mult)
                last.then_inc(normed, 1)
            if gate_w is not None:
                dve.wait_ge(logits_done, 1)
                nc.vector.tensor_copy(logits[:, :, :], ps_g[:, 0:TILES * E].rearrange("p (a b) -> p a b", b=E))

        @block.scalar
        def _(act):
            nc.scalar.activation(scratch[:, :], root[1], ACT.Sqrt)
            for half in range(2):
                h = slice(half * HALF, (half + 1) * HALF)
                act.wait_ge(var_ready, half + 1)
                last = nc.scalar.activation(std[:, h], var[:, h], ACT.Sqrt, scale=root[0], bias=root[1])
                if out_natural is not None:
                    last = nc.scalar.activation(std2[:, h], var[:, h], ACT.Sqrt, scale=second[0], bias=second[1])
                last.then_inc(std_ready, 1)
            for g in range(GROUPS):
                act.wait_ge(turned, g + 1)
                nc.scalar.activation(out_T[:, g * 512:(g + 1) * 512], ps_t[g % 2][:, :], ACT.Copy, scale=channel_scale)\
                    .then_inc(evacuated, 1)
            if then is not None:
                act.drain()
                nc.scalar.activation(scratch[:, :], root[1], then)

        @block.tensor
        def _(pe):
            def router(g):
                pe.wait_ge(evacuated, g + 1)
                for t in range(g * GROUP, (g + 1) * GROUP):
                    last = nc.tensor.matmul(ps_g[:, t * E:(t + 1) * E], out_T[:, t * P:(t + 1) * P],
                                            gate_w[:, :], start=True, stop=True)
                return last

            if ident_loaded is not None:
                pe.wait_ge(ident_loaded, 16)
            for g in range(GROUPS):
                pe.wait_ge(normed, g + 1)
                if g >= 2:
                    pe.wait_ge(evacuated, g - 1)
                for j in range(GROUP):
                    last = nc.tensor.transpose(ps_t[g % 2][:, j * P:(j + 1) * P], zn[g % 2][:, j, :], ident)
                last.then_inc(turned, 1)
                if gate_w is not None and g > 0:
                    router(g - 1)
            if gate_w is not None:
                router(GROUPS - 1).then_inc(logits_done, 1)

        if out_natural is not None:
            @block.gpsimd
            def _(pool):
                for t in range(TILES):
                    if t % HALF == 0:
                        pool.wait_ge(rstd2_ready, t // HALF + 1)
                    nc.gpsimd.tensor_scalar(out_natural[:, t, :], src[:, t, :], mean[:, t:t + 1],
                                            rstd2[:, t:t + 1], ALU.subtract, ALU.mult)


LAGS = 4


def rotate(eng, step, lags=LAGS):
    for t in range(4):
        step(t, t, t // TPB)
    with eng.Fori(1, TILES // 4) as i:
        for r in range(4):
            step(i * 4 + r, r, i * 2 + r // TPB)
    for t in range(TILES, TILES + lags):
        step(t, t % 4, t // TPB)


def live(t, lag):
    return not isinstance(t, int) or 0 <= t - lag < TILES



def project_small(nc, tag, w, zT, ctx2T, ident, qT_all, kT_all, v2_all):
    with ExitStack() as stack:
        m = Memory(nc, stack, tag)
        pq = [m.ps(f"pq{i}") for i in range(2)]
        pk = m.ps("pk")
        pv = m.ps("pv", 1024)
        q_done, q_out, k_done, v_done = m.sem("q_done"), m.sem("q_out"), m.sem("k_done"), m.sem("v_done")
        block = stack.enter_context(nc.Block())

        @block.tensor
        def _(pe):
            nc.tensor.matmul(pk[:, :].rearrange("p (b k) -> p b k", k=KEYS), w["wk"][:, :], ctx2T[:, :, 0, :],
                             start=True, stop=True).then_inc(k_done, 1)
            for b in range(B):
                last = nc.tensor.matmul(pv[:, b * D:(b + 1) * D],
                                        ctx2T[:, b, :, :].rearrange("p a k -> p (a k)"),
                                        w["wv"][:, :], start=True, stop=True)
            last.then_inc(v_done, 1)
            for g in range(GROUPS):
                if g >= 2:
                    pe.wait_ge(q_out, g - 1)
                nc.tensor.matmul(pq[g % 2][:, :], w["wq"][:, :], zT[:, g * 512:(g + 1) * 512],
                                 start=True, stop=True).then_inc(q_done, 1)

        @block.scalar
        def _(act):
            act.wait_ge(k_done, 1)
            nc.scalar.activation(kT_all[:, :], pk[:, :], ACT.Identity, bias=w["bk"][:, 0:1])
            for g in range(GROUPS):
                act.wait_ge(q_done, g + 1)
                nc.scalar.activation(qT_all[:, g * 512:(g + 1) * 512], pq[g % 2][:, :], ACT.Identity,
                                     bias=w["bq"][:, 0:1]).then_inc(q_out, 1)

        @block.vector
        def _(dve):
            dve.wait_ge(v_done, 1)
            nc.vector.tensor_tensor(v2_all[:, :, :], pv[:, :].rearrange("p (b d) -> p b d", d=D),
                                    w["bv"][:, :].unsqueeze(1).broadcast_to([P, B, D]), ALU.add)


def attend_small(nc, tag, x, w, qT_all, kT_all, v2_all, ident, headmask, scale, neg=None, loads=None):
    with ExitStack() as stack:
        m = Memory(nc, stack, tag)
        qs = [m.sb(f"qs{i}", [P, P]) for i in range(2)]
        kbd = [m.sb(f"kbd{i}", [P, HEADS, KEYS]) for i in range(2)]
        NA = D + HEADS
        vaug = [m.sb(f"vaug{i}", [P, 8 * (NA + 16)]) for i in range(2)]
        sm = [m.sb(f"sm{i}", [P, HEADS, KEYS]) for i in range(2)]
        mx = [m.sb(f"mx{i}", [P, HEADS]) for i in range(2)]
        pT = [m.sb(f"pT{i}", [P, 8, P]) for i in range(2)]
        rden = m.sb("rden", [P, HEADS])
        on = [m.sb(f"on{i}", [P, D]) for i in range(2)]
        onT = [m.sb(f"onT{i}", [P, P]) for i in range(2)]
        ps_s = [m.ps(f"ps_s{i}", 1024) for i in range(2)]
        ps_t = m.ps("ps_t", 1024)
        ps_o = m.ps("ps_o")
        ps_w = m.ps("ps_w")
        (bias_added, k_ready, v_ready, q_ready, s_done, s_used, sub_done, p_ready, t_done, pT_ready, o_done, on_ready,
         ot_done, onT_ready, w_done, x_done, zeroed) = (m.sem(n) for n in (
             "bias_added", "k_ready", "v_ready", "q_ready", "s_done", "s_used", "sub_done", "p_ready", "t_done", "pT_ready", "o_done",
             "on_ready", "ot_done", "onT_ready", "w_done", "x_done", "zeroed"))
        block = stack.enter_context(nc.Block())
        if loads is not None:
            block.sync(loads)

        @block.gpsimd
        def _(pool):
            def step(t, r, b):
                if not live(t, 0):
                    return
                if r % 2 == 0:
                    b2 = r // 2
                    wait(pool, s_done, t - 2)
                    nc.gpsimd.tensor_tensor(kbd[b2][:, :, :],
                                            kT_all[:, ds(b, KEYS)].unsqueeze(1).broadcast_to([P, HEADS, KEYS]),
                                            headmask.unsqueeze(2).broadcast_to([P, HEADS, KEYS]), ALU.mult)\
                        .then_inc(k_ready, 1)
                wait(pool, s_done, t - 1)
                nc.gpsimd.tensor_copy(qs[r % 2][:, :], qT_all[:, ds(t, P)]).then_inc(q_ready, 1)
                row = x[:, bass.ds(t, 1), :].rearrange("p a b -> p (a b)")
                nc.gpsimd.tensor_tensor(row, row, w["bo"][:, :], ALU.add).then_inc(bias_added, 1)

            rotate(pool, step, 0)

        @block.tensor
        def _(pe):
            def step(t, r, b):
                p = r % 2
                if live(t, 0):
                    pe.wait_ge(q_ready, t + 1)
                    if r % 2 == 0:
                        pe.wait_ge(k_ready, b + 1)
                    wait(pe, s_used if neg is not None else sub_done, t - 1)
                    for h in range(2):
                        last = nc.tensor.matmul(ps_s[p][:, h * 512:(h + 1) * 512], qs[p][:, :],
                                                kbd[r // 2][:, 8 * h:8 * h + 8, :].rearrange("p a b -> p (a b)"),
                                                start=True, stop=True)
                    last.then_inc(s_done, 1)
                if live(t, 1):
                    pe.wait_ge(p_ready, t)
                    wait(pe, pT_ready, t - 1)
                    for j in range(8):
                        last = nc.tensor.transpose(ps_t[:, j * P:(j + 1) * P],
                                                   sm[1 - p][:, 2 * j:2 * j + 2, :].rearrange("p a b -> p (a b)"), ident)
                    last.then_inc(t_done, 1)
                if live(t, 3):
                    pe.wait_ge(on_ready, t - 2)
                    wait(pe, x_done, t - 3)
                    nc.tensor.transpose(ps_w[:, P:2 * P], on[1 - p][:, :], ident).then_inc(ot_done, 1)
                if live(t, 2):
                    pe.wait_ge(pT_ready, t - 1)
                    vb = ((r - 2) % 4) // 2
                    if r % 2 == 0:
                        pe.wait_ge(v_ready, b)
                    for j in range(8):
                        last = nc.tensor.matmul(ps_o[:, 0:NA], pT[p][:, j, :],
                                                vaug[vb][:, j * NA:(j + 1) * NA], start=j == 0, stop=j == 7)
                    last.then_inc(o_done, 1)
                if live(t, 3):
                    pe.wait_ge(onT_ready, t - 2)
                    nc.tensor.matmul(ps_w[:, 0:P], onT[1 - p][:, :], w["wo"][:, :],
                                     start=True, stop=True).then_inc(w_done, 1)

            rotate(pe, step)

        @block.scalar
        def _(act):
            act.wait_ge(zeroed, 1)

            def step(t, r, b):
                p = r % 2
                if live(t, 0) and p == 0:
                    wait(act, o_done, t - 2)
                    for half in range(2):
                        rows = slice(64 * half, 64 * half + 64)
                        out = vaug[r // 2][rows, :].rearrange("p (j c) -> p j c", c=NA + 16)
                        src = v2_all[rows, bass.ds(b, 1), :].rearrange("p a (j e d) -> p (a j) e d", e=2, d=HD)
                        last = nc.scalar.activation(out[:, :, HD * half:HD * half + HD], src[:, :, half, :], ACT.Copy)
                    last.then_inc(v_ready, 1)
                if live(t, 1):
                    act.wait_ge(t_done, t)
                    wait(act, o_done, t - 2)
                    nc.scalar.activation(pT[1 - p][:, :, :].rearrange("p a b -> p (a b)"), ps_t[:, :], ACT.Copy)\
                        .then_inc(pT_ready, 1)
                if live(t, 3):
                    act.wait_ge(ot_done, t - 2)
                    wait(act, w_done, t - 4)
                    nc.scalar.activation(onT[1 - p][:, :], ps_w[:, P:2 * P], ACT.Copy).then_inc(onT_ready, 1)
                if live(t, 0):
                    act.wait_ge(sub_done, t + 1)
                    flat = sm[p][:, :, :].rearrange("p a b -> p (a b)")
                    nc.scalar.activation(flat, flat, ACT.Exp, scale=1.0 if neg is not None else scale)\
                        .then_inc(p_ready, 1)

            rotate(act, step)

        @block.vector
        def _(dve):
            for i in range(2):
                nc.vector.memset(vaug[i][:, :], 0.0)
            dve.drain()
            for i in range(2):
                for half in range(2):
                    rows = slice(64 * half, 64 * half + 64)
                    for j in range(8):
                        c = j * NA + D + 2 * j + half
                        last = nc.vector.memset(vaug[i][rows, c:c + 1], 1.0)
            last.then_inc(zeroed, 1)

            def step(t, r, b):
                p = r % 2
                if live(t, 4):
                    dve.wait_ge(w_done, t - 3)
                    dve.wait_ge(bias_added, t - 3)
                    row = x[:, bass.ds(t - 4, 1), :].rearrange("p a b -> p (a b)")
                    nc.vector.tensor_tensor(row, row, ps_w[:, 0:P], ALU.add).then_inc(x_done, 1)
                if live(t, 0):
                    dve.wait_ge(s_done, t + 1)
                    wait(dve, t_done, t - 1)
                    s3 = ps_s[p][:, :].rearrange("p (h k) -> p h k", k=KEYS)
                    if neg is not None:
                        tile = neg[:, bass.ds(t, 1), :] if neg.shape[1] == TILES else neg[:, r % 2:r % 2 + 1, :]
                        nc.vector.scalar_tensor_tensor(out=sm[p][:, :, :], in0=s3, scalar=scale,
                                                       in1=tile.broadcast_to([P, HEADS, KEYS]),
                                                       op0=ALU.mult, op1=ALU.add).then_inc(s_used, 1)
                        s3 = sm[p][:, :, :]
                        dve.drain()
                    nc.vector.tensor_reduce(mx[p][:, :], s3, X, ALU.max)
                    dve.drain()
                    last = nc.vector.tensor_tensor(sm[p][:, :, :], s3,
                                                   mx[p][:, :].unsqueeze(2).broadcast_to([P, HEADS, KEYS]), ALU.subtract)
                    last.then_inc(sub_done, 1)
                if live(t, 2):
                    dve.wait_ge(o_done, t - 1)
                    wait(dve, ot_done, t - 3)
                    nc.vector.reciprocal(rden[:, :], ps_o[:, D:NA])
                    dve.drain()
                    nc.vector.tensor_tensor(on[p][:, :].rearrange("p (h d) -> p h d", d=HD),
                                            ps_o[:, 0:D].rearrange("p (h d) -> p h d", d=HD),
                                            rden[:, :].unsqueeze(2).broadcast_to([P, HEADS, HD]), ALU.mult)\
                        .then_inc(on_ready, 1)

            rotate(dve, step)



def project_wide(nc, tag, w, ctxT, kT_all, vT_all):
    with ExitStack() as stack:
        m = Memory(nc, stack, tag)
        pb = [m.ps(f"pb{i}") for i in range(4)]
        done, out = m.sem("done"), m.sem("out")
        block = stack.enter_context(nc.Block())

        @block.tensor
        def _(pe):
            n = 0
            for name in ("wk", "wv"):
                for j in range(8):
                    if n >= 4:
                        pe.wait_ge(out, n - 3)
                    nc.tensor.matmul(pb[n % 4][:, :], w[name][:, j * P:(j + 1) * P], ctxT[:, :],
                                     start=True, stop=True).then_inc(done, 1)
                    n += 1

        @block.scalar
        def _(act):
            n = 0
            for bias, dst in (("bk", kT_all), ("bv", vT_all)):
                for j in range(8):
                    act.wait_ge(done, n + 1)
                    nc.scalar.activation(dst[:, j, :], pb[n % 4][:, :], ACT.Identity,
                                         bias=w[bias][:, j:j + 1]).then_inc(out, 1)
                    n += 1


def attend_wide(nc, tag, x, w, zT, kT_all, vT_all, ident, neg, ident_b, loads=None):
    scale = 0.125
    with ExitStack() as stack:
        m = Memory(nc, stack, tag)
        qT = [m.sb(f"qT{i}", [P, 8, P]) for i in range(2)]
        kbd = [m.sb(f"kbd{i}", [P, 8, 2, KEYS]) for i in range(2)]
        vbd = m.sb("vbd", [P, 8, 2, KEYS])
        vw = [m.sb(f"vw{i}", [P, 8, D]) for i in range(2)]
        sm = [m.sb(f"sm{i}", [P, HEADS, KEYS]) for i in range(4)]
        mx = [m.sb(f"mx{i}", [P, HEADS]) for i in range(2)]
        den = [m.sb(f"den{i}", [P, HEADS]) for i in range(2)]
        pT = [m.sb(f"pT{i}", [P, 8, P]) for i in range(2)]
        ps_q = m.ps("ps_q", 1024)
        ps_s = m.ps("ps_s", 1024)
        ps_t = m.ps("ps_t", 1024)
        ps_v = m.ps("ps_v", 512)
        ps_o = m.ps("ps_o", 512)
        (bias_added, zeroed, k_ready, v_ready, vw_done, vw_ready, q_done, qT_ready, s_done, sub_done, exp_done,
         den_ready, p_ready, t_done, pT_ready, o_done, x_done) = (m.sem(n) for n in (
             "bias_added", "zeroed", "k_ready", "v_ready", "vw_done", "vw_ready", "q_done", "qT_ready", "s_done",
             "sub_done", "exp_done", "den_ready", "p_ready", "t_done", "pT_ready", "o_done", "x_done"))
        block = stack.enter_context(nc.Block())

        if loads is not None:
            block.sync(loads)

        @block.gpsimd
        def _(pool):
            nc.gpsimd.memset(vbd[:, :, :, :], 0.0)
            for i in range(2):
                last = nc.gpsimd.memset(kbd[i][:, :, :, :], 0.0)
            last.then_inc(zeroed, 1)

            def step(t, r, b):
                if live(t, 0):
                    row = x[:, bass.ds(t, 1), :].rearrange("p a b -> p (a b)")
                    nc.gpsimd.tensor_tensor(row, row, w["bo"][:, :], ALU.add).then_inc(bias_added, 1)
                if live(t, 2):
                    pool.wait_ge(den_ready, t - 1)
                    tile = sm[(r - 2) % 4][:, :, :]
                    nc.gpsimd.tensor_tensor(tile, tile, den[r % 2][:, :].unsqueeze(2)
                                            .broadcast_to([P, HEADS, KEYS]), ALU.mult).then_inc(p_ready, 1)

            rotate(pool, step)

        @block.tensor
        def _(pe):
            def step(t, r, b):
                p = r % 2
                if live(t, 0):
                    wait(pe, qT_ready, t)
                    for j in range(8):
                        last = nc.tensor.matmul(ps_q[:, j * P:(j + 1) * P], w["wq"][:, j * P:(j + 1) * P],
                                                zT[:, ds(t, P)], start=True, stop=True)
                    last.then_inc(q_done, 1)
                if live(t, 3):
                    pe.wait_ge(p_ready, t - 2)
                    wait(pe, pT_ready, t - 3)
                    tile = sm[(r - 3) % 4]
                    for j in range(8):
                        last = nc.tensor.transpose(ps_t[:, j * P:(j + 1) * P],
                                                   tile[:, 2 * j:2 * j + 2, :].rearrange("p a b -> p (a b)"), ident)
                    last.then_inc(t_done, 1)
                if live(t, 1):
                    pe.wait_ge(qT_ready, t)
                    if p == 1:
                        pe.wait_ge(k_ready, b + 1)
                    wait(pe, sub_done, t - 1)
                    for half in range(2):
                        nc.tensor.matmul(ps_s[:, half * 512:(half + 1) * 512].rearrange("p (h k) -> p h k", k=KEYS),
                                         ident_b, neg[:, bass.ds(t - 1, 1), :].broadcast_to([P, 8, KEYS]),
                                         start=True, stop=False, skip_group_check=True)
                        for j in range(4 * half, 4 * half + 4):
                            last = nc.tensor.matmul(ps_s[:, j * P:(j + 1) * P], qT[1 - p][:, j, :],
                                                    kbd[((r - 1) % 4) // 2][:, j, :, :].rearrange("p a b -> p (a b)"),
                                                    start=False, stop=j % 4 == 3, skip_group_check=True)
                    last.then_inc(s_done, 1)
                if live(t, 4):
                    pe.wait_ge(pT_ready, t - 3)
                    wait(pe, x_done, t - 4)
                    if p == 0:
                        pe.wait_ge(vw_ready, b * 2 - 2)
                    for j in range(8):
                        last = nc.tensor.matmul(ps_o[:, 0:D], pT[p][:, j, :], vw[r // 2][:, j, :],
                                                start=j == 0, stop=j == 7)
                    last.then_inc(o_done, 1)
                if live(t, 2):
                    pe.wait_ge(v_ready, b)
                    wait(pe, vw_ready, b * 2 - 2 + p)
                    for j in range(4 * p, 4 * p + 4):
                        last = nc.tensor.matmul(ps_v[:, (j % 4) * P:(j % 4 + 1) * P],
                                                vbd[:, j, :, :].rearrange("p a b -> p (a b)"), w["wo"][:, j, :],
                                                start=True, stop=True)
                    last.then_inc(vw_done, 1)

            rotate(pe, step)

        @block.scalar
        def _(act):
            act.wait_ge(zeroed, 1)

            def step(t, r, b):
                p = r % 2
                if live(t, 0) and p == 0:
                    wait(act, s_done, t - 2)
                    for half in range(2):
                        rows = slice(64 * half, 64 * half + 64)
                        last = nc.scalar.activation(kbd[r // 2][rows, :, half, :], kT_all[rows, :, ds(b, KEYS)], ACT.Copy)
                    last.then_inc(k_ready, 1)
                if live(t, 3):
                    act.wait_ge(t_done, t - 2)
                    wait(act, o_done, t - 4)
                    nc.scalar.activation(pT[1 - p][:, :, :].rearrange("p a b -> p (a b)"), ps_t[:, :], ACT.Copy)\
                        .then_inc(pT_ready, 1)
                if live(t, 2) and p == 0:
                    wait(act, vw_done, b * 2 - 2)
                    for half in range(2):
                        rows = slice(64 * half, 64 * half + 64)
                        last = nc.scalar.activation(vbd[rows, :, half, :], vT_all[rows, :, ds(b - 1, KEYS)], ACT.Copy)
                    last.then_inc(v_ready, 1)
                if live(t, 1):
                    act.wait_ge(sub_done, t)
                    flat = sm[(r - 1) % 4][:, :, :].rearrange("p a b -> p (a b)")
                    nc.scalar.activation(flat, flat, ACT.Exp, scale=scale).then_inc(exp_done, 1)
                if live(t, 2):
                    act.wait_ge(vw_done, b * 2 - 1 + p)
                    wait(act, o_done, t - 4 - p)
                    nc.scalar.activation(vw[((r - 2) % 4) // 2][:, 4 * p:4 * p + 4, :].rearrange("p a b -> p (a b)"),
                                         ps_v[:, :], ACT.Copy).then_inc(vw_ready, 1)

            rotate(act, step)

        @block.vector
        def _(dve):
            def step(t, r, b):
                p = r % 2
                if live(t, 0):
                    dve.wait_ge(q_done, t + 1)
                    wait(dve, s_done, t - 1)
                    nc.vector.tensor_tensor(qT[p][:, :, :], ps_q[:, :].rearrange("p (j q) -> p j q", q=P),
                                            w["bq"][:, :].unsqueeze(2).broadcast_to([P, 8, P]), ALU.add)\
                        .then_inc(qT_ready, 1)
                if live(t, 2):
                    dve.wait_ge(exp_done, t - 1)
                    wait(dve, p_ready, t - 3)
                    nc.vector.reduce_sum(den[p][:, :], sm[(r - 2) % 4][:, :, :], X)
                    dve.drain()
                    nc.vector.reciprocal(den[p][:, :], den[p][:, :]).then_inc(den_ready, 1)
                if live(t, 1):
                    dve.wait_ge(s_done, t)
                    wait(dve, t_done, t - 4)
                    s3 = ps_s[:, :].rearrange("p (h k) -> p h k", k=KEYS)
                    nc.vector.tensor_reduce(mx[1 - p][:, :], s3, X, ALU.max)
                    dve.drain()
                    nc.vector.tensor_tensor(sm[(r - 1) % 4][:, :, :], s3,
                                            mx[1 - p][:, :].unsqueeze(2).broadcast_to([P, HEADS, KEYS]), ALU.subtract)\
                        .then_inc(sub_done, 1)
                if live(t, 4):
                    dve.wait_ge(o_done, t - 3)
                    dve.wait_ge(bias_added, t - 3)
                    row = x[:, bass.ds(t - 4, 1), :].rearrange("p a b -> p (a b)")
                    nc.vector.tensor_tensor(row, row, ps_o[:, 0:D], ALU.add).then_inc(x_done, 1)

            rotate(dve, step)



def project_self(nc, tag, w, zT, ident, qT_all, kT_all, v_all, eps_tile):
    with ExitStack() as stack:
        m = Memory(nc, stack, tag)
        zs = [m.sb(f"zs{i}", [P, P]) for i in range(2)]
        qk = m.sb("qk", [P, TILES, 2 * D])
        sq = [m.sb(f"sq{i}", [P, 2 * D]) for i in range(2)]
        ms = m.sb("ms", [P, TILES, 2 * HEADS])
        ps_p = [m.ps(f"ps_p{i}") for i in range(2)]
        ps_t = [m.ps(f"ps_t{i}") for i in range(2)]
        (z_ready, p_done, sq_ready, ms_ready, root_ready, n_ready, t_done, t_used) = (m.sem(n) for n in (
            "z_ready", "p_done", "sq_ready", "ms_ready", "root_ready", "n_ready", "t_done", "t_used"))
        block = stack.enter_context(nc.Block())
        msf = ms[:, :, :].rearrange("p a b -> p (a b)")

        @block.gpsimd
        def _(pool):
            with pool.Fori(0, TILES // 2) as i:
                for r in range(2):
                    t = i * 2 + r
                    pool.wait_ge(p_done, i * 2)
                    nc.gpsimd.tensor_copy(zs[r][:, :], zT[:, ds(t, P)]).then_inc(z_ready, 1)

        @block.tensor
        def _(pe):
            with pe.Fori(0, TILES // 2) as i:
                for r in range(2):
                    t = i * 2 + r
                    pe.wait_ge(z_ready, t + 1)
                    pe.wait_ge(ms_ready, i * 2)
                    nc.tensor.matmul(ps_p[r][:, 0:3 * D], zs[r][:, :], w["wqkv"][:, :],
                                     start=True, stop=True).then_inc(p_done, 1)
            for t in range(TILES):
                pe.wait_ge(n_ready, t + 1)
                if t >= 2:
                    pe.wait_ge(t_used, t - 1)
                for half in range(2):
                    last = nc.tensor.transpose(ps_t[t % 2][:, half * P:(half + 1) * P],
                                               qk[:, t, half * D:(half + 1) * D], ident)
                last.then_inc(t_done, 1)

        @block.scalar
        def _(act):
            with act.Fori(0, TILES // 2) as i:
                for r in range(2):
                    t = i * 2 + r
                    act.wait_ge(p_done, t + 1)
                    act.wait_ge(ms_ready, i * 2)
                    nc.scalar.activation(sq[r][:, :], ps_p[r][:, 0:2 * D], ACT.Square).then_inc(sq_ready, 1)
            act.wait_ge(ms_ready, TILES)
            nc.scalar.activation(msf, msf, ACT.Sqrt, bias=eps_tile, scale=1.0 / HD).then_inc(root_ready, 1)

        @block.vector
        def _(dve):
            with dve.Fori(0, TILES // 2) as i:
                for r in range(2):
                    t = i * 2 + r
                    dve.wait_ge(sq_ready, t + 1)
                    nc.vector.tensor_copy(qk[:, bass.ds(t, 1), :].rearrange("p a b -> p (a b)"), ps_p[r][:, 0:2 * D])
                    nc.vector.tensor_copy(v_all[:, bass.ds(t, 1), :].rearrange("p a b -> p (a b)"), ps_p[r][:, 2 * D:3 * D])
                    nc.vector.reduce_sum(ms[:, bass.ds(t, 1), :].rearrange("p a b -> p (a b)"),
                                         sq[r][:, :].rearrange("p (h d) -> p h d", d=HD), X).then_inc(ms_ready, 1)
            dve.wait_ge(root_ready, 1)
            nc.vector.reciprocal(msf, msf)
            dve.drain()
            with dve.Fori(0, TILES) as t:
                tile = qk[:, bass.ds(t, 1), :].rearrange("p a (h d) -> p (a h) d", d=HD)
                scale = ms[:, bass.ds(t, 1), :].rearrange("p a h -> p (a h)").unsqueeze(2).broadcast_to([P, 2 * HEADS, HD])
                nc.vector.tensor_tensor(tile, tile, scale, ALU.mult).then_inc(n_ready, 1)
            for t in range(TILES):
                dve.wait_ge(t_done, t + 1)
                nc.vector.tensor_scalar(qT_all[:, t * P:(t + 1) * P], ps_t[t % 2][:, 0:P], w["qn"][:, 0:1], None, ALU.mult)
                nc.vector.tensor_scalar(kT_all[:, t * P:(t + 1) * P], ps_t[t % 2][:, P:2 * P], w["kn"][:, 0:1], None,
                                        ALU.mult).then_inc(t_used, 1)


def attend_self(nc, tag, x2, w, qT_all, kT_all, v_all, ident, headmask, causal, ident_b):
    scale = float(HD) ** -0.5
    NA = D + HEADS
    CH = 12
    with ExitStack() as stack:
        m = Memory(nc, stack, tag)
        qs = [m.sb(f"qs{i}", [P, P]) for i in range(2)]
        keys = m.sb("keys", [P, S])
        kbd = m.sb("kbd", [P, HEADS, S])
        vaug = [m.sb(f"vaug{i}", [P, HEADS * (NA + HD)]) for i in range(2)]
        sm = [m.sb(f"sm{i}", [P, 512]) for i in range(3)]
        mx = [m.sb(f"mx{i}", [P, 4]) for i in range(2)]
        pT = [m.sb(f"pT{i}", [P, 4, P]) for i in range(2)]
        rden = m.sb("rden", [P, HEADS])
        on = m.sb("on", [P, D])
        onT = m.sb("onT", [P, P])
        ps_s = [m.ps(f"ps_s{i}") for i in range(2)]
        ps_t = [m.ps(f"ps_t{i}") for i in range(2)]
        ps_o = [m.ps(f"ps_o{i}") for i in range(2)]
        ps_w = m.ps("ps_w")
        (zeroed, q_ready, k_ready, v_ready, s_done, sub_done, p_ready, t_done, pT_ready, pv_done, on_ready,
         ot_done, onT_ready, w_done, x_done) = (m.sem(n) for n in (
             "zeroed", "q_ready", "k_ready", "v_ready", "s_done", "sub_done", "p_ready", "t_done", "pT_ready",
             "pv_done", "on_ready", "ot_done", "onT_ready", "w_done", "x_done"))
        block = stack.enter_context(nc.Block())

        def rotate_chunks(eng, step, lags):
            for r in range(CH):
                step(r, r, 0)
            with eng.Fori(1, B) as b:
                for r in range(CH):
                    step(b * CH + r, r, b)
            for r in range(lags):
                step(B * CH + r, r, B)

        def alive(n, lag):
            return not isinstance(n, int) or 0 <= n - lag < B * CH

        def blocks(r):
            if r < 4:
                return [(4 * r + i, 0, 128 * i) for i in range(4)]
            return [(2 * (r - 4) + i // 2, i % 2, 128 * i) for i in range(4)]

        NORMALISE = {7: 0, 15: 1}
        TURN = {8: 0, 16: 1}
        PROJECT = {10: 0, 18: 1}
        ADD = {11: 0, 19: 1}

        def finishing(table, r, b):
            for at, par in table.items():
                if at == r and not (isinstance(b, int) and b >= B):
                    return par, b * 2 + par
                if at == r + CH and not (isinstance(b, int) and b == 0):
                    return par, (b - 1) * 2 + par
            return None

        @block.gpsimd
        def _(pool):
            def fill(b):
                def q_copy(par):
                    nc.gpsimd.tensor_copy(qs[par][:, :], qT_all[:, ds(b * 2 + par, P)]).then_inc(q_ready, 1)
                wait(pool, s_done, b * CH - CH + 4)
                q_copy(0)
                nc.gpsimd.tensor_copy(keys[:, :], kT_all[:, ds(b, S)])
                pool.drain()
                for g in range(4):
                    wait(pool, s_done, b * CH - CH + 6 + 2 * g)
                    hs = slice(4 * g, 4 * g + 4)
                    nc.gpsimd.tensor_tensor(kbd[:, hs, :],
                                            keys[:, :].unsqueeze(1).broadcast_to([P, 4, S]),
                                            headmask[:, hs].unsqueeze(2).broadcast_to([P, 4, S]),
                                            ALU.mult).then_inc(k_ready, 1)
                q_copy(1)
                wait(pool, pv_done, b * CH)
                for kb in range(2):
                    out = vaug[kb][:, :].rearrange("p (h c) -> p h c", c=NA + HD)[:, :, 0:HD]
                    src = v_all[:, bass.ds(b * 2 + kb, 1), :].rearrange("p a (h d) -> p (a h) d", d=HD)
                    nc.gpsimd.tensor_copy(out, src).then_inc(v_ready, 1)

            pool.wait_ge(zeroed, 1)
            fill(0)
            with pool.Fori(1, B) as b:
                fill(b)

        @block.tensor
        def _(pe):
            def step(n, r, b):
                if alive(n, 0):
                    if r in (0, 4):
                        pe.wait_ge(q_ready, b * 2 + 1 + r // 4)
                    if r < 4:
                        pe.wait_ge(k_ready, b * 4 + r + 1)
                    wait(pe, sub_done, n - 1)
                    out = ps_s[r % 2]
                    if r < 4:
                        keys = kbd[:, 4 * r:4 * r + 4, 0:P]
                        out3 = out[:, :].rearrange("p (h k) -> p h k", k=P)
                        diag, heads = out3, 4
                    else:
                        keys = kbd[:, 2 * (r - 4):2 * (r - 4) + 2, :]
                        out3 = out[:, :].rearrange("p (h k) -> p h k", k=S)
                        diag, heads = out3[:, :, P:S], 2
                    nc.tensor.matmul(out3, qs[r // 4 if r < 4 else 1][:, :], keys, start=True, stop=False)
                    nc.tensor.matmul(diag, ident_b, causal.unsqueeze(1).broadcast_to([P, heads, P]),
                                     start=False, stop=True).then_inc(s_done, 1)
                if alive(n, 2):
                    pe.wait_ge(p_ready, n - 1)
                    wait(pe, pT_ready, n - 3)
                    for i in range(4):
                        last = nc.tensor.transpose(ps_t[r % 2][:, i * P:(i + 1) * P],
                                                   sm[(r + 1) % 3][:, i * P:(i + 1) * P], ident)
                    last.then_inc(t_done, 1)
                if alive(n, 3):
                    pe.wait_ge(pT_ready, n - 2)
                    c = (r - 3) % CH
                    par = 0 if c < 4 else 1
                    if c in (0, 4):
                        pe.wait_ge(v_ready, b * 2 + par + 1)
                        wait(pe, on_ready, b * 2 + par - 1)
                    for i, (h, kb, col) in enumerate(blocks(c)):
                        last = nc.tensor.matmul(ps_o[par][:, 0:NA], pT[(r - 3) % 2][:, i, :],
                                                vaug[kb][:, h * NA:(h + 1) * NA],
                                                start=c in (0, 4) and i == 0, stop=c in (3, 11) and i == 3)
                    last.then_inc(pv_done, 1)
                if found := finishing(TURN, r, b):
                    par, tile = found
                    pe.wait_ge(on_ready, tile + 1)
                    wait(pe, x_done, tile)
                    nc.tensor.transpose(ps_w[:, 0:P], on[:, :], ident).then_inc(ot_done, 1)
                if found := finishing(PROJECT, r, b):
                    par, tile = found
                    pe.wait_ge(onT_ready, tile + 1)
                    nc.tensor.matmul(ps_w[:, P:2 * P], onT[:, :], w["wo"][:, :], start=True, stop=True)\
                        .then_inc(w_done, 1)

            rotate_chunks(pe, step, 8)

        @block.scalar
        def _(act):
            def step(n, r, b):
                if alive(n, 2):
                    act.wait_ge(t_done, n - 1)
                    wait(act, pv_done, n - 3)
                    nc.scalar.activation(pT[r % 2][:, :, :].rearrange("p a b -> p (a b)"), ps_t[r % 2][:, :],
                                         ACT.Copy).then_inc(pT_ready, 1)
                if alive(n, 0):
                    act.wait_ge(sub_done, n + 1)
                    nc.scalar.activation(sm[r % 3][:, :], sm[r % 3][:, :], ACT.Exp, scale=scale).then_inc(p_ready, 1)
                if found := finishing(TURN, r, b):
                    par, tile = found
                    act.wait_ge(ot_done, tile + 1)
                    wait(act, w_done, tile)
                    nc.scalar.activation(onT[:, :], ps_w[:, 0:P], ACT.Copy).then_inc(onT_ready, 1)

            rotate_chunks(act, step, 8)

        @block.vector
        def _(dve):
            for kb in range(2):
                nc.vector.memset(vaug[kb][:, :], 0.0)
            dve.drain()
            for kb in range(2):
                ones = vaug[kb][:, 0:HEADS * (NA + 1)].rearrange("p (h c) -> p h c", c=NA + 1)[:, :, D:D + 1]
                last = nc.vector.memset(ones, 1.0)
            last.then_inc(zeroed, 1)

            def step(n, r, b):
                if alive(n, 0):
                    heads = 4 if r < 4 else 2
                    dve.wait_ge(s_done, n + 1)
                    wait(dve, t_done, n - 2)
                    s3 = ps_s[r % 2][:, :].rearrange("p (h k) -> p h k", h=heads)
                    nc.vector.tensor_reduce(mx[r % 2][:, 0:heads], s3, X, ALU.max)
                    dve.drain()
                    nc.vector.tensor_tensor(sm[r % 3][:, :].rearrange("p (h k) -> p h k", h=heads), s3,
                                            mx[r % 2][:, 0:heads].unsqueeze(2).broadcast_to([P, heads, 512 // heads]),
                                            ALU.subtract).then_inc(sub_done, 1)
                if found := finishing(NORMALISE, r, b):
                    par, tile = found
                    dve.wait_ge(pv_done, (b if r == 7 else b - 1) * CH + (4 if par == 0 else CH))
                    wait(dve, ot_done, tile)
                    nc.vector.reciprocal(rden[:, :], ps_o[par][:, D:NA])
                    dve.drain()
                    nc.vector.tensor_tensor(on[:, :].rearrange("p (h d) -> p h d", d=HD),
                                            ps_o[par][:, 0:D].rearrange("p (h d) -> p h d", d=HD),
                                            rden[:, :].unsqueeze(2).broadcast_to([P, HEADS, HD]), ALU.mult)\
                        .then_inc(on_ready, 1)
                if found := finishing(ADD, r, b):
                    par, tile = found
                    dve.wait_ge(w_done, tile + 1)
                    row = x2[:, bass.ds(tile, 1), KEEP:D].rearrange("p a b -> p (a b)")
                    nc.vector.tensor_tensor(row, row, ps_w[:, P + KEEP:2 * P], ALU.add).then_inc(x_done, 1)

            rotate_chunks(dve, step, 8)



def attend_two_way(nc, tag, x, w, zT, ctxT, ctx_nat, ident, ones):
    with ExitStack() as stack:
        m = Memory(nc, stack, tag)
        R = m.sb("R", [P, B * KEYS + KEYS])
        qrow = m.sb("qrow", [P, B * KEYS])
        wq_bc = m.sb("wq_bc", [P, P])
        const = m.sb("const", [P, 1])
        two = range(2)
        zs = [m.sb(f"zs{i}", [P, S]) for i in two]
        cn = [m.sb(f"cn{i}", [KEYS, D]) for i in two]
        a = [m.sb(f"a{i}", [P, TPB, KEYS]) for i in two]
        mx = [m.sb(f"mx{i}", [P, TPB]) for i in two]
        rs = [m.sb(f"rs{i}", [P, TPB]) for i in two]
        aT = [m.sb(f"aT{i}", [KEYS, S]) for i in two]
        row = [m.sb(f"row{i}", [1, S]) for i in two]
        one = [m.sb(f"one{i}", [1, 2]) for i in two]
        c2q = [m.sb(f"c2q{i}", [P, S]) for i in two]
        prod = [m.sb(f"prod{i}", [P, S]) for i in two]
        tmp = [m.sb(f"tmp{i}", [P, S]) for i in two]
        q2c = [m.sb(f"q2c{i}", [P, 1]) for i in two]
        w14 = [m.sb(f"w14{i}", [P, D]) for i in two]
        ps_s = [m.ps(f"ps_s{i}") for i in two]
        ps_a = [m.ps(f"ps_a{i}") for i in two]
        ps_c = [m.ps(f"ps_c{i}") for i in two]
        ps_q = m.ps("ps_q")
        (wq_ready, qrow_done, set_up, slots_ready, s_done, sub_done, exp_done, a_ready, a_turned, aT_ready,
         row_sub, row_exp, row_ready, c_done, c2q_ready, ready, o_done, x_done, bias_added) = (m.sem(n) for n in (
             "wq_ready", "qrow_done", "set_up", "slots_ready", "s_done", "sub_done", "exp_done", "a_ready",
             "a_turned", "aT_ready", "row_sub", "row_exp", "row_ready", "c_done", "c2q_ready", "ready",
             "o_done", "x_done", "bias_added"))
        block = stack.enter_context(nc.Block())

        @block.gpsimd
        def _(pool):
            def bias(i):
                for t in range(2 * TPB):
                    row = x[:, bass.ds(i * 2 * TPB + t, 1), :].rearrange("p a b -> p (a b)")
                    last = nc.gpsimd.tensor_tensor(row, row, w["b_l"][:, :], ALU.add)
                last.then_inc(bias_added, 1)

            with pool.Fori(0, B // 2) as i:
                pool.wait_ge(x_done, i * 2)
                for r in two:
                    nc.gpsimd.tensor_copy(zs[r][:, :], zT[:, ds(i * 2 + r, S)])
                    nc.gpsimd.tensor_copy(cn[r][:, :], ctx_nat[:, bass.ds(i * 2 + r, 1), :]
                                          .rearrange("p a b -> p (a b)")).then_inc(slots_ready, 1)
                bias(i)

        @block.tensor
        def _(pe):
            pe.wait_ge(wq_ready, 1)
            nc.tensor.matmul(ps_q[:, :], wq_bc[:, :], ctxT[:, :], start=True, stop=True).then_inc(qrow_done, 1)
            pe.wait_ge(set_up, 1)
            with pe.Fori(0, B // 2) as i:
                for r in two:
                    pe.wait_ge(slots_ready, i * 2 + r + 1)
                    for j in range(TPB):
                        last = nc.tensor.matmul(ps_s[r][:, j * P:(j + 1) * P], zs[r][:, j * P:(j + 1) * P],
                                                R[:, bass.ds((i * 2 + r) * KEYS, 2 * KEYS)], start=True, stop=True)
                    last.then_inc(s_done, 1)
                for r in two:
                    pe.wait_ge(a_ready, i * 2 + r + 1)
                    for j in range(TPB):
                        nc.tensor.transpose(ps_a[r][0:1, S + j * P:S + (j + 1) * P], mx[r][:, j:j + 1], ident)
                    for j in range(TPB):
                        last = nc.tensor.transpose(ps_a[r][0:KEYS, j * P:(j + 1) * P], a[r][:, j, :], ident)
                    last.then_inc(a_turned, 1)
                for r in two:
                    pe.wait_ge(aT_ready, i * 2 + r + 1)
                    nc.tensor.matmul(ps_c[r][:, 0:S], cn[r][:, :], aT[r][:, :], start=True, stop=True)
                    pe.wait_ge(row_ready, i * 2 + r + 1)
                    nc.tensor.matmul(ps_c[r][:, S:2 * S], ones, row[r][:, :], start=True, stop=True)\
                        .then_inc(c_done, 1)
                for r in two:
                    pe.wait_ge(ready, i * 2 + r + 1)
                    for j in range(TPB):
                        cols = slice(j * P, (j + 1) * P)
                        out = ps_s[r][:, S + j * P:S + (j + 1) * P]
                        nc.tensor.matmul(out, zs[r][:, cols], w14[r][:, :], start=True, stop=False)
                        nc.tensor.matmul(out, c2q[r][:, cols], w["wl"][:, 1, :], start=False, stop=False)
                        last = nc.tensor.matmul(out, prod[r][:, cols], w["wl"][:, 2, :], start=False, stop=True)
                    last.then_inc(o_done, 1)

        @block.scalar
        def _(act):
            with act.Fori(0, B // 2) as i:
                for r in two:
                    act.wait_ge(sub_done, i * 2 + r + 1)
                    flat = a[r][:, :, :].rearrange("p a b -> p (a b)")
                    nc.scalar.activation(flat, flat, ACT.Exp).then_inc(exp_done, 1)
                for r in two:
                    act.wait_ge(a_turned, i * 2 + r + 1)
                    nc.scalar.activation(aT[r][:, :], ps_a[r][0:KEYS, 0:S], ACT.Copy).then_inc(aT_ready, 1)
                    act.wait_ge(row_sub, i * 2 + r + 1)
                    nc.scalar.activation(row[r][:, :], row[r][:, :], ACT.Exp).then_inc(row_exp, 1)
                for r in two:
                    act.wait_ge(c_done, i * 2 + r + 1)
                    nc.scalar.activation(c2q[r][:, :], ps_c[r][:, 0:S], ACT.Copy).then_inc(c2q_ready, 1)

        @block.vector
        def _(dve):
            nc.vector.tensor_copy(wq_bc[:, :], w["w_q"][:, 0:1].broadcast_to([P, P]))
            nc.vector.tensor_tensor(const[:, :], w["b_q"][:, 0:1], w["b_c"][:, 0:1], ALU.add).then_inc(wq_ready, 1)
            nc.vector.tensor_scalar(R[:, 0:B * KEYS], ctxT[:, :], w["w_cq"][:, 0:1], w["w_c"][:, 0:1],
                                    ALU.mult, ALU.add)
            nc.vector.memset(R[:, B * KEYS:], 0.0)
            dve.drain()
            nc.vector.tensor_tensor(const[:, :], const[:, :], w["b_cq"][:, 0:1], ALU.add)
            dve.drain()
            dve.wait_ge(qrow_done, 1)
            nc.vector.tensor_scalar(qrow[:, :], ps_q[:, :], const[:, 0:1], None, ALU.add).then_inc(set_up, 1)
            dve.drain()
            with dve.Fori(0, B // 2) as i:
                for r in two:
                    dve.wait_ge(s_done, i * 2 + r + 1)
                    nc.vector.tensor_tensor(a[r][:, :, :],
                                            ps_s[r][:, 0:S].rearrange("p (j k) -> p j k", k=P)[:, :, 0:KEYS],
                                            qrow[:, ds(i * 2 + r, KEYS)].unsqueeze(1).broadcast_to([P, TPB, KEYS]),
                                            ALU.add)
                    dve.drain()
                    nc.vector.tensor_reduce(mx[r][:, :], a[r][:, :, :], X, ALU.max)
                    dve.drain()
                    nc.vector.tensor_tensor(a[r][:, :, :], a[r][:, :, :],
                                            mx[r][:, :].unsqueeze(2).broadcast_to([P, TPB, KEYS]), ALU.subtract)\
                        .then_inc(sub_done, 1)
                for r in two:
                    dve.wait_ge(exp_done, i * 2 + r + 1)
                    nc.vector.reduce_sum(rs[r][:, :], a[r][:, :, :], X)
                    dve.drain()
                    nc.vector.reciprocal(rs[r][:, :], rs[r][:, :])
                    dve.drain()
                    nc.vector.tensor_tensor(a[r][:, :, :], a[r][:, :, :],
                                            rs[r][:, :].unsqueeze(2).broadcast_to([P, TPB, KEYS]), ALU.mult)\
                        .then_inc(a_ready, 1)
                for r in two:
                    dve.wait_ge(aT_ready, i * 2 + r + 1)
                    nc.vector.tensor_reduce(one[r][:, 0:1], ps_a[r][0:1, S:2 * S], X, ALU.max)
                    dve.drain()
                    nc.vector.tensor_scalar(row[r][:, :], ps_a[r][0:1, S:2 * S], one[r][:, 0:1], None, ALU.subtract)\
                        .then_inc(row_sub, 1)
                for r in two:
                    dve.wait_ge(row_exp, i * 2 + r + 1)
                    nc.vector.reduce_sum(one[r][:, 1:2], row[r][:, :], X)
                    dve.drain()
                    nc.vector.reciprocal(one[r][:, 1:2], one[r][:, 1:2])
                    dve.drain()
                    nc.vector.tensor_scalar(row[r][:, :], row[r][:, :], one[r][:, 1:2], None, ALU.mult)\
                        .then_inc(row_ready, 1)
                for r in two:
                    dve.wait_ge(c2q_ready, i * 2 + r + 1)
                    nc.vector.tensor_tensor(tmp[r][:, :], zs[r][:, :], ps_c[r][:, S:2 * S], ALU.mult)
                    dve.drain()
                    nc.vector.reduce_sum(q2c[r][:, :], tmp[r][:, :], X)
                    dve.drain()
                    nc.vector.scalar_tensor_tensor(out=w14[r][:, :], in0=w["wl"][:, 3, :], scalar=q2c[r][:, 0:1],
                                                   in1=w["wl"][:, 0, :], op0=ALU.mult, op1=ALU.add)
                    nc.vector.tensor_tensor(prod[r][:, :], zs[r][:, :], c2q[r][:, :], ALU.mult).then_inc(ready, 1)
                dve.wait_ge(bias_added, i + 1)
                for r in two:
                    dve.wait_ge(o_done, i * 2 + r + 1)
                    xs = x[:, bass.ds((i * 2 + r) * TPB, TPB), :]
                    nc.vector.tensor_tensor(xs, xs, ps_s[r][:, S:2 * S].rearrange("p (j d) -> p j d", d=D), ALU.add)\
                        .then_inc(x_done, 1)



def top2_gates(nc, m, dve, act_sem, dve_sem, L, e, G, E, rank, eps):
    sh = [P, TILES, E]
    sel, pick = m.sb("g_sel", sh), m.sb("g_pick", sh)
    rest, key = m.sb("g_rest", sh), m.sb("g_key", sh)
    mx, s1, s2 = m.sb("g_mx", [P, TILES]), m.sb("g_s1", [P, TILES]), m.sb("g_s2", [P, TILES])
    wide = lambda t: t[:, :].unsqueeze(2).broadcast_to(sh)
    ranks = rank[:, 0:E].unsqueeze(1).broadcast_to(sh)

    def first_of_max(values, out):
        nc.vector.tensor_reduce(mx[:, :], values, X, ALU.max)
        dve.drain()
        nc.vector.tensor_tensor(key[:, :, :], values, wide(mx), ALU.is_equal)
        dve.drain()
        nc.vector.tensor_tensor(key[:, :, :], key[:, :, :], ranks, ALU.mult)
        dve.drain()
        nc.vector.tensor_reduce(s1[:, :], key[:, :, :], X, ALU.max)
        dve.drain()
        nc.vector.tensor_tensor(out, key[:, :, :], wide(s1), ALU.is_equal)

    nc.vector.tensor_reduce(mx[:, :], L[:, :, :], X, ALU.max)
    dve.drain()
    nc.vector.tensor_tensor(e[:, :, :], L[:, :, :], wide(mx), ALU.subtract).then_inc(dve_sem, 1)
    dve.drain()
    first_of_max(L[:, :, :], sel[:, :, :])
    dve.drain()
    nc.vector.scalar_tensor_tensor(out=rest[:, :, :], in0=sel[:, :, :], scalar=-3.0e38, in1=L[:, :, :],
                                   op0=ALU.mult, op1=ALU.add)
    dve.drain()
    first_of_max(rest[:, :, :], pick[:, :, :])
    dve.drain()
    nc.vector.tensor_tensor(sel[:, :, :], sel[:, :, :], pick[:, :, :], ALU.add)
    dve.wait_ge(act_sem, 1)
    dve.drain()
    nc.vector.tensor_tensor(sel[:, :, :], sel[:, :, :], e[:, :, :], ALU.mult)
    nc.vector.reduce_sum(s1[:, :], e[:, :, :], X)
    dve.drain()
    nc.vector.reduce_sum(s2[:, :], sel[:, :, :], X)
    dve.drain()
    nc.vector.scalar_tensor_tensor(out=s2[:, :], in0=s1[:, :], scalar=eps, in1=s2[:, :], op0=ALU.mult, op1=ALU.add)
    dve.drain()
    nc.vector.reciprocal(s2[:, :], s2[:, :])
    dve.drain()
    nc.vector.tensor_tensor(G[:, :, :], sel[:, :, :], wide(s2), ALU.mult)
    dve.drain()



def experts_gated(nc, tag, x, zT, L, rank, E, NF, w1, w3, w2):
    U = 2 * GROUPS * NF
    K = 2 * GROUPS
    with ExitStack() as stack:
        m = Memory(nc, stack, tag)
        W1 = [m.sb(f"W1_{i}", [P, NF * P]) for i in range(2)]
        W3 = [m.sb(f"W3_{i}", [P, NF * P]) for i in range(2)]
        W2 = [m.sb(f"W2_{i}", [P, NF, D]) for i in range(2)]
        s = [m.sb(f"s{i}", [P, 512]) for i in range(2)]
        h = [m.sb(f"h{i}", [P, NF, 512]) for i in range(2)]
        G = m.sb("G", [P, TILES, E])
        gate_exp = m.sb("gate_exp", [P, TILES, E])
        ps_a = [m.ps(f"ps_a{i}") for i in range(2)]
        ps_b = [m.ps(f"ps_b{i}") for i in range(2)]
        ps_y = [m.ps(f"ps_y{i}") for i in range(2)]
        w_loaded = [m.sem(f"w_loaded{i}") for i in range(2)]
        logits_shifted, gates_exp = m.sem("logits_shifted"), m.sem("gates_exp")
        up_done, s_ready, h_ready, down_done, added = (m.sem(n) for n in (
            "up_done", "s_ready", "h_ready", "down_done", "added"))
        block = stack.enter_context(nc.Block())

        @block.sync
        def _(sp):
            def load(p, e):
                for dst, src in ((W1[e][:, :], w1), (W3[e][:, :], w3),
                                 (W2[e][:, :, :].rearrange("p a b -> p (a b)"), w2)):
                    sp.dma_start(dst, src[bass.ds(p * 2 + e, 1)].rearrange("a p n -> p (a n)"))\
                        .then_inc(w_loaded[e], 16)

            for e in range(2):
                load(0, e)
            with sp.Fori(1, E // 2) as p:
                for e in range(2):
                    sp.wait_ge(down_done, p * K - K + (e + 1) * GROUPS)
                    load(p, e)

        @block.tensor
        def _(pe):
            with pe.Fori(0, E // 2) as p:
                def down(k, f):
                    if f == 0:
                        pe.wait_ge(added, p * K + (k - 1 if k >= 2 else 0))
                    pe.wait_ge(h_ready, p * U + k * NF + f + 1)
                    for j in range(GROUP):
                        last = nc.tensor.matmul(ps_y[k % 2][:, j * D:(j + 1) * D], h[k % 2][:, f, j * P:(j + 1) * P],
                                                W2[k // GROUPS][:, f, :], start=f == 0 and j == 0, stop=f == NF - 1,
                                                skip_group_check=True)
                    if f == NF - 1:
                        last.then_inc(down_done, 1)

                for k in range(K):
                    e, g = k // GROUPS, k % GROUPS
                    if g == 0:
                        pe.wait_ge(w_loaded[e], p * 48 + 48)
                    for f in range(NF):
                        u = k * NF + f
                        if u >= 2:
                            pe.wait_ge(h_ready, p * U + u - 1)
                        rhs = zT[:, g * 512:(g + 1) * 512]
                        nc.tensor.matmul(ps_a[u % 2][:, :], W1[e][:, f * P:(f + 1) * P], rhs,
                                         start=True, stop=True).then_inc(up_done, 1)
                        nc.tensor.matmul(ps_b[u % 2][:, :], W3[e][:, f * P:(f + 1) * P], rhs,
                                         start=True, stop=True).then_inc(up_done, 1)
                        if k > 0:
                            down(k - 1, f)
                for f in range(NF):
                    down(K - 1, f)

        @block.scalar
        def _(act):
            act.wait_ge(logits_shifted, 1)
            e_flat = gate_exp[:, :, :].rearrange("p a b -> p (a b)")
            nc.scalar.activation(e_flat, e_flat, ACT.Exp).then_inc(gates_exp, 1)
            with act.Fori(0, E // 2) as p:
                for u in range(U):
                    act.wait_ge(up_done, p * 2 * U + 2 * u + 1)
                    if u >= 2:
                        act.wait_ge(h_ready, p * U + u - 1)
                    nc.scalar.activation(s[u % 2][:, :], ps_a[u % 2][:, :], ACT.Silu).then_inc(s_ready, 1)

        @block.vector
        def _(dve):
            top2_gates(nc, m, dve, gates_exp, logits_shifted, L, gate_exp, G, E, rank, 0.0)
            with dve.Fori(0, E // 2) as p:
                def add(k):
                    dve.wait_ge(down_done, p * K + k + 1)
                    for j in range(GROUP):
                        t = (k % GROUPS) * GROUP + j
                        last = nc.vector.scalar_tensor_tensor(
                            out=x[:, t, :], in0=ps_y[k % 2][:, j * D:(j + 1) * D],
                            scalar=G[:, t, bass.ds(p * 2 + k // GROUPS, 1)], in1=x[:, t, :],
                            op0=ALU.mult, op1=ALU.add)
                    last.then_inc(added, 1)

                for k in range(K):
                    for f in range(NF):
                        u = k * NF + f
                        dve.wait_ge(s_ready, p * U + u + 1)
                        dve.wait_ge(up_done, p * 2 * U + 2 * u + 2)
                        if k >= 2 and f == 0:
                            dve.wait_ge(down_done, p * K + k - 1)
                        nc.vector.tensor_tensor(h[k % 2][:, f, :], s[u % 2][:, :], ps_b[u % 2][:, :], ALU.mult)\
                            .then_inc(h_ready, 1)
                    if k > 0:
                        add(k - 1)
                add(K - 1)



def experts_mixed(nc, tag, x, x2, w, zT, L, rank):
    HID = ("a0", "a1", "u0", "u1", "b0", "b1", "g0", "v0", "g1", "v1", "c0", "c1", "d0", "p0", "p1")
    ORDER = HID[:13] + ("y0", "p0", "p1", "y1", "y2", "y3")
    ACT_OPS = ("a0", "a1", "u0", "u1", "b0", "b1", "g0", "g1", "c0", "c1", "d0", "p0", "p1")
    NB = 5
    DOWN = {"y0": (("u0", "u1"), "e0_down", 0), "y1": (("m0", "m1"), "e1_down", 1),
            "y2": (("c0", "c1"), "e2_l4", 2), "y3": (("p0", "p1"), "e3_out", 3)}
    UP = {"a": ("e2_l1", None), "u": ("e0_up", None), "g": ("e1_w1", None), "v": ("e1_w2", None),
          "b": ("e2_l2", ("a0", "a1")), "c": ("e2_l3", ("b0", "b1")), "d": ("e3_down", None), "p": ("e3_up", ("d0",))}
    with ExitStack() as stack:
        m = Memory(nc, stack, tag)
        h = {n: m.sb("h_" + n, [P, 512]) for n in ACT_OPS + ("m0", "m1")}
        G = m.sb("G", [P, TILES, 4])
        gate_exp = m.sb("gate_exp", [P, TILES, 4])
        ps_h = [m.ps(f"ps_h{i}") for i in range(NB)]
        ps_y = [m.ps(f"ps_y{i}") for i in range(2)]
        logits_shifted, gates_exp = m.sem("logits_shifted"), m.sem("gates_exp")
        block_done, act_done, gated_done, down_done, added = (m.sem(n) for n in (
            "block_done", "act_done", "gated_done", "down_done", "added"))
        block = stack.enter_context(nc.Block())
        bank = {n: ps_h[i % NB] for i, n in enumerate(HID)}

        def wait_for(eng, names, g):
            gated = [int(n[1]) + 1 for n in names if n[0] == "m"]
            acts = [ACT_OPS.index(n) + 1 for n in names if n[0] != "m"]
            if gated:
                eng.wait_ge(gated_done, g * 2 + max(gated))
            if acts:
                eng.wait_ge(act_done, g * len(ACT_OPS) + max(acts))

        @block.tensor
        def _(pe):
            with pe.Fori(0, GROUPS) as g:
                for name in ORDER:
                    if name in DOWN:
                        inputs, wn, e = DOWN[name]
                        pe.wait_ge(added, g * 4 + max(0, e - 1))
                        wait_for(pe, inputs, g)
                        for j in range(GROUP):
                            for i, inp in enumerate(inputs):
                                last = nc.tensor.matmul(ps_y[e % 2][:, j * D:(j + 1) * D], h[inp][:, j * P:(j + 1) * P],
                                                        w[wn][:, i, :], start=i == 0, stop=i == 1)
                        last.then_inc(down_done, 1)
                        continue
                    n = HID.index(name)
                    wn, inputs = UP[name[0]]
                    needed = list(inputs or ())
                    if n >= NB:
                        old = HID[n - NB]
                        needed.append("m" + old[1] if old[0] in "gv" else old)
                    wait_for(pe, needed, g)
                    cols = slice(int(name[1]) * P, int(name[1]) * P + P)
                    if inputs is None:
                        last = nc.tensor.matmul(bank[name][:, :], w[wn][:, 0, cols], zT[:, ds(g, 512)],
                                                start=True, stop=True)
                    else:
                        for i, inp in enumerate(inputs):
                            last = nc.tensor.matmul(bank[name][:, :], w[wn][:, i, cols], h[inp][:, :],
                                                    start=i == 0, stop=i == len(inputs) - 1)
                    last.then_inc(block_done, 1)

        @block.scalar
        def _(act):
            act.wait_ge(logits_shifted, 1)
            e_flat = gate_exp[:, :, :].rearrange("p a b -> p (a b)")
            nc.scalar.activation(e_flat, e_flat, ACT.Exp).then_inc(gates_exp, 1)
            with act.Fori(0, GROUPS) as g:
                for name in ACT_OPS:
                    act.wait_ge(block_done, g * len(HID) + HID.index(name) + 1)
                    gate = name[0] == "g"
                    nc.scalar.activation(h[name][:, :], bank[name][:, :], ACT.Tanh if gate else ACT.Gelu,
                                         scale=0.5 if gate else 1.0).then_inc(act_done, 1)

        @block.vector
        def _(dve):
            top2_gates(nc, m, dve, gates_exp, logits_shifted, L, gate_exp, G, 4, rank, 1.0e-8)
            with dve.Fori(0, GROUPS) as g:
                for k in range(2):
                    wait_for(dve, (f"g{k}",), g)
                    tanh, out = h[f"g{k}"][:, :], h[f"m{k}"][:, :]
                    nc.vector.scalar_tensor_tensor(out=tanh, in0=tanh, scalar=1.0, in1=bank[f"g{k}"][:, :],
                                                   op0=ALU.add, op1=ALU.mult)
                    dve.drain()
                    dve.wait_ge(block_done, g * len(HID) + HID.index(f"v{k}") + 1)
                    nc.vector.scalar_tensor_tensor(out=out, in0=tanh, scalar=0.5, in1=bank[f"v{k}"][:, :],
                                                   op0=ALU.mult, op1=ALU.mult).then_inc(gated_done, 1)
                for e in range(4):
                    dve.wait_ge(down_done, g * 4 + e + 1)
                    for j in range(GROUP):
                        row = x2[:, bass.ds(g * GROUP + j, 1), KEEP:D].rearrange("p a b -> p (a b)")
                        last = nc.vector.scalar_tensor_tensor(
                            out=row, in0=ps_y[e % 2][:, j * D + KEEP:(j + 1) * D],
                            scalar=G[:, bass.ds(g * GROUP + j, 1), e], in1=row, op0=ALU.mult, op1=ALU.add)
                    last.then_inc(added, 1)
                    dve.drain()
            nc.vector.tensor_tensor(x[:, :, :], x[:, :, :], x2[:, :, :], ALU.add)



def experts_many(nc, tag, x, zT, L, bias, eg, eu, ed, ident):
    E, W, GRP = 64, 64, 8
    ALL = E + 2
    CE = 6
    CH = ALL // CE
    NC = CE * W
    NBK = NC // P
    SENTINEL = 3.0e38
    with ExitStack() as stack:
        m = Memory(nc, stack, tag)
        zs = m.sb("zs", [P, P])
        s = [m.sb(f"s{i}", [P, NC]) for i in range(3)]
        h = [m.sb(f"h{i}", [P, NC]) for i in range(3)]
        hT = [m.sb(f"hT{i}", [P, NC]) for i in range(3)]
        G = m.sb("G", [P, TILES, ALL])
        grp = m.sb("grp", [P, TILES, 12])
        grp_rest = m.sb("grp_rest", [P, TILES, 12])
        cand = m.sb("cand", [P, TILES, ALL])
        rest = m.sb("rest", [P, TILES, ALL])
        top = m.sb("top", [P, TILES, 8])
        den = m.sb("den", [P, TILES])
        ps_a = [m.ps(f"ps_a{i}") for i in range(3)]
        ps_b = [m.ps(f"ps_b{i}") for i in range(3)]
        ps_t = m.ps("ps_t")
        ps_y = m.ps("ps_y")
        (scores_ready, gates_ready, z_ready, a_done, b_done, s_ready, h_ready, g_ready, t_done, hT_ready,
         down_done, added) = (m.sem(n) for n in (
             "scores_ready", "gates_ready", "z_ready", "a_done", "b_done", "s_ready", "h_ready", "g_ready",
             "t_done", "hT_ready", "down_done", "added"))
        block = stack.enter_context(nc.Block())

        def rotate_chunks(eng, step, lags):
            for c in range(CH):
                step(c, c, 0)
            with eng.Fori(1, TILES) as t:
                for c in range(CH):
                    step(t * CH + c, c, t)
            for c in range(lags):
                step(TILES * CH + c, c, TILES)

        def alive(n, lag):
            return not isinstance(n, int) or 0 <= n - lag < TILES * CH

        def back(c, lag):
            return (c - lag) % CH

        @block.tensor
        def _(pe):
            def step(n, c, t):
                if alive(n, 2):
                    k = back(c, 2)
                    pe.wait_ge(g_ready, n - 1)
                    wait(pe, hT_ready, n - 2)
                    for i in range(NBK):
                        last = nc.tensor.transpose(ps_t[:, i * P:(i + 1) * P], h[k % 3][:, i * P:(i + 1) * P], ident)
                    last.then_inc(t_done, 1)
                if alive(n, 0):
                    if c == 0:
                        pe.wait_ge(z_ready, t + 1)
                    wait(pe, h_ready, n - 1 if c < 2 else n - 2)
                    cols = slice(c * NC, (c + 1) * NC)
                    nc.tensor.matmul(ps_a[c % 3][:, 0:NC], zs[:, :], eg[:, cols], start=True, stop=True)\
                        .then_inc(a_done, 1)
                    nc.tensor.matmul(ps_b[c % 3][:, 0:NC], zs[:, :], eu[:, cols], start=True, stop=True)\
                        .then_inc(b_done, 1)
                if alive(n, 3):
                    k = back(c, 3)
                    pe.wait_ge(hT_ready, n - 2)
                    if k == 0:
                        wait(pe, added, t)
                    for i in range(NBK):
                        last = nc.tensor.matmul(ps_y[:, 0:D], hT[k % 3][:, i * P:(i + 1) * P], ed[:, NBK * k + i, :],
                                                start=k == 0 and i == 0, stop=k == CH - 1 and i == NBK - 1)
                    last.then_inc(down_done, 1)

            rotate_chunks(pe, step, 3)

        @block.scalar
        def _(act):
            act_in = L[:, :, :].rearrange("p a b -> p (a b)")
            nc.scalar.activation(act_in, act_in, ACT.Sigmoid).then_inc(scores_ready, 1)

            def step(n, c, t):
                if alive(n, 0):
                    act.wait_ge(a_done, n + 1)
                    wait(act, h_ready, n - 1 if c < 2 else n - 2)
                    nc.scalar.activation(s[c % 3][:, :], ps_a[c % 3][:, 0:NC], ACT.Silu).then_inc(s_ready, 1)
                if alive(n, 2):
                    act.wait_ge(t_done, n - 1)
                    k = back(c, 2)
                    wait(act, down_done, n - 3 if k < 2 else n - 4)
                    nc.scalar.activation(hT[k % 3][:, :], ps_t[:, 0:NC], ACT.Copy).then_inc(hT_ready, 1)

            rotate_chunks(act, step, 3)

        @block.gpsimd
        def _(pool):
            pool.wait_ge(gates_ready, 1)

            def step(n, c, t):
                if not alive(n, 0):
                    return
                if c == 0:
                    wait(pool, b_done, n)
                    nc.gpsimd.tensor_copy(zs[:, :], zT[:, ds(t, P)]).then_inc(z_ready, 1)
                pool.wait_ge(h_ready, n + 1)
                h3 = h[c % 3][:, :].rearrange("p (e i) -> p e i", i=W)
                gate = G[:, bass.ds(t, 1), c * CE:(c + 1) * CE].rearrange("p a b -> p (a b)")
                nc.gpsimd.tensor_tensor(h3, h3, gate.unsqueeze(2).broadcast_to([P, CE, W]), ALU.mult)\
                    .then_inc(g_ready, 1)

            rotate_chunks(pool, step, 0)

        @block.vector
        def _(dve):
            flat = lambda a: a.rearrange("p a b -> p (a b)")
            dve.wait_ge(scores_ready, 1)
            nc.vector.tensor_tensor(L[:, :, :], L[:, :, :], bias.unsqueeze(1).broadcast_to([P, TILES, E]), ALU.add)
            nc.vector.memset(grp[:, :, GRP:12], SENTINEL)
            nc.vector.memset(cand[:, :, E:ALL], SENTINEL)
            dve.drain()
            nc.vector.tensor_reduce(grp[:, :, 0:GRP], L[:, :, :].rearrange("p t (g e) -> p t g e", e=GRP), X, ALU.max)
            dve.drain()
            for t in range(TILES):
                nc.vector.max(top[:, t, :], grp[:, t, :])
            dve.drain()
            for t in range(TILES):
                nc.vector.match_replace(grp_rest[:, t, :], top[:, t, :], grp[:, t, :], -SENTINEL)
            dve.drain()
            nc.vector.tensor_tensor(grp[:, :, 0:GRP], grp[:, :, 0:GRP], grp_rest[:, :, 0:GRP], ALU.not_equal)
            dve.drain()
            for t in range(TILES):
                nc.vector.tensor_tensor(cand[:, t, 0:E].rearrange("p (g e) -> p g e", e=GRP),
                                        L[:, t, :].rearrange("p (g e) -> p g e", e=GRP),
                                        grp[:, t, 0:GRP].unsqueeze(2).broadcast_to([P, GRP, GRP]), ALU.mult)
            dve.drain()
            for t in range(TILES):
                nc.vector.max(top[:, t, :], cand[:, t, :])
            dve.drain()
            for t in range(TILES):
                nc.vector.match_replace(rest[:, t, :], top[:, t, :], cand[:, t, :], -SENTINEL)
            nc.vector.reduce_sum(den[:, :], top[:, :, 2:8], X)
            dve.drain()
            nc.vector.tensor_tensor(rest[:, :, 0:E], rest[:, :, 0:E], cand[:, :, 0:E], ALU.not_equal)
            nc.vector.tensor_scalar(den[:, :], den[:, :], 1.0e-8, None, ALU.add)
            dve.drain()
            nc.vector.tensor_tensor(rest[:, :, 0:E], rest[:, :, 0:E], cand[:, :, 0:E], ALU.mult)
            nc.vector.reciprocal(den[:, :], den[:, :])
            dve.drain()
            nc.vector.tensor_tensor(G[:, :, 0:E], rest[:, :, 0:E],
                                    den[:, :].unsqueeze(2).broadcast_to([P, TILES, E]), ALU.mult)
            nc.vector.memset(G[:, :, E:ALL], 1.0).then_inc(gates_ready, 1)

            def step(n, c, t):
                if alive(n, 0):
                    dve.wait_ge(s_ready, n + 1)
                    dve.wait_ge(b_done, n + 1)
                    wait(dve, t_done, n - 1 if c < 2 else n - 2)
                    nc.vector.tensor_tensor(h[c % 3][:, :], s[c % 3][:, :], ps_b[c % 3][:, 0:NC], ALU.mult)\
                        .then_inc(h_ready, 1)
                if alive(n, 3) and back(c, 3) == CH - 1:
                    dve.wait_ge(down_done, n - 2)
                    row = x[:, bass.ds(t - 1, 1), :].rearrange("p a b -> p (a b)")
                    nc.vector.tensor_tensor(row, row, ps_y[:, 0:D], ALU.add).then_inc(added, 1)

            rotate_chunks(dve, step, 3)



def arrive(nc, sem, value):
    with nc.Block() as block:
        @block.sync
        def _(sp):
            sp.wait_ge(sem, value)


def build(nc, A, out):
    with ExitStack() as top:
        m = Memory(nc, top)
        x = m.sb("x", [P, TILES, D])
        zT = m.sb("zT", [P, TILES * P])
        ident = m.sb("ident", [P, P])
        headmask = m.sb("headmask", [P, HEADS])
        rank = m.sb("rank", [P, 8])
        ones = m.sb("ones", [1, P])
        eps = m.sb("eps", [P, 3])
        logits = {E: m.sb(f"logits{E}", [P, TILES, E]) for E in (4, 8, 64)}
        ctxT = m.sb("ctxT", [P, B * KEYS])
        ctx2T = m.sb("ctx2T", [P, B, 2, KEYS])
        ctx_nat = m.sb("ctx_nat", [KEYS, B, D])
        small2 = {n: m.sb("L2" + n, sh) for n, sh in (
            ("wq", [P, D]), ("wk", [P, D]), ("wv", [P, D]), ("wo", [P, D]), ("bq", [P, 1]), ("bk", [P, 1]),
            ("bv", [P, D]), ("bo", [P, D]))}
        two_way = {n: m.sb("L3" + n, sh) for n, sh in (
            ("w_cq", [P, 1]), ("w_c", [P, 1]), ("w_q", [P, 1]), ("b_cq", [P, 1]), ("b_c", [P, 1]), ("b_q", [P, 1]),
            ("wl", [P, 4, D]), ("b_l", [P, D]))}
        gate2 = m.sb("gate2", [P, 8])
        gate3 = m.sb("gate3", [P, 64])
        bias3 = m.sb("bias3", [P, 64])
        x_loaded = [m.sem(f"x_loaded{g}") for g in range(GROUPS)]
        ident_loaded, first_loaded, soon_loaded, later_loaded = (m.sem(n) for n in (
            "ident_loaded", "first_loaded", "soon_loaded", "later_loaded"))
        many_loaded, stored = m.sem("many_loaded"), m.sem("stored")
        root_ln, root_rms = (1.0, eps[:, 0:1]), (1.0, eps[:, 1:2])
        root_both = (1.0 + EPS_RMS, eps[:, 2:3])

        early = ExitStack()
        me = Memory(nc, early)
        self_w = {n: me.sb("L0f" + n, sh) for n, sh in (
            ("wqkv", [P, 3 * D]), ("wo", [P, D]), ("qn", [P, 1]), ("kn", [P, 1]), ("n1", [P, 1]), ("n2", [P, 1]),
            ("gate", [P, 4]), ("e0_up", [P, 1, 256]), ("e0_down", [P, 2, D]), ("e1_w1", [P, 1, 256]),
            ("e1_w2", [P, 1, 256]), ("e1_down", [P, 2, D]), ("e2_l1", [P, 1, 256]), ("e2_l2", [P, 2, 256]),
            ("e2_l3", [P, 2, 256]), ("e2_l4", [P, 2, D]), ("e3_down", [P, 1, D]), ("e3_up", [P, 1, 256]),
            ("e3_out", [P, 2, D]))}
        small0 = {n: me.sb("L0" + n, sh) for n, sh in (
            ("wq", [P, D]), ("wk", [P, D]), ("wv", [P, D]), ("wo", [P, D]), ("bq", [P, 1]), ("bk", [P, 1]),
            ("bv", [P, D]), ("bo", [P, D]))}
        wide1 = {n: me.sb("L1" + n, sh) for n, sh in (
            ("wq", [P, 1024]), ("wk", [P, 1024]), ("wv", [P, 1024]), ("wo", [P, 8, D]), ("bq", [P, 8]), ("bk", [P, 8]),
            ("bv", [P, 8]), ("bo", [P, D]))}
        gate1 = me.sb("gate1", [P, 8])
        mask0 = me.sb("mask0", [P, TPB, KEYS])
        mask1 = me.sb("mask1", [P, TILES, KEYS], U8)
        neg1 = me.sb("neg1", [P, TILES, KEYS], BF16)
        causal = me.sb("causal", [P, P])
        causal_b = me.sb("causal_b", [P, P], BF16)
        ident_b = me.sb("ident_b", [P, P], BF16)

        whole = lambda tile: tile[tuple(slice(None) for _ in tile.shape)]
        ctx_rows = me.sb("ctx_rows", [P, B * KEYS // P, D])
        first = [(ctx_rows, A["ctx"].rearrange("(t p) d -> p t d", p=P)),
                 (headmask, A["headmask"]), (mask0, A["mask0"].rearrange("(t p) k -> p t k", p=P))]
        first += [(t, A["L0" + k]) for k, t in small0.items()]
        first += [(causal, A["causal"]), (rank, A["rank"]), (mask1, A["mask1"].rearrange("(t p) k -> p t k", p=P)),
                  (ctx_nat, A["ctx"].rearrange("(b k) d -> k b d", k=KEYS))]
        soon = [(t, A["L0f" + k]) for k, t in self_w.items()] + [(t, A["L1" + k]) for k, t in wide1.items()]
        soon += [(gate1, A["gate1"])]
        later = [(t, A["L2" + k]) for k, t in small2.items()] + [(t, A["L3" + k]) for k, t in two_way.items()]
        later += [(gate2, A["gate2"]), (gate3, A["gate3"]), (bias3, A["bias3"])]

        with nc.Block() as block:
            @block.sync
            def _(sp):
                for g in range(GROUPS):
                    tiles = slice(g * GROUP, (g + 1) * GROUP)
                    sp.dma_start(x[:, tiles, :], A["x"].rearrange("(t p) d -> p t d", p=P)[:, tiles, :])\
                        .then_inc(x_loaded[g], 16)
                    if g == 0:
                        sp.dma_start(ident[:, :], A["ident"]).then_inc(ident_loaded, 16)

            @block.vector
            def _(dve):
                nc.vector.memset(eps[:, 0:1], EPS_LN)
                nc.vector.memset(eps[:, 1:2], EPS_RMS)
                nc.vector.memset(eps[:, 2:3], EPS_LN * EPS_RMS)
                nc.vector.memset(ones[:, :], 1.0)

        def load(tiles, loaded):
            def program(sp):
                for tile, src in tiles:
                    sp.dma_start(whole(tile), src).then_inc(loaded, 16)
            return program

        idn, hm = ident[:, :], headmask[:, :]

        def finish():
            with nc.Block() as block:
                @block.sync
                def _(sp):
                    sp.dma_start(out.rearrange("(t p) d -> p t d", p=P), x[:, :, :]).then_inc(stored, 16)
                    sp.wait_ge(stored, 16)

        normalise(nc, "n0_", x, idn, root_ln, zT, arrived=x_loaded, ident_loaded=ident_loaded, then=ACT.Exp,
                  loads=load(first, first_loaded))
        with ExitStack() as stack:
            ms = Memory(nc, stack, "su_")
            ps_c = ms.ps("ps_c")
            turned, masked, copied = ms.sem("turned"), ms.sem("masked"), ms.sem("copied")
            block = stack.enter_context(nc.Block())

            @block.tensor
            def _(pe):
                pe.wait_ge(first_loaded, 16 * len(first))
                for i in range(B * KEYS // P):
                    last = nc.tensor.transpose(ps_c[:, i * P:(i + 1) * P], ctx_rows[:, i, :], idn)
                last.then_inc(turned, 1)

            @block.scalar
            def _(act):
                act.wait_ge(turned, 1)
                for i in range(2):
                    nc.scalar.activation(ctx2T[:, :, i, :], ps_c[:, :].rearrange("p (b k) -> p b k", k=KEYS), ACT.Copy)
                act.drain()
                nc.scalar.activation(ctxT[:, :].rearrange("p (b k) -> p b k", k=KEYS), ctx2T[:, :, 0, :], ACT.Copy)

            @block.vector
            def _(dve):
                dve.wait_ge(first_loaded, 16 * len(first))
                nc.vector.tensor_scalar(mask0[:, :, :], mask0[:, :, :], -1.0e9, None, ALU.mult)
                nc.vector.tensor_copy(ident_b[:, :], ident[:, :])
                nc.vector.tensor_scalar(causal_b[:, :], causal[:, :], BIG, -BIG, ALU.mult, ALU.add)
                nc.vector.tensor_scalar(neg1[:, :, :], mask1[:, :, :], BIG, -BIG, ALU.mult, ALU.add)

        with ExitStack() as stack:
            ml = Memory(nc, stack, "a0_")
            qT_all, kT_all, v2_all = ml.sb("qT", [P, TILES * P]), ml.sb("kT", [P, B * KEYS]), ml.sb("v2", [P, B, D])
            project_small(nc, "p0_", small0, zT, ctx2T, idn, qT_all, kT_all, v2_all)
            attend_small(nc, "t0_", x, small0, qT_all, kT_all, v2_all, idn, hm, HD ** -0.5, neg=mask0,
                         loads=load(soon, soon_loaded))
        with ExitStack() as stack:
            ml = Memory(nc, stack, "f0_")
            x2 = ml.sb("x2", [P, TILES, D])
            arrive(nc, soon_loaded, 16 * len(soon))
            normalise(nc, "n1_", x, idn, root_both, zT, second=root_ln, out_natural=x2,
                      channel_scale=self_w["n1"][:, 0:1])
            with ExitStack() as inner:
                mi = Memory(nc, inner, "s0_")
                qT_all, kT_all = mi.sb("qT", [P, TILES * P]), mi.sb("kT", [P, TILES * P])
                v_all = mi.sb("v", [P, TILES, D])
                project_self(nc, "q0_", self_w, zT, idn, qT_all, kT_all, v_all, eps[:, 1:2])
                attend_self(nc, "u0_", x2, self_w, qT_all, kT_all, v_all, idn, hm, causal_b[:, :], ident_b[:, :])
            normalise(nc, "n3_", x2, idn, root_rms, zT, center=False, channel_scale=self_w["n2"][:, 0:1],
                      gate_w=self_w["gate"], logits=logits[4], then=ACT.Exp)
            experts_mixed(nc, "e0_", x, x2, self_w, zT, logits[4], rank)
        clear_spent(nc)
        normalise(nc, "n4_", x, idn, root_ln, zT, then=ACT.Exp)
        with ExitStack() as stack:
            ml = Memory(nc, stack, "a1_")
            kT_all, vT_all = ml.sb("kT", [P, 8, B * KEYS]), ml.sb("vT", [P, 8, B * KEYS])
            project_wide(nc, "p1_", wide1, ctxT, kT_all, vT_all)
            attend_wide(nc, "t1_", x, wide1, zT, kT_all, vT_all, idn, neg1, ident_b[:, :],
                        loads=load(later, later_loaded))
        normalise(nc, "n5_", x, idn, root_ln, zT, gate_w=gate1, logits=logits[8], then=ACT.Exp)
        experts_gated(nc, "e1_", x, zT, logits[8], rank, 8, 4, A["L1w1"], A["L1w3"], A["L1w2"])
        early.close()
        clear_spent(nc)
        eg, eu = m.sb("eg", [P, 66 * 64]), m.sb("eu", [P, 66 * 64])
        ed = m.sb("ed", [P, 33, D])
        with nc.Block() as block:
            @block.sync
            def _(sp):
                sp.wait_ge(later_loaded, 16 * len(later))
                for dst, src in ((eg[:, 0:4096], "L3eg"), (eg[:, 4096:], "L3sg"), (eu[:, 0:4096], "L3eu"),
                                 (eu[:, 4096:], "L3su"),
                                 (ed[:, 0:32, :].rearrange("p a b -> p (a b)"), "L3ed"), (ed[:, 32, :], "L3sd")):
                    sp.dma_start(dst, A[src]).then_inc(many_loaded, 16)
        normalise(nc, "n6_", x, idn, root_ln, zT, then=ACT.Exp)
        with ExitStack() as stack:
            ml = Memory(nc, stack, "a2_")
            qT_all, kT_all, v2_all = ml.sb("qT", [P, TILES * P]), ml.sb("kT", [P, B * KEYS]), ml.sb("v2", [P, B, D])
            project_small(nc, "p2_", small2, zT, ctx2T, idn, qT_all, kT_all, v2_all)
            attend_small(nc, "t2_", x, small2, qT_all, kT_all, v2_all, idn, hm, HD ** -0.5)
        normalise(nc, "n7_", x, idn, root_ln, zT, gate_w=gate2, logits=logits[8], then=ACT.Exp)
        experts_gated(nc, "e2_", x, zT, logits[8], rank, 8, 2, A["L2w1"], A["L2w3"], A["L2w2"])
        clear_spent(nc)
        normalise(nc, "n8_", x, idn, root_ln, zT, then=ACT.Exp)
        attend_two_way(nc, "t3_", x, two_way, zT, ctxT, ctx_nat, idn, ones[:, :])
        arrive(nc, many_loaded, 6 * 16)
        normalise(nc, "n9_", x, idn, root_ln, zT, gate_w=gate3, logits=logits[64], then=ACT.Sigmoid)
        experts_many(nc, "e3_", x, zT, logits[64], bias3[:, :], eg, eu, ed, idn)
        finish()


def lay_out(i):
    import numpy as np

    c = lambda a: np.ascontiguousarray(a)
    rows = lambda v: c(np.broadcast_to(v.reshape(1, -1), (P, v.size)))
    col = lambda v: c(v.reshape(-1, 1))
    split = lambda a: c(a.reshape(-1, P, a.shape[-1]).transpose(1, 0, 2))
    f = {k: np.asarray(v) for k, v in i.items()}
    a = {"x": f["x"].reshape(-1, D), "ctx": f["ctx_1024"].reshape(-1, D),
         "mask0": f["mask_1x1xSxS2_fk1"].reshape(S, KEYS),
         "mask1": f["mask_BxSxS2_bk1"].reshape(B * S, KEYS),
         "ident": np.eye(P, dtype=np.float32),
         "headmask": np.repeat(np.eye(HEADS, dtype=np.float32), HD, axis=0),
         "rank": np.tile(np.arange(8, 0, -1, dtype=np.float32), (P, 1)),
         "causal": np.tril(np.ones((P, P), np.float32))}
    for n, b in (("q", "q"), ("k", "k")):
        a["L0w" + n], a["L0b" + b] = f["L0_xattn_w" + n], col(f["L0_xattn_b" + b])
        a["L2w" + n], a["L2b" + b] = c(f["L2_xattn_W" + n].T), col(f["L2_xattn_b" + b])
    for n in "vo":
        a["L0w" + n], a["L0b" + n] = f["L0_xattn_w" + n], rows(f["L0_xattn_b" + n])
        a["L2w" + n], a["L2b" + n] = c(f["L2_xattn_W" + n].T), rows(f["L2_xattn_b" + n])
    g = lambda n: f["L0_ffn_" + n]
    a["L0fwqkv"] = c(np.concatenate([g("wq").T, g("wk").T, g("wv").T], axis=1))
    a["L0fwo"] = c(g("wo").T)
    a["L0fqn"], a["L0fkn"] = col(np.tile(g("qn_w"), HEADS)), col(np.tile(g("kn_w"), HEADS))
    a["L0fn1"], a["L0fn2"] = col(g("n1_w")), col(g("n2_w"))
    a["L0fgate"] = c(g("gate_w").T)
    for n in ("e0_up", "e0_down", "e1_w1", "e1_w2", "e1_down", "e2_l1", "e2_l2", "e2_l3", "e2_l4", "e3_down",
              "e3_up", "e3_out"):
        a["L0f" + n] = split(g(n).T)
    for n in "qkv":
        a["L1w" + n] = c(f["L1_xattn_w" + n].transpose(1, 0, 2).reshape(D, 1024))
        a["L1b" + n] = c(f["L1_xattn_b" + n].reshape(8, P).T)
    a["L1wo"], a["L1bo"] = split(f["L1_xattn_wo"]), rows(f["L1_xattn_bo"])
    a["gate1"], a["gate2"] = f["L1_ffn_gate_w"], c(f["L2_ffn_Wg"].T)
    down = lambda w: c(w.reshape(8, -1, P, D).transpose(0, 2, 1, 3).reshape(8, P, -1))
    a["L1w1"], a["L1w3"], a["L1w2"] = f["L1_ffn_w1"], f["L1_ffn_w3"], down(f["L1_ffn_w2"])
    a["L2w1"], a["L2w3"] = c(f["L2_ffn_W1"].transpose(0, 2, 1)), c(f["L2_ffn_W2"].transpose(0, 2, 1))
    a["L2w2"] = down(f["L2_ffn_W3"].transpose(0, 2, 1))
    for n in ("w_cq", "w_c", "w_q"):
        a["L3" + n] = col(f["L3_xattn_" + n])
    for n in ("b_cq", "b_c", "b_q"):
        a["L3" + n] = c(np.broadcast_to(f["L3_xattn_" + n].reshape(1, 1), (P, 1)))
    a["L3wl"], a["L3b_l"] = split(f["L3_xattn_W_l"].T), rows(f["L3_xattn_b_l"])
    a["gate3"], a["bias3"] = c(f["L3_ffn_gate_w"].T), rows(f["L3_ffn_gate_bias"])
    for n in ("eg", "eu"):
        a["L3" + n] = c(f[f"L3_ffn_{n}_w"].transpose(2, 0, 1).reshape(D, -1))
    a["L3sg"], a["L3su"] = c(f["L3_ffn_sg_w"].T), c(f["L3_ffn_su_w"].T)
    a["L3ed"] = c(f["L3_ffn_ed_w"].transpose(0, 2, 1).reshape(32, P, D).transpose(1, 0, 2).reshape(P, -1))
    a["L3sd"] = c(f["L3_ffn_sd_w"].T)
    return a


def kernel(**inputs):
    import numpy as np
    import concourse.bacc as bacc
    from concourse.bass_utils import run_bass_kernel_spmd

    nc = bacc.Bacc("TRN2", target_bir_lowering=False, num_devices=1)
    arrays = {f"in_{n}": np.ascontiguousarray(a) for n, a in lay_out(inputs).items()}
    aps = {n[3:]: nc.dram_tensor(n, a.shape, mybir.dt.from_np(a.dtype), kind="ExternalInput").ap()
           for n, a in arrays.items()}
    out = nc.dram_tensor("out", (B * S, D), F32, kind="ExternalOutput").ap()
    build(nc, aps, out)
    r = run_bass_kernel_spmd(nc, [arrays], core_ids=[0])
    return r.results[0]["out"].reshape(B, S, D)
```

```python
from contextlib import ExitStack

import concourse.bass as bass
from concourse import mybir

F32 = mybir.dt.float32
F32R = mybir.dt.float32r
BF16 = mybir.dt.bfloat16
U8 = mybir.dt.uint8
ALU = mybir.AluOpType
ACT = mybir.ActivationFunctionType
X = mybir.AxisListType.X

P = 128
B, S, D = 8, 256, 128
KEYS = 64
TILES = B * S // P
TPB = S // P
HEADS = 16
HD = D // HEADS
GROUP = 4
GROUPS = TILES // GROUP
BIG = 1.0e30
EPS_LN, EPS_RMS = 1.0e-5, 1.1920929e-07
KEEP = 32


def wait(eng, sem, value):
    if not isinstance(value, int) or value > 0:
        eng.wait_ge(sem, value)


def ds(i, n):
    return bass.ds(i * n, n)


class Memory:

    def __init__(self, nc, stack, tag=""):
        self.nc, self.stack, self.tag = nc, stack, tag

    def sb(self, name, shape, dt=F32):
        return self.stack.enter_context(self.nc.sbuf_tensor(self.tag + name, shape, dt))

    def ps(self, name, cols=512):
        return self.stack.enter_context(self.nc.psum_tensor(self.tag + name, [P, cols], F32))

    def sem(self, name):
        handle = self.stack.enter_context(self.nc.semaphore(self.tag + name))
        if self.tag:
            SPENT.append(handle.num)
        return handle


SPENT = []


def clear_spent(nc):
    with nc.Block() as block:
        @block.gpsimd
        def _(pool):
            nums = sorted(set(SPENT))
            while nums:
                n = 1
                while n < len(nums) and nums[n] == nums[0] + n:
                    n += 1
                pool.sem_clear(range(nums[0], nums[0] + n))
                nums = nums[n:]
    SPENT.clear()



def normalise(nc, tag, src, ident, root, out_T, center=True, second=None, out_natural=None, channel_scale=1.0,
              gate_w=None, logits=None, arrived=None, ident_loaded=None, then=None, loads=None, parts=None,
              meanwhile=None, before=None):
    HALF = TILES // 2
    with ExitStack() as stack:
        m = Memory(nc, stack, tag)
        stats = m.sb("stats", [P, TILES, 6])
        sum2, dif, ssq, mean, dif2, var, std, rstd, std2, rstd2 = (m.sb(n, [P, TILES]) for n in (
            "sum2", "dif", "ssq", "mean", "dif2", "var", "std", "rstd", "std2", "rstd2"))
        scratch = m.sb("scratch", [P, 1])
        zn = [m.sb(f"zn{i}", [P, GROUP, D]) for i in range(2)]
        ps_t = [m.ps(f"ps_t{i}") for i in range(2)]
        E = gate_w.shape[1] if gate_w is not None else 0
        ps_g = m.ps("ps_g", max(512, TILES * E)) if gate_w is not None else None
        var_ready, std_ready, rstd2_ready = m.sem("var_ready"), m.sem("std_ready"), m.sem("rstd2_ready")
        normed, turned = m.sem("normed"), m.sem("turned")
        evacuated, logits_done, high_ready = m.sem("evacuated"), m.sem("logits_done"), m.sem("high_ready")
        block = stack.enter_context(nc.Block())

        if loads is not None:
            block.sync(loads)

        @block.vector
        def _(dve):
            def low_part(g):
                cols = slice(g * 512, (g + 1) * 512)
                dve.wait_ge(high_ready, g + 1)
                nc.vector.tensor_tensor(parts[1][:, cols], out_T[:, cols], parts[0][:, cols], ALU.subtract)

            for half in range(2):
                h = slice(half * HALF, (half + 1) * HALF)
                for t in range(half * HALF, (half + 1) * HALF):
                    if arrived is not None and t % GROUP == 0:
                        dve.wait_ge(arrived[t // GROUP], 16)
                    nc.vector.bn_stats(stats[:, t, :], src[:, t, :])
                dve.drain()
                nc.vector.tensor_tensor(sum2[:, h], stats[:, h, 1], stats[:, h, 4], ALU.add)
                nc.vector.tensor_tensor(dif[:, h], stats[:, h, 1], stats[:, h, 4], ALU.subtract)
                nc.vector.tensor_tensor(ssq[:, h], stats[:, h, 2], stats[:, h, 5], ALU.add)
                dve.drain()
                nc.vector.tensor_scalar(mean[:, h], sum2[:, h], 0.5, None, ALU.mult)
                nc.vector.scalar_tensor_tensor(out=dif2[:, h], in0=dif[:, h], scalar=0.25, in1=dif[:, h],
                                               op0=ALU.mult, op1=ALU.mult)
                dve.drain()
                last = nc.vector.scalar_tensor_tensor(out=var[:, h], in0=ssq[:, h], scalar=1.0 / D, in1=dif2[:, h],
                                                      op0=ALU.mult, op1=ALU.add)
                if not center:
                    dve.drain()
                    nc.vector.tensor_tensor(dif2[:, h], mean[:, h], mean[:, h], ALU.mult)
                    dve.drain()
                    last = nc.vector.tensor_tensor(var[:, h], var[:, h], dif2[:, h], ALU.add)
                last.then_inc(var_ready, 1)
            for g in range(GROUPS):
                if g % 2 == 0:
                    half = g // 2
                    h = slice(half * HALF, (half + 1) * HALF)
                    dve.wait_ge(std_ready, half + 1)
                    nc.vector.reciprocal(rstd[:, h], std[:, h])
                    if out_natural is not None:
                        nc.vector.reciprocal(rstd2[:, h], std2[:, h]).then_inc(rstd2_ready, 1)
                    dve.drain()
                if g >= 2:
                    dve.wait_ge(turned, g - 1)
                for j in range(GROUP):
                    t = g * GROUP + j
                    if center:
                        last = nc.vector.tensor_scalar(zn[g % 2][:, j, :], src[:, t, :], mean[:, t:t + 1],
                                                       rstd[:, t:t + 1], ALU.subtract, ALU.mult)
                    else:
                        last = nc.vector.tensor_scalar(zn[g % 2][:, j, :], src[:, t, :], rstd[:, t:t + 1], None,
                                                       ALU.mult)
                last.then_inc(normed, 1)
                if parts is not None and g > 0:
                    low_part(g - 1)
            if parts is not None:
                low_part(GROUPS - 1)
            if out_natural is not None:
                for t in range(HALF, TILES):
                    nc.vector.tensor_scalar(out_natural[:, t, :], src[:, t, :], mean[:, t:t + 1],
                                            rstd2[:, t:t + 1], ALU.subtract, ALU.mult)
            if gate_w is not None:
                dve.wait_ge(logits_done, 1)
                nc.vector.tensor_copy(logits[:, :, :], ps_g[:, 0:TILES * E].rearrange("p (a b) -> p a b", b=E))

        @block.scalar
        def _(act):
            if before is not None:
                before(act)
            nc.scalar.activation(scratch[:, :], root[1], ACT.Sqrt)
            for half in range(2):
                h = slice(half * HALF, (half + 1) * HALF)
                act.wait_ge(var_ready, half + 1)
                last = nc.scalar.activation(std[:, h], var[:, h], ACT.Sqrt, scale=root[0], bias=root[1])
                if out_natural is not None:
                    last = nc.scalar.activation(std2[:, h], var[:, h], ACT.Sqrt, scale=second[0], bias=second[1])
                last.then_inc(std_ready, 1)
            for g in range(GROUPS):
                act.wait_ge(turned, g + 1)
                nc.scalar.activation(out_T[:, g * 512:(g + 1) * 512], ps_t[g % 2][:, :], ACT.Copy, scale=channel_scale)\
                    .then_inc(evacuated, 1)
                if parts is not None:
                    act.wait_ge(evacuated, g + 1)
                    nc.scalar.activation(parts[0][:, g * 512:(g + 1) * 512], out_T[:, g * 512:(g + 1) * 512], ACT.Copy)\
                        .then_inc(high_ready, 1)
            if then is not None:
                act.drain()
                nc.scalar.activation(scratch[:, :], root[1], then)

        @block.tensor
        def _(pe):
            def router(g):
                pe.wait_ge(evacuated, g + 1)
                for t in range(g * GROUP, (g + 1) * GROUP):
                    last = nc.tensor.matmul(ps_g[:, t * E:(t + 1) * E], out_T[:, t * P:(t + 1) * P],
                                            gate_w[:, :], start=True, stop=True)
                return last

            if ident_loaded is not None:
                pe.wait_ge(ident_loaded, 16)
            for g in range(GROUPS):
                pe.wait_ge(normed, g + 1)
                if g >= 2:
                    pe.wait_ge(evacuated, g - 1)
                for j in range(GROUP):
                    last = nc.tensor.transpose(ps_t[g % 2][:, j * P:(j + 1) * P], zn[g % 2][:, j, :], ident)
                last.then_inc(turned, 1)
                if gate_w is not None and g > 0:
                    router(g - 1)
            if gate_w is not None:
                router(GROUPS - 1).then_inc(logits_done, 1)

        if meanwhile is not None:
            block.gpsimd(meanwhile)

        if out_natural is not None:
            @block.gpsimd
            def _(pool):
                pool.wait_ge(rstd2_ready, 1)
                for t in range(HALF):
                    nc.gpsimd.tensor_scalar(out_natural[:, t, :], src[:, t, :], mean[:, t:t + 1],
                                            rstd2[:, t:t + 1], ALU.subtract, ALU.mult)


LAGS = 4


def rotate(eng, step, lags=LAGS):
    for t in range(4):
        step(t, t, t // TPB)
    with eng.Fori(1, TILES // 4) as i:
        for r in range(4):
            step(i * 4 + r, r, i * 2 + r // TPB)
    for t in range(TILES, TILES + lags):
        step(t, t % 4, t // TPB)


def live(t, lag):
    return not isinstance(t, int) or 0 <= t - lag < TILES



def project_small(nc, tag, w, zT, ctx2T, ident, qT_all, kT_all, v2_all):
    with ExitStack() as stack:
        m = Memory(nc, stack, tag)
        pq = [m.ps(f"pq{i}") for i in range(2)]
        pk = m.ps("pk")
        pv = m.ps("pv", 1024)
        q_done, q_out, k_done, v_done = m.sem("q_done"), m.sem("q_out"), m.sem("k_done"), m.sem("v_done")
        block = stack.enter_context(nc.Block())

        @block.tensor
        def _(pe):
            nc.tensor.matmul(pk[:, :].rearrange("p (b k) -> p b k", k=KEYS), w["wk"][:, :], ctx2T[:, :, 0, :],
                             start=True, stop=True).then_inc(k_done, 1)
            for b in range(B):
                last = nc.tensor.matmul(pv[:, b * D:(b + 1) * D],
                                        ctx2T[:, b, :, :].rearrange("p a k -> p (a k)"),
                                        w["wv"][:, :], start=True, stop=True)
            last.then_inc(v_done, 1)
            for g in range(GROUPS):
                if g >= 2:
                    pe.wait_ge(q_out, g - 1)
                nc.tensor.matmul(pq[g % 2][:, :], w["wq"][:, :], zT[:, g * 512:(g + 1) * 512],
                                 start=True, stop=True).then_inc(q_done, 1)

        @block.scalar
        def _(act):
            act.wait_ge(k_done, 1)
            nc.scalar.activation(kT_all[:, :], pk[:, :], ACT.Identity, bias=w["bk"][:, 0:1])
            for g in range(GROUPS):
                act.wait_ge(q_done, g + 1)
                nc.scalar.activation(qT_all[:, g * 512:(g + 1) * 512], pq[g % 2][:, :], ACT.Identity,
                                     bias=w["bq"][:, 0:1]).then_inc(q_out, 1)

        @block.vector
        def _(dve):
            dve.wait_ge(v_done, 1)
            nc.vector.tensor_tensor(v2_all[:, :, :], pv[:, :].rearrange("p (b d) -> p b d", d=D),
                                    w["bv"][:, :].unsqueeze(1).broadcast_to([P, B, D]), ALU.add)


def attend_small(nc, tag, x, w, qT_all, kT_all, v2_all, ident, headmask, scale, neg=None, loads=None):
    with ExitStack() as stack:
        m = Memory(nc, stack, tag)
        qs = [m.sb(f"qs{i}", [P, P]) for i in range(2)]
        kbd = [m.sb(f"kbd{i}", [P, HEADS, KEYS]) for i in range(2)]
        NA = 8 * HD + 8
        vaug = [m.sb(f"vaug{i}", [P, 2, 4 * (NA + 2 * HD)]) for i in range(2)]
        sm = [m.sb(f"sm{i}", [P, HEADS, KEYS]) for i in range(2)]
        mx = [m.sb(f"mx{i}", [P, HEADS]) for i in range(2)]
        pT = [m.sb(f"pT{i}", [P, 8, P]) for i in range(2)]
        rden = m.sb("rden", [P, 2, 8])
        on = [m.sb(f"on{i}", [P, D]) for i in range(2)]
        onT = [m.sb(f"onT{i}", [P, P]) for i in range(2)]
        ps_s = [m.ps(f"ps_s{i}", 1024) for i in range(2)]
        ps_t = m.ps("ps_t", 1024)
        ps_o = m.ps("ps_o")
        ps_w = m.ps("ps_w")
        (bias_added, k_ready, v_ready, q_ready, s_done, s_used, sub_done, p_ready, t_done, pT_ready, o_done, on_ready,
         ot_done, onT_ready, w_done, x_done, zeroed) = (m.sem(n) for n in (
             "bias_added", "k_ready", "v_ready", "q_ready", "s_done", "s_used", "sub_done", "p_ready", "t_done", "pT_ready", "o_done",
             "on_ready", "ot_done", "onT_ready", "w_done", "x_done", "zeroed"))
        block = stack.enter_context(nc.Block())
        if loads is not None:
            block.sync(loads)

        @block.gpsimd
        def _(pool):
            def step(t, r, b):
                if not live(t, 0):
                    return
                if r % 2 == 0:
                    b2 = r // 2
                    wait(pool, s_done, t - 2)
                    nc.gpsimd.tensor_tensor(kbd[b2][:, :, :],
                                            kT_all[:, ds(b, KEYS)].unsqueeze(1).broadcast_to([P, HEADS, KEYS]),
                                            headmask.unsqueeze(2).broadcast_to([P, HEADS, KEYS]), ALU.mult)\
                        .then_inc(k_ready, 1)
                wait(pool, s_done, t - 1)
                nc.gpsimd.tensor_copy(qs[r % 2][:, :], qT_all[:, ds(t, P)]).then_inc(q_ready, 1)
                row = x[:, bass.ds(t, 1), :].rearrange("p a b -> p (a b)")
                nc.gpsimd.tensor_tensor(row, row, w["bo"][:, :], ALU.add).then_inc(bias_added, 1)

            rotate(pool, step, 0)

        @block.tensor
        def _(pe):
            def step(t, r, b):
                p = r % 2
                if live(t, 0):
                    pe.wait_ge(q_ready, t + 1)
                    if r % 2 == 0:
                        pe.wait_ge(k_ready, b + 1)
                    wait(pe, s_used if neg is not None else sub_done, t - 1)
                    for h in range(2):
                        last = nc.tensor.matmul(ps_s[p][:, h * 512:(h + 1) * 512], qs[p][:, :],
                                                kbd[r // 2][:, 8 * h:8 * h + 8, :].rearrange("p a b -> p (a b)"),
                                                start=True, stop=True)
                    last.then_inc(s_done, 1)
                if live(t, 1):
                    pe.wait_ge(p_ready, t)
                    wait(pe, pT_ready, t - 1)
                    for j in range(8):
                        last = nc.tensor.transpose(ps_t[:, j * P:(j + 1) * P],
                                                   sm[1 - p][:, 2 * j:2 * j + 2, :].rearrange("p a b -> p (a b)"), ident)
                    last.then_inc(t_done, 1)
                if live(t, 3):
                    pe.wait_ge(on_ready, t - 2)
                    wait(pe, x_done, t - 3)
                    nc.tensor.transpose(ps_w[:, P:2 * P], on[1 - p][:, :], ident).then_inc(ot_done, 1)
                if live(t, 2):
                    pe.wait_ge(pT_ready, t - 1)
                    vb = ((r - 2) % 4) // 2
                    if r % 2 == 0:
                        pe.wait_ge(v_ready, b)
                    for j in range(8):
                        a, pair = j // 4, j % 4
                        last = nc.tensor.matmul(ps_o[:, a * NA:(a + 1) * NA], pT[p][:, j, :],
                                                vaug[vb][:, a, pair * NA:(pair + 1) * NA],
                                                start=pair == 0, stop=pair == 3)
                    last.then_inc(o_done, 1)
                if live(t, 3):
                    pe.wait_ge(onT_ready, t - 2)
                    nc.tensor.matmul(ps_w[:, 0:P], onT[1 - p][:, :], w["wo"][:, :],
                                     start=True, stop=True).then_inc(w_done, 1)

            rotate(pe, step)

        @block.scalar
        def _(act):
            act.wait_ge(zeroed, 1)

            def step(t, r, b):
                p = r % 2
                if live(t, 0) and p == 0:
                    wait(act, o_done, t - 2)
                    for half in range(2):
                        rows = slice(64 * half, 64 * half + 64)
                        out = vaug[r // 2][rows, :, :].rearrange("p a (j c) -> p (a j) c", c=NA + 2 * HD)
                        src = v2_all[rows, bass.ds(b, 1), :].rearrange("p a (j e d) -> p (a j) e d", e=2, d=HD)
                        last = nc.scalar.activation(out[:, :, HD * half:HD * half + HD], src[:, :, half, :], ACT.Copy)
                    last.then_inc(v_ready, 1)
                if live(t, 1):
                    act.wait_ge(t_done, t)
                    wait(act, o_done, t - 2)
                    nc.scalar.activation(pT[1 - p][:, :, :].rearrange("p a b -> p (a b)"), ps_t[:, :], ACT.Copy)\
                        .then_inc(pT_ready, 1)
                if live(t, 3):
                    act.wait_ge(ot_done, t - 2)
                    wait(act, w_done, t - 4)
                    nc.scalar.activation(onT[1 - p][:, :], ps_w[:, P:2 * P], ACT.Copy).then_inc(onT_ready, 1)
                if live(t, 0):
                    act.wait_ge(sub_done, t + 1)
                    flat = sm[p][:, :, :].rearrange("p a b -> p (a b)")
                    nc.scalar.activation(flat, flat, ACT.Exp, scale=1.0 if neg is not None else scale)\
                        .then_inc(p_ready, 1)

            rotate(act, step)

        @block.vector
        def _(dve):
            for i in range(2):
                nc.vector.memset(vaug[i][:, :, :], 0.0)
            dve.drain()
            for i in range(2):
                for half in range(2):
                    rows = slice(64 * half, 64 * half + 64)
                    for pair in range(4):
                        c = pair * NA + 8 * HD + 2 * pair + half
                        last = nc.vector.memset(vaug[i][rows, :, c:c + 1], 1.0)
            last.then_inc(zeroed, 1)

            def step(t, r, b):
                p = r % 2
                if live(t, 4):
                    dve.wait_ge(w_done, t - 3)
                    dve.wait_ge(bias_added, t - 3)
                    row = x[:, bass.ds(t - 4, 1), :].rearrange("p a b -> p (a b)")
                    nc.vector.tensor_tensor(row, row, ps_w[:, 0:P], ALU.add).then_inc(x_done, 1)
                if live(t, 0):
                    dve.wait_ge(s_done, t + 1)
                    wait(dve, t_done, t - 1)
                    s3 = ps_s[p][:, :].rearrange("p (h k) -> p h k", k=KEYS)
                    if neg is not None:
                        tile = neg[:, bass.ds(t, 1), :] if neg.shape[1] == TILES else neg[:, r % 2:r % 2 + 1, :]
                        nc.vector.scalar_tensor_tensor(out=sm[p][:, :, :], in0=s3, scalar=scale,
                                                       in1=tile.broadcast_to([P, HEADS, KEYS]),
                                                       op0=ALU.mult, op1=ALU.add).then_inc(s_used, 1)
                        s3 = sm[p][:, :, :]
                        dve.drain()
                    nc.vector.tensor_reduce(mx[p][:, :], s3, X, ALU.max)
                    dve.drain()
                    last = nc.vector.tensor_tensor(sm[p][:, :, :], s3,
                                                   mx[p][:, :].unsqueeze(2).broadcast_to([P, HEADS, KEYS]), ALU.subtract)
                    last.then_inc(sub_done, 1)
                if live(t, 2):
                    dve.wait_ge(o_done, t - 1)
                    wait(dve, ot_done, t - 3)
                    halves = ps_o[:, 0:2 * NA].rearrange("p (a c) -> p a c", c=NA)
                    nc.vector.reciprocal(rden[:, :, :], halves[:, :, 8 * HD:NA])
                    dve.drain()
                    nc.vector.tensor_tensor(on[p][:, :].rearrange("p (a h d) -> p a h d", a=2, d=HD),
                                            halves[:, :, 0:8 * HD].rearrange("p a (h d) -> p a h d", d=HD),
                                            rden[:, :, :].unsqueeze(3).broadcast_to([P, 2, 8, HD]), ALU.mult)\
                        .then_inc(on_ready, 1)

            rotate(dve, step)



def project_wide(nc, tag, w, ctxT, kT_all, vT_all):
    with ExitStack() as stack:
        m = Memory(nc, stack, tag)
        pb = [m.ps(f"pb{i}") for i in range(4)]
        done, out = m.sem("done"), m.sem("out")
        block = stack.enter_context(nc.Block())

        @block.tensor
        def _(pe):
            n = 0
            for name in ("wk", "wv"):
                for j in range(8):
                    if n >= 4:
                        pe.wait_ge(out, n - 3)
                    nc.tensor.matmul(pb[n % 4][:, :], w[name][:, j * P:(j + 1) * P], ctxT[:, :],
                                     start=True, stop=True).then_inc(done, 1)
                    n += 1

        @block.scalar
        def _(act):
            n = 0
            for bias, dst in (("bk", kT_all), ("bv", vT_all)):
                for j in range(8):
                    act.wait_ge(done, n + 1)
                    nc.scalar.activation(dst[:, j, :], pb[n % 4][:, :], ACT.Identity,
                                         bias=w[bias][:, j:j + 1]).then_inc(out, 1)
                    n += 1


def attend_wide(nc, tag, x, w, zT, kT_all, vT_all, ident, neg, ident_b, loads=None):
    scale = 0.125
    with ExitStack() as stack:
        m = Memory(nc, stack, tag)
        qT = [m.sb(f"qT{i}", [P, 8, P]) for i in range(2)]
        kbd = [m.sb(f"kbd{i}", [P, 8, 2, KEYS]) for i in range(2)]
        vbd = m.sb("vbd", [P, 8, 2, KEYS])
        vw = [m.sb(f"vw{i}", [P, 8, D]) for i in range(2)]
        sm = [m.sb(f"sm{i}", [P, HEADS, KEYS]) for i in range(4)]
        mx = [m.sb(f"mx{i}", [P, HEADS]) for i in range(2)]
        den = [m.sb(f"den{i}", [P, HEADS]) for i in range(2)]
        pT = [m.sb(f"pT{i}", [P, 8, P]) for i in range(2)]
        ps_q = m.ps("ps_q", 1024)
        ps_s = m.ps("ps_s", 1024)
        ps_t = m.ps("ps_t", 1024)
        ps_v = m.ps("ps_v", 512)
        ps_o = m.ps("ps_o", 512)
        (bias_added, zeroed, k_ready, v_ready, vw_done, vw_ready, q_done, qT_ready, s_done, sub_done, exp_done,
         den_ready, p_ready, t_done, pT_ready, o_done, x_done) = (m.sem(n) for n in (
             "bias_added", "zeroed", "k_ready", "v_ready", "vw_done", "vw_ready", "q_done", "qT_ready", "s_done",
             "sub_done", "exp_done", "den_ready", "p_ready", "t_done", "pT_ready", "o_done", "x_done"))
        block = stack.enter_context(nc.Block())

        if loads is not None:
            block.sync(loads)

        @block.gpsimd
        def _(pool):
            nc.gpsimd.memset(vbd[:, :, :, :], 0.0)
            for i in range(2):
                last = nc.gpsimd.memset(kbd[i][:, :, :, :], 0.0)
            last.then_inc(zeroed, 1)

            def step(t, r, b):
                if live(t, 0):
                    row = x[:, bass.ds(t, 1), :].rearrange("p a b -> p (a b)")
                    nc.gpsimd.tensor_tensor(row, row, w["bo"][:, :], ALU.add).then_inc(bias_added, 1)
                if live(t, 2):
                    pool.wait_ge(den_ready, t - 1)
                    tile = sm[(r - 2) % 4][:, :, :]
                    nc.gpsimd.tensor_tensor(tile, tile, den[r % 2][:, :].unsqueeze(2)
                                            .broadcast_to([P, HEADS, KEYS]), ALU.mult).then_inc(p_ready, 1)

            rotate(pool, step)

        @block.tensor
        def _(pe):
            def step(t, r, b):
                p = r % 2
                if live(t, 0):
                    wait(pe, qT_ready, t)
                    for j in range(8):
                        last = nc.tensor.matmul(ps_q[:, j * P:(j + 1) * P], w["wq"][:, j * P:(j + 1) * P],
                                                zT[:, ds(t, P)], start=True, stop=True)
                    last.then_inc(q_done, 1)
                if live(t, 3):
                    pe.wait_ge(p_ready, t - 2)
                    wait(pe, pT_ready, t - 3)
                    tile = sm[(r - 3) % 4]
                    for j in range(8):
                        last = nc.tensor.transpose(ps_t[:, j * P:(j + 1) * P],
                                                   tile[:, 2 * j:2 * j + 2, :].rearrange("p a b -> p (a b)"), ident)
                    last.then_inc(t_done, 1)
                if live(t, 1):
                    pe.wait_ge(qT_ready, t)
                    if p == 1:
                        pe.wait_ge(k_ready, b + 1)
                    wait(pe, sub_done, t - 1)
                    for half in range(2):
                        nc.tensor.matmul(ps_s[:, half * 512:(half + 1) * 512].rearrange("p (h k) -> p h k", k=KEYS),
                                         ident_b, neg[:, bass.ds(t - 1, 1), :].broadcast_to([P, 8, KEYS]),
                                         start=True, stop=False, skip_group_check=True)
                        for j in range(4 * half, 4 * half + 4):
                            last = nc.tensor.matmul(ps_s[:, j * P:(j + 1) * P], qT[1 - p][:, j, :],
                                                    kbd[((r - 1) % 4) // 2][:, j, :, :].rearrange("p a b -> p (a b)"),
                                                    start=False, stop=j % 4 == 3, skip_group_check=True)
                    last.then_inc(s_done, 1)
                if live(t, 4):
                    pe.wait_ge(pT_ready, t - 3)
                    wait(pe, x_done, t - 4)
                    if p == 0:
                        pe.wait_ge(vw_ready, b * 2 - 2)
                    for j in range(8):
                        last = nc.tensor.matmul(ps_o[:, 0:D], pT[p][:, j, :], vw[r // 2][:, j, :],
                                                start=j == 0, stop=j == 7)
                    last.then_inc(o_done, 1)
                if live(t, 2):
                    pe.wait_ge(v_ready, b)
                    wait(pe, vw_ready, b * 2 - 2 + p)
                    for j in range(4 * p, 4 * p + 4):
                        last = nc.tensor.matmul(ps_v[:, (j % 4) * P:(j % 4 + 1) * P],
                                                vbd[:, j, :, :].rearrange("p a b -> p (a b)"), w["wo"][:, j, :],
                                                start=True, stop=True)
                    last.then_inc(vw_done, 1)

            rotate(pe, step)

        @block.scalar
        def _(act):
            act.wait_ge(zeroed, 1)

            def step(t, r, b):
                p = r % 2
                if live(t, 0) and p == 0:
                    wait(act, s_done, t - 2)
                    for half in range(2):
                        rows = slice(64 * half, 64 * half + 64)
                        last = nc.scalar.activation(kbd[r // 2][rows, :, half, :], kT_all[rows, :, ds(b, KEYS)], ACT.Copy)
                    last.then_inc(k_ready, 1)
                if live(t, 3):
                    act.wait_ge(t_done, t - 2)
                    wait(act, o_done, t - 4)
                    nc.scalar.activation(pT[1 - p][:, :, :].rearrange("p a b -> p (a b)"), ps_t[:, :], ACT.Copy)\
                        .then_inc(pT_ready, 1)
                if live(t, 2) and p == 0:
                    wait(act, vw_done, b * 2 - 2)
                    for half in range(2):
                        rows = slice(64 * half, 64 * half + 64)
                        last = nc.scalar.activation(vbd[rows, :, half, :], vT_all[rows, :, ds(b - 1, KEYS)], ACT.Copy)
                    last.then_inc(v_ready, 1)
                if live(t, 1):
                    act.wait_ge(sub_done, t)
                    flat = sm[(r - 1) % 4][:, :, :].rearrange("p a b -> p (a b)")
                    nc.scalar.activation(flat, flat, ACT.Exp, scale=scale).then_inc(exp_done, 1)
                if live(t, 2):
                    act.wait_ge(vw_done, b * 2 - 1 + p)
                    wait(act, o_done, t - 4 - p)
                    nc.scalar.activation(vw[((r - 2) % 4) // 2][:, 4 * p:4 * p + 4, :].rearrange("p a b -> p (a b)"),
                                         ps_v[:, :], ACT.Copy).then_inc(vw_ready, 1)

            rotate(act, step)

        @block.vector
        def _(dve):
            def step(t, r, b):
                p = r % 2
                if live(t, 0):
                    dve.wait_ge(q_done, t + 1)
                    wait(dve, s_done, t - 1)
                    nc.vector.tensor_tensor(qT[p][:, :, :], ps_q[:, :].rearrange("p (j q) -> p j q", q=P),
                                            w["bq"][:, :].unsqueeze(2).broadcast_to([P, 8, P]), ALU.add)\
                        .then_inc(qT_ready, 1)
                if live(t, 2):
                    dve.wait_ge(exp_done, t - 1)
                    wait(dve, p_ready, t - 3)
                    nc.vector.reduce_sum(den[p][:, :], sm[(r - 2) % 4][:, :, :], X)
                    dve.drain()
                    nc.vector.reciprocal(den[p][:, :], den[p][:, :]).then_inc(den_ready, 1)
                if live(t, 1):
                    dve.wait_ge(s_done, t)
                    wait(dve, t_done, t - 4)
                    s3 = ps_s[:, :].rearrange("p (h k) -> p h k", k=KEYS)
                    nc.vector.tensor_reduce(mx[1 - p][:, :], s3, X, ALU.max)
                    dve.drain()
                    nc.vector.tensor_tensor(sm[(r - 1) % 4][:, :, :], s3,
                                            mx[1 - p][:, :].unsqueeze(2).broadcast_to([P, HEADS, KEYS]), ALU.subtract)\
                        .then_inc(sub_done, 1)
                if live(t, 4):
                    dve.wait_ge(o_done, t - 3)
                    dve.wait_ge(bias_added, t - 3)
                    row = x[:, bass.ds(t - 4, 1), :].rearrange("p a b -> p (a b)")
                    nc.vector.tensor_tensor(row, row, ps_o[:, 0:D], ALU.add).then_inc(x_done, 1)

            rotate(dve, step)



HG = 4
ROWS = 3 * HG * HD


def project_self(nc, tag, w, zT, ident, q_all, k_all, v_all, eps_tile):
    HALF = TILES // 2
    with ExitStack() as stack:
        m = Memory(nc, stack, tag)
        qk = m.sb("qk", [P, TILES, 2 * D])
        thrice = [m.sb(f"thrice{i}", [P, 2 * HEADS // HG, 3, HG * HD]) for i in range(3)]
        sq = [m.sb(f"sq{i}", [P, 2 * D]) for i in range(2)]
        ms = m.sb("ms", [P, TILES, 2 * HEADS])
        ps_p = [m.ps(f"ps_p{i}") for i in range(2)]
        ps_t = {n: [m.ps(f"ps_{n}{i}") for i in range(2)] for n in "qk"}
        (p_done, sq_ready, ms_ready, root_ready, inverse_ready, n_ready, t_done, high_ready, low_ready) = (
            m.sem(n) for n in ("p_done", "sq_ready", "ms_ready", "root_ready", "inverse_ready", "n_ready", "t_done",
                               "high_ready", "low_ready"))
        block = stack.enter_context(nc.Block())
        halves = [range(h * HALF, (h + 1) * HALF) for h in range(2)]
        flat = lambda half: ms[:, half.start:half.stop, :].rearrange("p a b -> p (a b)")
        low_rows = {"q": slice(64, 96), "k": slice(32, 64)}
        out_of = {"q": q_all, "k": k_all}

        @block.tensor
        def _(pe):
            def project(t):
                if t >= 2:
                    pe.wait_ge(ms_ready, t - 1)
                nc.tensor.matmul(ps_p[t % 2][:, 0:3 * D], zT[:, t * P:(t + 1) * P], w["wqkv"][:, :],
                                 start=True, stop=True).then_inc(p_done, 1)

            def turn(t):
                pe.wait_ge(n_ready, t + 1)
                if t >= 2:
                    pe.wait_ge(low_ready, t - 1)
                for i, n in enumerate("qk"):
                    for g in range(HEADS // HG):
                        last = nc.tensor.transpose(ps_t[n][t % 2][0:ROWS, g * P:(g + 1) * P],
                                                   thrice[t % 3][:, i * HEADS // HG + g, :, :]
                                                   .rearrange("p a b -> p (a b)"), ident)
                last.then_inc(t_done, 1)

            for t in range(HALF):
                project(t)
            for t in range(HALF):
                project(t + HALF)
                turn(t)
            for t in halves[1]:
                turn(t)

        @block.scalar
        def _(act):
            def squares(t):
                act.wait_ge(p_done, t + 1)
                if t >= 2:
                    act.wait_ge(ms_ready, t - 1)
                nc.scalar.activation(v_all[:, t, :], ps_p[t % 2][:, 2 * D:3 * D], ACT.Copy)
                nc.scalar.activation(sq[t % 2][:, :], ps_p[t % 2][:, 0:2 * D], ACT.Square).then_inc(sq_ready, 1)

            def roots(h):
                act.wait_ge(ms_ready, (h + 1) * HALF)
                nc.scalar.activation(flat(halves[h]), flat(halves[h]), ACT.Sqrt, bias=eps_tile, scale=1.0 / HD)\
                    .then_inc(root_ready, 1)

            def high(t):
                act.wait_ge(t_done, t + 1)
                for n in "qk":
                    last = nc.scalar.activation(out_of[n][:, t, :, :].rearrange("p g c -> p (g c)"),
                                                ps_t[n][t % 2][0:ROWS, :], ACT.Copy, scale=w[n + "n"][:, 0:1])
                last.then_inc(high_ready, 1)

            for t in range(HALF):
                squares(t)
            roots(0)
            for t in range(HALF):
                squares(t + HALF)
                high(t)
            roots(1)
            for t in halves[1]:
                high(t)

        @block.gpsimd
        def _(pool):
            for h in range(2):
                pool.wait_ge(inverse_ready, h + 1)
                for t in halves[h]:
                    if t >= 3:
                        pool.wait_ge(t_done, t - 2)
                    groups = lambda ap: ap.rearrange("p (g h) d -> p g h d", h=HG)
                    tile = groups(qk[:, t, :].rearrange("p (h d) -> p h d", d=HD))
                    scale = groups(ms[:, t, :].unsqueeze(2).broadcast_to([P, 2 * HEADS, HD]))
                    for i in range(3):
                        last = nc.gpsimd.tensor_tensor(thrice[t % 3][:, :, i, :].rearrange("p g (h d) -> p g h d", d=HD),
                                                       tile, scale, ALU.mult)
                    last.then_inc(n_ready, 1)

        @block.vector
        def _(dve):
            def mean_squares(t):
                dve.wait_ge(sq_ready, t + 1)
                nc.vector.tensor_copy(qk[:, t, :], ps_p[t % 2][:, 0:2 * D])
                nc.vector.reduce_sum(ms[:, t, :], sq[t % 2][:, :].rearrange("p (h d) -> p h d", d=HD), X)\
                    .then_inc(ms_ready, 1)

            def inverses(h):
                dve.wait_ge(root_ready, h + 1)
                nc.vector.reciprocal(flat(halves[h]), flat(halves[h])).then_inc(inverse_ready, 1)

            def low(t):
                dve.wait_ge(high_ready, t + 1)
                for n in "qk":
                    r = low_rows[n]
                    part = out_of[n][r, t, :, :].rearrange("p g c -> p (g c)")
                    last = nc.vector.scalar_tensor_tensor(out=part, in0=ps_t[n][t % 2][r, :], scalar=w[n + "n"][r, 0:1],
                                                          in1=part, op0=ALU.mult, op1=ALU.subtract)
                last.then_inc(low_ready, 1)

            for t in range(HALF):
                mean_squares(t)
            inverses(0)
            for t in range(HALF):
                mean_squares(t + HALF)
                low(t)
            inverses(1)
            for t in halves[1]:
                low(t)


def attend_self(nc, tag, x2, w, q_all, k_all, v_all, ident, groupmask, causal, ident_b):
    scale = float(HD) ** -0.5
    NA = 8 * HD + 8
    CH = 12
    with ExitStack() as stack:
        m = Memory(nc, stack, tag)
        qs = [m.sb(f"qs{i}", [ROWS, HEADS // HG, P], F32R) for i in range(2)]
        keys = m.sb("keys", [ROWS, TPB, HEADS // HG, P])
        kbd = m.sb("kbd", [ROWS, HEADS, S], F32R)
        vaug = [m.sb(f"vaug{i}", [P, 2, 8 * (NA + HD)]) for i in range(2)]
        sm = [m.sb(f"sm{i}", [P, 512]) for i in range(3)]
        mx = [m.sb(f"mx{i}", [P, 4]) for i in range(2)]
        pT = [m.sb(f"pT{i}", [P, 4, P]) for i in range(2)]
        rden = m.sb("rden", [P, 2, 8])
        on = m.sb("on", [P, D])
        onT = m.sb("onT", [P, P])
        ps_s = [m.ps(f"ps_s{i}") for i in range(2)]
        ps_t = [m.ps(f"ps_t{i}") for i in range(2)]
        ps_o = [m.ps(f"ps_o{i}") for i in range(2)]
        ps_w = m.ps("ps_w")
        pool_zeroed, keys_loaded, q_loaded = m.sem("pool_zeroed"), m.sem("keys_loaded"), [m.sem(f"q_loaded{i}") for i in range(2)]
        (zeroed, k_ready, far_ready, v_ready, s_done, sub_done, p_ready, t_done, pT_ready, pv_done, on_ready,
         ot_done, onT_ready, w_done, x_done) = (m.sem(n) for n in (
             "zeroed", "k_ready", "far_ready", "v_ready", "s_done", "sub_done", "p_ready", "t_done", "pT_ready",
             "pv_done", "on_ready", "ot_done", "onT_ready", "w_done", "x_done"))
        block = stack.enter_context(nc.Block())

        def rotate_chunks(eng, step, lags):
            for r in range(CH):
                step(r, r, 0)
            with eng.Fori(1, B) as b:
                for r in range(CH):
                    step(b * CH + r, r, b)
            for r in range(lags):
                step(B * CH + r, r, B)

        def alive(n, lag):
            return not isinstance(n, int) or 0 <= n - lag < B * CH

        def blocks(r):
            if r < 4:
                return [(4 * r + i, 0, 128 * i) for i in range(4)]
            return [(2 * (r - 4) + i // 2, i % 2, 128 * i) for i in range(4)]

        NORMALISE = {7: 0, 15: 1}
        TURN = {8: 0, 16: 1}
        PROJECT = {10: 0, 18: 1}
        ADD = {11: 0, 19: 1}

        def finishing(table, r, b):
            for at, par in table.items():
                if at == r and not (isinstance(b, int) and b >= B):
                    return par, b * 2 + par
                if at == r + CH and not (isinstance(b, int) and b == 0):
                    return par, (b - 1) * 2 + par
            return None

        @block.sync
        def _(sp):
            def copies(b):
                def queries(par):
                    sp.dma_start(qs[par][:, :, :].bitcast(F32), q_all[:, bass.ds(b * 2 + par, 1), :, :]
                                 .rearrange("p a g c -> p (a g) c").bitcast(F32)).then_inc(q_loaded[par], 16)

                wait(sp, s_done, b * CH - CH + 4)
                queries(0)
                sp.dma_start(keys[:, :, :, :], k_all[:, ds(b, TPB), :, :].bitcast(F32)).then_inc(keys_loaded, 16)
                wait(sp, s_done, b * CH)
                queries(1)

            copies(0)
            with sp.Fori(1, B) as b:
                copies(b)

        def spread(eng, g, kb):
            return eng.tensor_tensor(kbd[:, HG * g:HG * (g + 1), kb * P:(kb + 1) * P],
                                     keys[:, kb, g, :].unsqueeze(1).broadcast_to([ROWS, HG, P]),
                                     groupmask.unsqueeze(2).broadcast_to([ROWS, HG, P]), ALU.mult)

        @block.gpsimd
        def _(pool):
            def fill(b):
                pool.wait_ge(keys_loaded, b * 16 + 16)
                for g in range(4):
                    wait(pool, s_done, b * CH - CH + 6 + 2 * g)
                    for kb in range(1 if isinstance(b, int) else TPB):
                        last = spread(nc.gpsimd, g, kb)
                    last.then_inc(k_ready, 1)
                if isinstance(b, int):
                    pool.wait_ge(zeroed, 1)
                wait(pool, pv_done, b * CH)
                for kb in range(2):
                    out = vaug[kb][:, :, :].rearrange("p a (h c) -> p (a h) c", c=NA + HD)[:, :, 0:HD]
                    src = v_all[:, bass.ds(b * 2 + kb, 1), :].rearrange("p a (h d) -> p (a h) d", d=HD)
                    nc.gpsimd.tensor_copy(out, src).then_inc(v_ready, 1)

            nc.gpsimd.memset(vaug[1][:, :, :], 0.0).then_inc(pool_zeroed, 1)
            fill(0)
            with pool.Fori(1, B) as b:
                fill(b)

        @block.tensor
        def _(pe):
            def step(n, r, b):
                if alive(n, 0):
                    if r in (0, 4):
                        pe.wait_ge(q_loaded[r // 4], b * 16 + 16)
                    if r < 4:
                        pe.wait_ge(k_ready, b * 4 + r + 1)
                    if r == 4 and isinstance(b, int):
                        pe.wait_ge(far_ready, 1)
                    wait(pe, sub_done, n - 1)
                    out = ps_s[r % 2]
                    if r < 4:
                        keys = kbd[:, 4 * r:4 * r + 4, 0:P]
                        out3 = out[:, :].rearrange("p (h k) -> p h k", k=P)
                        diag, heads = out3, 4
                    else:
                        keys = kbd[:, 2 * (r - 4):2 * (r - 4) + 2, :]
                        out3 = out[:, :].rearrange("p (h k) -> p h k", k=S)
                        diag, heads = out3[:, :, P:S], 2
                    group = r if r < 4 else (r - 4) // 2
                    nc.tensor.matmul(out3, qs[0 if r < 4 else 1][:, group, :], keys, start=True, stop=False)
                    nc.tensor.matmul(diag, ident_b, causal.unsqueeze(1).broadcast_to([P, heads, P]),
                                     start=False, stop=True).then_inc(s_done, 1)
                if alive(n, 2):
                    pe.wait_ge(p_ready, n - 1)
                    wait(pe, pT_ready, n - 3)
                    for i in range(4):
                        last = nc.tensor.transpose(ps_t[r % 2][:, i * P:(i + 1) * P],
                                                   sm[(r + 1) % 3][:, i * P:(i + 1) * P], ident)
                    last.then_inc(t_done, 1)
                if alive(n, 3):
                    pe.wait_ge(pT_ready, n - 2)
                    c = (r - 3) % CH
                    par = 0 if c < 4 else 1
                    if c in (0, 4):
                        pe.wait_ge(v_ready, b * 2 + par + 1)
                        wait(pe, on_ready, b * 2 + par - 1)
                    for i, (h, kb, col) in enumerate(blocks(c)):
                        a, own = h // 8, h % 8
                        last = nc.tensor.matmul(ps_o[par][:, a * NA:(a + 1) * NA], pT[(r - 3) % 2][:, i, :],
                                                vaug[kb][:, a, own * NA:(own + 1) * NA],
                                                start=own == 0 and kb == 0, stop=own == 7 and kb == par)
                    last.then_inc(pv_done, 1)
                if found := finishing(TURN, r, b):
                    par, tile = found
                    pe.wait_ge(on_ready, tile + 1)
                    wait(pe, x_done, tile)
                    nc.tensor.transpose(ps_w[:, 0:P], on[:, :], ident).then_inc(ot_done, 1)
                if found := finishing(PROJECT, r, b):
                    par, tile = found
                    pe.wait_ge(onT_ready, tile + 1)
                    nc.tensor.matmul(ps_w[:, P:2 * P], onT[:, :], w["wo"][:, :], start=True, stop=True)\
                        .then_inc(w_done, 1)

            rotate_chunks(pe, step, 8)

        @block.scalar
        def _(act):
            def step(n, r, b):
                if alive(n, 2):
                    act.wait_ge(t_done, n - 1)
                    wait(act, pv_done, n - 3)
                    nc.scalar.activation(pT[r % 2][:, :, :].rearrange("p a b -> p (a b)"), ps_t[r % 2][:, :],
                                         ACT.Copy).then_inc(pT_ready, 1)
                if alive(n, 0):
                    act.wait_ge(sub_done, n + 1)
                    nc.scalar.activation(sm[r % 3][:, :], sm[r % 3][:, :], ACT.Exp, scale=scale).then_inc(p_ready, 1)
                if found := finishing(TURN, r, b):
                    par, tile = found
                    act.wait_ge(ot_done, tile + 1)
                    wait(act, w_done, tile)
                    nc.scalar.activation(onT[:, :], ps_w[:, 0:P], ACT.Copy).then_inc(onT_ready, 1)

            rotate_chunks(act, step, 8)

        @block.vector
        def _(dve):
            nc.vector.memset(vaug[0][:, :, :], 0.0)
            dve.wait_ge(pool_zeroed, 1)
            dve.drain()
            for kb in range(2):
                ones = vaug[kb][:, :, 0:8 * (NA + 1)].rearrange("p a (h c) -> p a h c", c=NA + 1)
                last = nc.vector.memset(ones[:, :, :, 8 * HD:8 * HD + 1], 1.0)
            last.then_inc(zeroed, 1)
            dve.wait_ge(keys_loaded, 16)
            for g in range(4):
                last = spread(nc.vector, g, 1)
            last.then_inc(far_ready, 1)

            def step(n, r, b):
                if alive(n, 0):
                    heads = 4 if r < 4 else 2
                    dve.wait_ge(s_done, n + 1)
                    wait(dve, t_done, n - 2)
                    s3 = ps_s[r % 2][:, :].rearrange("p (h k) -> p h k", h=heads)
                    nc.vector.tensor_reduce(mx[r % 2][:, 0:heads], s3, X, ALU.max)
                    dve.drain()
                    nc.vector.tensor_tensor(sm[r % 3][:, :].rearrange("p (h k) -> p h k", h=heads), s3,
                                            mx[r % 2][:, 0:heads].unsqueeze(2).broadcast_to([P, heads, 512 // heads]),
                                            ALU.subtract).then_inc(sub_done, 1)
                if found := finishing(NORMALISE, r, b):
                    par, tile = found
                    dve.wait_ge(pv_done, (b if r == 7 else b - 1) * CH + (4 if par == 0 else CH))
                    wait(dve, ot_done, tile)
                    halves = ps_o[par][:, 0:2 * NA].rearrange("p (a c) -> p a c", c=NA)
                    nc.vector.reciprocal(rden[:, :, :], halves[:, :, 8 * HD:NA])
                    dve.drain()
                    nc.vector.tensor_tensor(on[:, :].rearrange("p (a h d) -> p a h d", a=2, d=HD),
                                            halves[:, :, 0:8 * HD].rearrange("p a (h d) -> p a h d", d=HD),
                                            rden[:, :, :].unsqueeze(3).broadcast_to([P, 2, 8, HD]), ALU.mult)\
                        .then_inc(on_ready, 1)
                if found := finishing(ADD, r, b):
                    par, tile = found
                    dve.wait_ge(w_done, tile + 1)
                    row = x2[:, bass.ds(tile, 1), KEEP:D].rearrange("p a b -> p (a b)")
                    nc.vector.tensor_tensor(row, row, ps_w[:, P + KEEP:2 * P], ALU.add).then_inc(x_done, 1)

            rotate_chunks(dve, step, 8)



def attend_two_way(nc, tag, x, w, zT, ctxT, ctx_nat, ident, ones, many):
    with ExitStack() as stack:
        m = Memory(nc, stack, tag)
        R = m.sb("R", [P, B * KEYS + KEYS])
        qrow = m.sb("qrow", [P, B * KEYS])
        wq_bc = m.sb("wq_bc", [P, P])
        const = m.sb("const", [P, 1])
        NS = 4
        seqs = range(NS)
        a = [m.sb(f"a{i}", [P, TPB, KEYS]) for i in seqs]
        mx = [m.sb(f"mx{i}", [P, TPB]) for i in seqs]
        rs = [m.sb(f"rs{i}", [P, TPB]) for i in seqs]
        aT = [m.sb(f"aT{i}", [KEYS, S]) for i in seqs]
        row = [m.sb(f"row{i}", [1, S]) for i in seqs]
        one = [m.sb(f"one{i}", [1, 2]) for i in seqs]
        c2q = [m.sb(f"c2q{i}", [P, S]) for i in seqs]
        prod = [m.sb(f"prod{i}", [P, S]) for i in seqs]
        tmp = [m.sb(f"tmp{i}", [P, S]) for i in seqs]
        q2c = [m.sb(f"q2c{i}", [P, 1]) for i in seqs]
        w14 = [m.sb(f"w14{i}", [P, D]) for i in seqs]
        ps_s = [m.ps(f"ps_s{i}") for i in seqs]
        ps_a = [m.ps(f"ps_a{i}") for i in seqs]
        ps_c, ps_q = ps_a, ps_s[NS - 1]
        (wq_ready, qrow_done, set_up, s_done, sub_done, exp_done, a_ready, a_turned, aT_ready,
         row_sub, row_exp, row_ready, c_done, c2q_ready, ready, o_done, x_done, bias_added) = (m.sem(n) for n in (
             "wq_ready", "qrow_done", "set_up", "s_done", "sub_done", "exp_done", "a_ready",
             "a_turned", "aT_ready", "row_sub", "row_exp", "row_ready", "c_done", "c2q_ready", "ready",
             "o_done", "x_done", "bias_added"))
        block = stack.enter_context(nc.Block())

        block.sync(many.loads)

        @block.gpsimd
        def _(pool):
            for i in range(B // NS):
                for t in range(i * NS * TPB, (i + 1) * NS * TPB):
                    last = nc.gpsimd.tensor_tensor(x[:, t, :], x[:, t, :], w["b_l"][:, :], ALU.add)
                last.then_inc(bias_added, 1)
                for piece in (2 * i, 2 * i + 1):
                    many.make_low(pool, piece)

        @block.tensor
        def _(pe):
            pe.wait_ge(wq_ready, 1)
            nc.tensor.matmul(ps_q[:, :], wq_bc[:, :], ctxT[:, :], start=True, stop=True).then_inc(qrow_done, 1)
            pe.wait_ge(set_up, 1)
            for i in range(B // NS):
                for r in seqs:
                    wait(pe, x_done, (i - 1) * NS + r + 1)
                    for j in range(TPB):
                        last = nc.tensor.matmul(ps_s[r][:, j * P:(j + 1) * P], zT[:, (i * NS + r) * S + j * P:(i * NS + r) * S + (j + 1) * P],
                                                R[:, bass.ds((i * NS + r) * KEYS, 2 * KEYS)], start=True, stop=True)
                    last.then_inc(s_done, 1)
                for r in seqs:
                    pe.wait_ge(a_ready, i * NS + r + 1)
                    for j in range(TPB):
                        nc.tensor.transpose(ps_a[r][0:1, S + j * P:S + (j + 1) * P], mx[r][:, j:j + 1], ident)
                    for j in range(TPB):
                        last = nc.tensor.transpose(ps_a[r][0:KEYS, j * P:(j + 1) * P], a[r][:, j, :], ident)
                    last.then_inc(a_turned, 1)
                for r in seqs:
                    pe.wait_ge(aT_ready, i * NS + r + 1)
                    pe.wait_ge(row_sub, i * NS + r + 1)
                    nc.tensor.matmul(ps_c[r][:, 0:S], ctx_nat[:, i * NS + r, :], aT[r][:, :], start=True, stop=True)
                    pe.wait_ge(row_ready, i * NS + r + 1)
                    nc.tensor.matmul(ps_c[r][:, S:2 * S], ones, row[r][:, :], start=True, stop=True)\
                        .then_inc(c_done, 1)
                for r in seqs:
                    pe.wait_ge(ready, i * NS + r + 1)
                    for j in range(TPB):
                        cols = slice(j * P, (j + 1) * P)
                        out = ps_s[r][:, S + j * P:S + (j + 1) * P]
                        nc.tensor.matmul(out, zT[:, (i * NS + r) * S + j * P:(i * NS + r) * S + (j + 1) * P], w14[r][:, :], start=True, stop=False)
                        nc.tensor.matmul(out, c2q[r][:, cols], w["wl"][:, 1, :], start=False, stop=False)
                        last = nc.tensor.matmul(out, prod[r][:, cols], w["wl"][:, 2, :], start=False, stop=True)
                    last.then_inc(o_done, 1)

        @block.scalar
        def _(act):
            for i in range(B // NS):
                for r in seqs:
                    act.wait_ge(sub_done, i * NS + r + 1)
                    flat = a[r][:, :, :].rearrange("p a b -> p (a b)")
                    nc.scalar.activation(flat, flat, ACT.Exp).then_inc(exp_done, 1)
                for r in seqs:
                    act.wait_ge(a_turned, i * NS + r + 1)
                    nc.scalar.activation(aT[r][:, :], ps_a[r][0:KEYS, 0:S], ACT.Copy).then_inc(aT_ready, 1)
                    act.wait_ge(row_sub, i * NS + r + 1)
                    nc.scalar.activation(row[r][:, :], row[r][:, :], ACT.Exp).then_inc(row_exp, 1)
                many.make_high(act, 2 * i + 1)
                for r in seqs:
                    act.wait_ge(c_done, i * NS + r + 1)
                    nc.scalar.activation(c2q[r][:, :], ps_c[r][:, 0:S], ACT.Copy).then_inc(c2q_ready, 1)
                if i < B // NS - 1:
                    many.make_high(act, 2 * i + 2)

        @block.vector
        def _(dve):
            nc.vector.tensor_copy(wq_bc[:, :], w["w_q"][:, 0:1].broadcast_to([P, P]))
            nc.vector.tensor_tensor(const[:, :], w["b_q"][:, 0:1], w["b_c"][:, 0:1], ALU.add).then_inc(wq_ready, 1)
            nc.vector.tensor_scalar(R[:, 0:B * KEYS], ctxT[:, :], w["w_cq"][:, 0:1], w["w_c"][:, 0:1],
                                    ALU.mult, ALU.add)
            nc.vector.memset(R[:, B * KEYS:], 0.0)
            dve.drain()
            nc.vector.tensor_tensor(const[:, :], const[:, :], w["b_cq"][:, 0:1], ALU.add)
            dve.drain()
            dve.wait_ge(qrow_done, 1)
            nc.vector.tensor_scalar(qrow[:, :], ps_q[:, :], const[:, 0:1], None, ALU.add).then_inc(set_up, 1)
            dve.drain()
            for i in range(B // NS):
                for r in seqs:
                    dve.wait_ge(s_done, i * NS + r + 1)
                    nc.vector.tensor_tensor(a[r][:, :, :],
                                            ps_s[r][:, 0:S].rearrange("p (j k) -> p j k", k=P)[:, :, 0:KEYS],
                                            qrow[:, ds(i * NS + r, KEYS)].unsqueeze(1).broadcast_to([P, TPB, KEYS]),
                                            ALU.add)
                    dve.drain()
                    nc.vector.tensor_reduce(mx[r][:, :], a[r][:, :, :], X, ALU.max)
                    dve.drain()
                    nc.vector.tensor_tensor(a[r][:, :, :], a[r][:, :, :],
                                            mx[r][:, :].unsqueeze(2).broadcast_to([P, TPB, KEYS]), ALU.subtract)\
                        .then_inc(sub_done, 1)
                for r in seqs:
                    dve.wait_ge(exp_done, i * NS + r + 1)
                    nc.vector.reduce_sum(rs[r][:, :], a[r][:, :, :], X)
                    dve.drain()
                    nc.vector.reciprocal(rs[r][:, :], rs[r][:, :])
                    dve.drain()
                    nc.vector.tensor_tensor(a[r][:, :, :], a[r][:, :, :],
                                            rs[r][:, :].unsqueeze(2).broadcast_to([P, TPB, KEYS]), ALU.mult)\
                        .then_inc(a_ready, 1)
                for r in seqs:
                    dve.wait_ge(aT_ready, i * NS + r + 1)
                    nc.vector.tensor_reduce(one[r][:, 0:1], ps_a[r][0:1, S:2 * S], X, ALU.max)
                    dve.drain()
                    nc.vector.tensor_scalar(row[r][:, :], ps_a[r][0:1, S:2 * S], one[r][:, 0:1], None, ALU.subtract)\
                        .then_inc(row_sub, 1)
                for r in seqs:
                    dve.wait_ge(row_exp, i * NS + r + 1)
                    nc.vector.reduce_sum(one[r][:, 1:2], row[r][:, :], X)
                    dve.drain()
                    nc.vector.reciprocal(one[r][:, 1:2], one[r][:, 1:2])
                    dve.drain()
                    nc.vector.tensor_scalar(row[r][:, :], row[r][:, :], one[r][:, 1:2], None, ALU.mult)\
                        .then_inc(row_ready, 1)
                for r in seqs:
                    dve.wait_ge(c2q_ready, i * NS + r + 1)
                    nc.vector.tensor_tensor(tmp[r][:, :], zT[:, ds(i * NS + r, S)], ps_c[r][:, S:2 * S], ALU.mult)
                    dve.drain()
                    nc.vector.reduce_sum(q2c[r][:, :], tmp[r][:, :], X)
                    dve.drain()
                    nc.vector.scalar_tensor_tensor(out=w14[r][:, :], in0=w["wl"][:, 3, :], scalar=q2c[r][:, 0:1],
                                                   in1=w["wl"][:, 0, :], op0=ALU.mult, op1=ALU.add)
                    nc.vector.tensor_tensor(prod[r][:, :], zT[:, ds(i * NS + r, S)], c2q[r][:, :], ALU.mult).then_inc(ready, 1)
                dve.wait_ge(bias_added, i + 1)
                for r in seqs:
                    dve.wait_ge(o_done, i * NS + r + 1)
                    xs = x[:, bass.ds((i * NS + r) * TPB, TPB), :]
                    nc.vector.tensor_tensor(xs, xs, ps_s[r][:, S:2 * S].rearrange("p (j d) -> p j d", d=D), ALU.add)\
                        .then_inc(x_done, 1)



def top2_gates(nc, m, dve, act_sem, dve_sem, L, e, G, E, rank, eps, done=None):
    sh = [P, TILES, E]
    sel, pick = m.sb("g_sel", sh), m.sb("g_pick", sh)
    rest, key = m.sb("g_rest", sh), m.sb("g_key", sh)
    mx, s1, s2 = m.sb("g_mx", [P, TILES]), m.sb("g_s1", [P, TILES]), m.sb("g_s2", [P, TILES])
    wide = lambda t: t[:, :].unsqueeze(2).broadcast_to(sh)
    ranks = rank[:, 0:E].unsqueeze(1).broadcast_to(sh)

    def first_of_max(values, out):
        nc.vector.tensor_reduce(mx[:, :], values, X, ALU.max)
        dve.drain()
        nc.vector.tensor_tensor(key[:, :, :], values, wide(mx), ALU.is_equal)
        dve.drain()
        nc.vector.tensor_tensor(key[:, :, :], key[:, :, :], ranks, ALU.mult)
        dve.drain()
        nc.vector.tensor_reduce(s1[:, :], key[:, :, :], X, ALU.max)
        dve.drain()
        nc.vector.tensor_tensor(out, key[:, :, :], wide(s1), ALU.is_equal)

    nc.vector.tensor_reduce(mx[:, :], L[:, :, :], X, ALU.max)
    dve.drain()
    nc.vector.tensor_tensor(e[:, :, :], L[:, :, :], wide(mx), ALU.subtract).then_inc(dve_sem, 1)
    dve.drain()
    first_of_max(L[:, :, :], sel[:, :, :])
    dve.drain()
    nc.vector.scalar_tensor_tensor(out=rest[:, :, :], in0=sel[:, :, :], scalar=-3.0e38, in1=L[:, :, :],
                                   op0=ALU.mult, op1=ALU.add)
    dve.drain()
    first_of_max(rest[:, :, :], pick[:, :, :])
    dve.drain()
    nc.vector.tensor_tensor(sel[:, :, :], sel[:, :, :], pick[:, :, :], ALU.add)
    dve.wait_ge(act_sem, 1)
    dve.drain()
    nc.vector.tensor_tensor(sel[:, :, :], sel[:, :, :], e[:, :, :], ALU.mult)
    nc.vector.reduce_sum(s1[:, :], e[:, :, :], X)
    dve.drain()
    nc.vector.reduce_sum(s2[:, :], sel[:, :, :], X)
    dve.drain()
    nc.vector.scalar_tensor_tensor(out=s2[:, :], in0=s1[:, :], scalar=eps, in1=s2[:, :], op0=ALU.mult, op1=ALU.add)
    dve.drain()
    nc.vector.reciprocal(s2[:, :], s2[:, :])
    dve.drain()
    last = nc.vector.tensor_tensor(G[:, :, :], sel[:, :, :], wide(s2), ALU.mult)
    if done is not None:
        last.then_inc(done, 1)
    dve.drain()



class StreamedExperts:

    NAMES = ("w1", "w3", "w2")

    def __init__(self, nc, m, zero, E, NF, w1, w3, w2):
        self.nc, self.zero, self.E, self.NF, self.src = nc, zero, E, NF, (w1, w3, w2)
        slots = lambda n, dt: [m.sb(f"{n}_{i}", [P, NF * P], dt) for i in range(2)]
        self.raw = {n: slots(n, F32) for n in self.NAMES}
        self.high = {n: slots(n + "h", F32R) for n in self.NAMES}
        self.low = {n: slots(n + "l", F32R) for n in self.NAMES}
        self.loaded = [m.sem(f"w_loaded{i}") for i in range(2)]
        self.low_made = m.sem("low_made")

    def load(self, sp, p, e):
        for name, src in zip(self.NAMES, self.src):
            sp.dma_start(self.raw[name][e][:, :], src[bass.ds(p * 2 + e, 1)].rearrange("a p n -> p (a n)"))\
                .then_inc(self.loaded[e], 16)

    def split_step(self, pool, e, i):
        name = self.NAMES[i % 3]
        raw, high, low = (w[name][e][:, :] for w in (self.raw, self.high, self.low))
        if i < 3:
            self.nc.gpsimd.tensor_tensor(high, raw, self.zero.broadcast_to([P, self.NF * P]), ALU.add)
            return
        if i == 3:
            pool.drain()
        last = self.nc.gpsimd.tensor_tensor(low, raw, high, ALU.subtract)
        if i == 5:
            last.then_inc(self.low_made, 1)

    def first_loads(self, sp):
        for e in range(2):
            self.load(sp, 0, e)

    def first_splits(self, pool):
        for e in range(2):
            pool.wait_ge(self.loaded[e], 48)
            for i in range(6):
                self.split_step(pool, e, i)


def three_passes(nc, out, lhs, rhs, start=True, stop=True):
    nc.tensor.matmul(out, lhs[1], rhs[0], start=start, stop=False, skip_group_check=True)
    nc.tensor.matmul(out, lhs[0], rhs[1], start=False, stop=False, skip_group_check=True)
    return nc.tensor.matmul(out, lhs[0], rhs[0], start=False, stop=stop, skip_group_check=True)


def experts_gated(nc, tag, x, z, L, rank, weights, ident, gates_dram, room, then_load=None):
    E, NF = weights.E, weights.NF
    U = 2 * GROUPS * NF
    K = 2 * GROUPS
    RING = 4
    LAG = max(NF, 3)


    def rotate_passes(eng, one_pass, tail):
        one_pass(0)
        with eng.Fori(1, E // 2) as p:
            one_pass(p)
        tail(E // 2)

    def there(p, u):
        return u >= 0 or not isinstance(p, int) or p > 0

    def finished(u):
        return (u - LAG) // NF if (u - LAG) % NF == NF - 1 else None

    with ExitStack() as stack:
        m = Memory(nc, stack, tag)
        s = [m.sb(f"s{i}", [P, 512]) for i in range(2)]
        h = [m.sb(f"h{i}", [P, 512]) for i in range(RING)]
        h_high = [m.sb(f"h_high{i}", [P, NF, 512], F32R) for i in range(2)]
        h_low = [m.sb(f"h_low{i}", [P, NF, 512], F32R) for i in range(2)]
        G = m.sb("G", [P, TILES, E])
        turned_gates = m.sb("turned_gates", [E, TILES * P])
        gate = [m.sb(f"gate{i}", [P, 512]) for i in range(GROUPS)]
        scaled = [m.sb(f"scaled{i}", [P, 512]) for i in range(2)]
        e_gates = m.sb("e_gates", [P, TILES, E])
        ps_a = [m.ps(f"ps_a{i}") for i in range(2)]
        ps_b = [m.ps(f"ps_b{i}") for i in range(2)]
        ps_y = [m.ps(f"ps_y{i}") for i in range(2)]
        ps_t = [m.ps(f"ps_t{i}") for i in range(2)]
        logits_shifted, gates_exp = m.sem("logits_shifted"), m.sem("gates_exp")
        gate_loaded = [m.sem(f"gate_loaded{i}") for i in range(GROUPS)]
        (gates_ready, gates_turned, gates_out, gates_stored, up_done, s_ready, h_ready, high_ready, low_even, low_odd,
         down_done, scale_done, summed, turned_back, x_done) = (m.sem(n) for n in (
             "gates_ready", "gates_turned", "gates_out", "gates_stored", "up_done", "s_ready", "h_ready",
             "high_ready", "low_even", "low_odd", "down_done", "scale_done", "summed", "turned_back",
             "x_done"))
        block = stack.enter_context(nc.Block())

        def wait_low(eng, p, u):
            eng.wait_ge(low_even if u % 2 == 0 else low_odd, p * (U // 2) + u // 2 + 1)

        def low_part(engine, u):
            k, f = u // NF, u % NF
            return engine.tensor_tensor(h_low[k % 2][:, f, :], h[u % RING][:, :], h_high[k % 2][:, f, :], ALU.subtract)

        @block.sync
        def _(sp):
            def fetch_gate(p, k):
                src = gates_dram[bass.ds(p * 2 + k // GROUPS, 1), k % GROUPS * 512:(k % GROUPS + 1) * 512]
                sp.dma_start(gate[k % GROUPS][:, :], src.partition_broadcast(P)).then_inc(gate_loaded[k % GROUPS], 16)

            def one_pass(p, more):
                for k in range(GROUPS):
                    if not isinstance(p, int) or p > 0:
                        sp.wait_ge(scale_done, p * K + k - GROUPS + 1)
                    fetch_gate(p, k)
                for e in range(2 if more else 0):
                    sp.wait_ge(weights.low_made, p * 2 + 1 + e)
                    weights.load(sp, p + 1, e)
                for k in range(GROUPS, K):
                    sp.wait_ge(scale_done, p * K + k - GROUPS + 1)
                    fetch_gate(p, k)

            sp.wait_ge(gates_stored, 16)
            one_pass(0, True)
            with sp.Fori(1, E // 2 - 1) as p:
                one_pass(p, True)
            one_pass(E // 2 - 1, False)
            if then_load is not None:
                then_load(sp)

        @block.gpsimd
        def _(pool):
            steps = 6 // (3 * NF // 2)

            def add(p, k):
                pool.wait_ge(scale_done, p * K + k + 1)
                cols = slice(k % GROUPS * 512, (k % GROUPS + 1) * 512)
                nc.gpsimd.tensor_tensor(room[:, cols], room[:, cols], scaled[k % 2][:, :], ALU.add).then_inc(summed, 1)

            def one_pass(p, second, next_first):
                for u in range(1, U, 2):
                    k, f = u // NF, u % NF
                    for e, wanted, at in ((1, second, 0), (0, next_first, GROUPS)):
                        if not wanted or not at <= k < at + 3:
                            continue
                        if k == at and f == 1:
                            pool.wait_ge(weights.loaded[e], p * 48 + (48 if e == 1 else 96))
                            pool.wait_ge(down_done, p * K + (0 if e == 1 else GROUPS))
                        for i in range(steps):
                            weights.split_step(pool, e, ((k - at) * NF // 2 + f // 2) * steps + i)
                    pool.wait_ge(high_ready, p * U + u + 1)
                    low_part(nc.gpsimd, u).then_inc(low_odd, 1)
                    for v in (u - 1, u):
                        if finished(v) is not None and there(p, finished(v)):
                            add(p, finished(v))

            nc.gpsimd.memset(room[:, :], 0.0)
            one_pass(0, False, True)
            with pool.Fori(1, E // 2 - 1) as p:
                one_pass(p, True, True)
            one_pass(E // 2 - 1, True, False)
            for u in range(LAG):
                if finished(u) is not None:
                    add(E // 2, finished(u))

        @block.tensor
        def _(pe):
            def turn_gates():
                pe.wait_ge(gates_ready, 1)
                for g in range(GROUPS):
                    if g >= 2:
                        pe.wait_ge(gates_out, g - 1)
                    for j in range(GROUP):
                        last = nc.tensor.transpose(ps_t[g % 2][0:E, j * P:(j + 1) * P], G[:, g * GROUP + j, :], ident)
                    last.then_inc(gates_turned, 1)

            def down(p, u):
                k, f = u // NF, u % NF
                if f == 0 and there(p, k - 2):
                    pe.wait_ge(scale_done, p * K + k - 1)
                wait_low(pe, p, u)
                lhs = [w["w2"][k // GROUPS % 2][:, f * D:(f + 1) * D] for w in (weights.high, weights.low)]
                rhs = [part[k % 2][:, f, :] for part in (h_high, h_low)]
                last = three_passes(nc, ps_y[k % 2][:, :], lhs, rhs, f == 0, f == NF - 1)
                if f == NF - 1:
                    last.then_inc(down_done, 1)

            def one_pass(p):
                for u in range(U):
                    k, f = u // NF, u % NF
                    e, g = k // GROUPS, k % GROUPS
                    if g == 0 and f == 0:
                        pe.wait_ge(weights.low_made, p * 2 + e + 1)
                    if isinstance(p, int) and u == 2:
                        turn_gates()
                    if there(p, u - 2):
                        pe.wait_ge(h_ready, p * U + u - 1)
                    rhs = [part[:, g * 512:(g + 1) * 512] for part in z]
                    for bank, name in ((ps_a[u % 2], "w1"), (ps_b[u % 2], "w3")):
                        lhs = [part[name][e][:, f * P:(f + 1) * P] for part in (weights.high, weights.low)]
                        three_passes(nc, bank[:, :], lhs, rhs).then_inc(up_done, 1)
                    if there(p, u - LAG):
                        down(p, u - LAG)

            def tail(p):
                for u in range(LAG):
                    down(p, u - LAG)

            rotate_passes(pe, one_pass, tail)
            pe.wait_ge(summed, E // 2 * K)
            for g in range(GROUPS):
                if g >= 2:
                    pe.wait_ge(x_done, g - 1)
                for j in range(GROUP):
                    t = g * GROUP + j
                    last = nc.tensor.transpose(ps_t[g % 2][:, j * P:(j + 1) * P], room[:, t * P:(t + 1) * P], ident)
                last.then_inc(turned_back, 1)

        @block.scalar
        def _(act):
            act.wait_ge(logits_shifted, 1)
            e_flat = e_gates[:, :, :].rearrange("p a b -> p (a b)")
            nc.scalar.activation(e_flat, e_flat, ACT.Exp).then_inc(gates_exp, 1)

            def store_gates():
                for g in range(GROUPS):
                    act.wait_ge(gates_turned, g + 1)
                    nc.scalar.activation(turned_gates[:, g * 512:(g + 1) * 512], ps_t[g % 2][0:E, :], ACT.Copy)\
                        .then_inc(gates_out, 1)
                act.wait_ge(gates_out, GROUPS)
                act.dma_start(gates_dram[0:E, :], turned_gates[:, :]).then_inc(gates_stored, 16)

            def high(p, u):
                k, f = u // NF, u % NF
                act.wait_ge(h_ready, p * U + u + 1)
                if f == 0 and there(p, k - 2):
                    act.wait_ge(down_done, p * K + k - 1)
                nc.scalar.activation(h_high[k % 2][:, f, :], h[u % RING][:, :], ACT.Copy).then_inc(high_ready, 1)

            def one_pass(p):
                for u in range(U):
                    act.wait_ge(up_done, p * 2 * U + 2 * u + 1)
                    if there(p, u - 2):
                        act.wait_ge(h_ready, p * U + u - 1)
                    nc.scalar.activation(s[u % 2][:, :], ps_a[u % 2][:, :], ACT.Silu).then_inc(s_ready, 1)
                    if isinstance(p, int) and u == 1:
                        store_gates()
                    if there(p, u - 1):
                        high(p, u - 1)

            rotate_passes(act, one_pass, lambda p: high(p, -1))

        @block.vector
        def _(dve):
            top2_gates(nc, m, dve, gates_exp, logits_shifted, L, e_gates, G, E, rank, 0.0, gates_ready)

            def scale(p, k):
                dve.wait_ge(down_done, p * K + k + 1)
                dve.wait_ge(gate_loaded[k % GROUPS], p * 32 + k // GROUPS * 16 + 16)
                if there(p, k - 2):
                    dve.wait_ge(summed, p * K + k - 1)
                nc.vector.tensor_tensor(scaled[k % 2][:, :], ps_y[k % 2][:, :], gate[k % GROUPS][:, :], ALU.mult)\
                    .then_inc(scale_done, 1)

            def one_pass(p):
                for u in range(U):
                    dve.wait_ge(s_ready, p * U + u + 1)
                    dve.wait_ge(up_done, p * 2 * U + 2 * u + 2)
                    if there(p, u - RING):
                        wait_low(dve, p, u - RING)
                    nc.vector.tensor_tensor(h[u % RING][:, :], s[u % 2][:, :], ps_b[u % 2][:, :], ALU.mult)\
                        .then_inc(h_ready, 1)
                    if u % 2 == 1:
                        dve.wait_ge(high_ready, p * U + u)
                        low_part(nc.vector, u - 1).then_inc(low_even, 1)
                    if finished(u) is not None and there(p, finished(u)):
                        scale(p, finished(u))

            def tail(p):
                for u in range(LAG):
                    if finished(u) is not None:
                        scale(p, finished(u))

            rotate_passes(dve, one_pass, tail)
            for g in range(GROUPS):
                dve.wait_ge(turned_back, g + 1)
                rows = x[:, g * GROUP:(g + 1) * GROUP, :].rearrange("p a b -> p (a b)")
                nc.vector.tensor_tensor(rows, rows, ps_t[g % 2][:, :], ALU.add).then_inc(x_done, 1)



def experts_mixed(nc, tag, x, x2, w, zT, L, rank):
    HID = ("a0", "a1", "u0", "u1", "b0", "b1", "g0", "v0", "g1", "v1", "c0", "c1", "d0", "p0", "p1")
    ORDER = HID[:13] + ("y0", "p0", "p1", "y1", "y2", "y3")
    ACT_OPS = ("a0", "a1", "u0", "u1", "b0", "b1", "g0", "g1", "c0", "c1", "d0", "p0", "p1")
    NB = 5
    DOWN = {"y0": (("u0", "u1"), "e0_down", 0), "y1": (("m0", "m1"), "e1_down", 1),
            "y2": (("c0", "c1"), "e2_l4", 2), "y3": (("p0", "p1"), "e3_out", 3)}
    UP = {"a": ("e2_l1", None), "u": ("e0_up", None), "g": ("e1_w1", None), "v": ("e1_w2", None),
          "b": ("e2_l2", ("a0", "a1")), "c": ("e2_l3", ("b0", "b1")), "d": ("e3_down", None), "p": ("e3_up", ("d0",))}
    with ExitStack() as stack:
        m = Memory(nc, stack, tag)
        h = {n: m.sb("h_" + n, [P, 512]) for n in ACT_OPS + ("m0", "m1")}
        G = m.sb("G", [P, TILES, 4])
        gate_exp = m.sb("gate_exp", [P, TILES, 4])
        ps_h = [m.ps(f"ps_h{i}") for i in range(NB)]
        ps_y = [m.ps(f"ps_y{i}") for i in range(2)]
        logits_shifted, gates_exp = m.sem("logits_shifted"), m.sem("gates_exp")
        block_done, act_done, gated_done, down_done, added = (m.sem(n) for n in (
            "block_done", "act_done", "gated_done", "down_done", "added"))
        block = stack.enter_context(nc.Block())
        bank = {n: ps_h[i % NB] for i, n in enumerate(HID)}

        def wait_for(eng, names, g):
            gated = [int(n[1]) + 1 for n in names if n[0] == "m"]
            acts = [ACT_OPS.index(n) + 1 for n in names if n[0] != "m"]
            if gated:
                eng.wait_ge(gated_done, g * 2 + max(gated))
            if acts:
                eng.wait_ge(act_done, g * len(ACT_OPS) + max(acts))

        def first_then_others(eng, group):
            group(0)
            with eng.Fori(1, GROUPS) as g:
                group(g)

        @block.tensor
        def _(pe):
            def group(g):
                for name in ORDER:
                    if name in DOWN:
                        inputs, wn, e = DOWN[name]
                        wait(pe, added, g * 4 + max(0, e - 1))
                        wait_for(pe, inputs, g)
                        for j in range(GROUP):
                            for i, inp in enumerate(inputs):
                                last = nc.tensor.matmul(ps_y[e % 2][:, j * D:(j + 1) * D], h[inp][:, j * P:(j + 1) * P],
                                                        w[wn][:, i, :], start=i == 0, stop=i == 1)
                        last.then_inc(down_done, 1)
                        continue
                    n = HID.index(name)
                    wn, inputs = UP[name[0]]
                    needed = list(inputs or ())
                    if n >= NB:
                        old = HID[n - NB]
                        needed.append("m" + old[1] if old[0] in "gv" else old)
                    wait_for(pe, needed, g)
                    cols = slice(int(name[1]) * P, int(name[1]) * P + P)
                    if inputs is None:
                        last = nc.tensor.matmul(bank[name][:, :], w[wn][:, 0, cols], zT[:, ds(g, 512)],
                                                start=True, stop=True)
                    else:
                        for i, inp in enumerate(inputs):
                            last = nc.tensor.matmul(bank[name][:, :], w[wn][:, i, cols], h[inp][:, :],
                                                    start=i == 0, stop=i == len(inputs) - 1)
                    last.then_inc(block_done, 1)

            first_then_others(pe, group)

        @block.scalar
        def _(act):
            act.wait_ge(logits_shifted, 1)
            e_flat = gate_exp[:, :, :].rearrange("p a b -> p (a b)")
            nc.scalar.activation(e_flat, e_flat, ACT.Exp).then_inc(gates_exp, 1)
            def group(g):
                for name in ACT_OPS:
                    act.wait_ge(block_done, g * len(HID) + HID.index(name) + 1)
                    gate = name[0] == "g"
                    nc.scalar.activation(h[name][:, :], bank[name][:, :], ACT.Tanh if gate else ACT.Gelu,
                                         scale=0.5 if gate else 1.0).then_inc(act_done, 1)

            first_then_others(act, group)

        @block.vector
        def _(dve):
            top2_gates(nc, m, dve, gates_exp, logits_shifted, L, gate_exp, G, 4, rank, 1.0e-8)
            def group(g):
                for k in range(2):
                    wait_for(dve, (f"g{k}",), g)
                    tanh, out = h[f"g{k}"][:, :], h[f"m{k}"][:, :]
                    nc.vector.scalar_tensor_tensor(out=tanh, in0=tanh, scalar=1.0, in1=bank[f"g{k}"][:, :],
                                                   op0=ALU.add, op1=ALU.mult)
                    dve.drain()
                    dve.wait_ge(block_done, g * len(HID) + HID.index(f"v{k}") + 1)
                    nc.vector.scalar_tensor_tensor(out=out, in0=tanh, scalar=0.5, in1=bank[f"v{k}"][:, :],
                                                   op0=ALU.mult, op1=ALU.mult).then_inc(gated_done, 1)
                for e in range(4):
                    dve.wait_ge(down_done, g * 4 + e + 1)
                    for j in range(GROUP):
                        row = x2[:, bass.ds(g * GROUP + j, 1), KEEP:D].rearrange("p a b -> p (a b)")
                        last = nc.vector.scalar_tensor_tensor(
                            out=row, in0=ps_y[e % 2][:, j * D + KEEP:(j + 1) * D],
                            scalar=G[:, bass.ds(g * GROUP + j, 1), e], in1=row, op0=ALU.mult, op1=ALU.add)
                    last.then_inc(added, 1)
                    dve.drain()

            first_then_others(dve, group)
            nc.vector.tensor_tensor(x[:, :, :], x[:, :, :], x2[:, :, :], ALU.add)



class ManyExperts:

    PIECES = 4

    def __init__(self, nc, m, cols, eg, eu, ed):
        self.nc, self.src = nc, (eg, eu, ed)
        self.piece = cols // self.PIECES
        self.raw = [m.sb(n + "_raw", [P, self.piece]) for n in ("eg", "eu", "ed")]
        self.loaded, self.high_made, self.low_made = (m.sem(n) for n in ("loaded", "high_made", "low_made"))

    def make_room(self, m):
        self.gate, self.up, self.down = self.parts = [
            [m.sb(n + part, [P, self.piece * self.PIECES], F32R) for part in ("_high", "_low")]
            for n in ("eg", "eu", "ed")]

    def load_piece(self, sp, i):
        for raw, src in zip(self.raw, self.src):
            sp.dma_start(raw[:, :], src[:, bass.ds(i * self.piece, self.piece)]).then_inc(self.loaded, 16)

    def loads(self, sp):
        for i in range(1, self.PIECES):
            sp.wait_ge(self.low_made, i)
            self.load_piece(sp, i)

    def make_high(self, act, i):
        act.wait_ge(self.loaded, i * 48 + 48)
        for raw, (high, _) in zip(self.raw, self.parts):
            last = self.nc.scalar.activation(high[:, bass.ds(i * self.piece, self.piece)], raw[:, :], ACT.Copy)
        last.then_inc(self.high_made, 1)

    def make_low(self, pool, i):
        pool.wait_ge(self.high_made, i + 1)
        for raw, (high, low) in zip(self.raw, self.parts):
            cols = bass.ds(i * self.piece, self.piece)
            last = self.nc.gpsimd.tensor_tensor(low[:, cols], raw[:, :], high[:, cols], ALU.subtract)
        last.then_inc(self.low_made, 1)


def experts_many(nc, tag, x, z, L, bias, weights, ident, gates_dram, room):
    E, W, GRP = 64, 64, 8
    BLOCKS = (E * W) // P + 1
    SHARED = BLOCKS - 1
    PAIRS = E // 2
    SLOTS = 4
    SENTINEL = 3.0e38
    turned_gates = room[0:E, :]
    with ExitStack() as stack:
        m = Memory(nc, stack, tag)
        s = [m.sb(f"s{i}", [P, 512]) for i in range(3)]
        h = [m.sb(f"h{i}", [P, 512]) for i in range(3)]
        h_parts = [[m.sb(f"h_{part}{i}", [P, 512], F32R) for part in ("high", "low")] for i in range(3)]
        y = m.sb("y", [P, 512])
        gate = [m.sb(f"gate{i}", [P, 512]) for i in range(SLOTS)]
        G = m.sb("G", [P, TILES, E])
        grp = m.sb("grp", [P, TILES, 12])
        grp_rest = m.sb("grp_rest", [P, TILES, 12])
        cand, rest = (raw[:, 0:TILES * (E + 2)].rearrange("p (t e) -> p t e", e=E + 2) for raw in weights.raw[0:2])
        top = m.sb("top", [P, TILES, 8])
        den = m.sb("den", [P, TILES])
        ps_a = [m.ps(f"ps_a{i}") for i in range(3)]
        ps_b = [m.ps(f"ps_b{i}") for i in range(3)]
        ps_g = m.ps("ps_g")
        ps_y = m.ps("ps_y")
        gate_loaded = [m.sem(f"gate_loaded{i}") for i in range(SLOTS)]
        gates_stored = [m.sem(f"gates_stored{g}") for g in range(GROUPS)]
        (scores_ready, gates_ready, gates_turned, gates_out, a_done, b_done, s_ready, h_ready, g_ready, high_ready,
         low_ready, down_done, y_out, y_turned, added) = (m.sem(n) for n in (
             "scores_ready", "gates_ready", "gates_turned", "gates_out", "a_done", "b_done", "s_ready", "h_ready",
             "g_ready", "high_ready", "low_ready", "down_done", "y_out", "y_turned", "added"))
        block = stack.enter_context(nc.Block())

        def rotate_blocks(eng, step, lags):
            for c in range(BLOCKS):
                step(c, c, 0)
            with eng.Fori(1, GROUPS) as g:
                for c in range(BLOCKS):
                    step(g * BLOCKS + c, c, g)
            for c in range(lags):
                step(GROUPS * BLOCKS + c, c, GROUPS)

        def alive(n, lag):
            return not isinstance(n, int) or 0 <= n - lag < GROUPS * BLOCKS

        def ends_group(n):
            return not (isinstance(n, int) and n < BLOCKS)

        def of(c, g, lag):
            return (c - lag) % BLOCKS, g if c >= lag else g - 1

        def place(c):
            return SHARED if c == 0 else c - 1

        @block.sync
        def _(sp):
            def fetch(g, pair):
                for e in range(2):
                    src = gates_dram[2 * pair + e:2 * pair + e + 1, ds(g, 512)].partition_broadcast(W)
                    sp.dma_start(gate[pair % SLOTS][e * W:(e + 1) * W, :], src).then_inc(gate_loaded[pair % SLOTS], 16)

            def group(g):
                for pair in range(PAIRS):
                    if pair >= SLOTS or not isinstance(g, int):
                        sp.wait_ge(g_ready, g * PAIRS + pair - SLOTS + 1)
                    fetch(g, pair)

            sp.wait_ge(gates_stored[0], 16)
            group(0)
            for g in range(1, GROUPS):
                sp.wait_ge(gates_stored[g], 16)
            with sp.Fori(1, GROUPS) as g:
                group(g)

        @block.tensor
        def _(pe):
            def turn_gates():
                pe.wait_ge(gates_ready, 1)
                for g in range(GROUPS):
                    if g > 0:
                        pe.wait_ge(gates_out, g)
                    for j in range(GROUP):
                        last = nc.tensor.transpose(ps_g[0:E, j * P:(j + 1) * P], G[:, g * GROUP + j, :], ident)
                    last.then_inc(gates_turned, 1)

            def step(n, c, g):
                if alive(n, 0):
                    wait(pe, h_ready, n - 2)
                    at = place(c)
                    cols = slice(at * P, (at + 1) * P)
                    rhs = [part[:, ds(g, 512)] for part in z]
                    for bank, w, done in ((ps_a, weights.gate, a_done), (ps_b, weights.up, b_done)):
                        three_passes(nc, bank[c % 3][:, :], [part[:, cols] for part in w], rhs).then_inc(done, 1)
                if isinstance(n, int) and n == 2:
                    turn_gates()
                if alive(n, 3):
                    k, group = of(c, g, 3)
                    pe.wait_ge(low_ready, n - 2)
                    if k == 0:
                        wait(pe, y_out, group)
                    rhs = [part[:, :] for part in h_parts[k % 3]]
                    lhs = [w[:, place(k) * D:(place(k) + 1) * D] for w in weights.down]
                    three_passes(nc, ps_y[:, :], lhs, rhs, k == 0, k == BLOCKS - 1).then_inc(down_done, 1)
                if c == 4 and ends_group(n):
                    pe.wait_ge(y_out, g)
                    for j in range(GROUP):
                        last = nc.tensor.transpose(ps_g[:, j * P:(j + 1) * P], y[:, j * P:(j + 1) * P], ident)
                    last.then_inc(y_turned, 1)

            rotate_blocks(pe, step, 5)

        @block.scalar
        def _(act):
            act_in = L[:, :, :].rearrange("p a b -> p (a b)")
            nc.scalar.activation(act_in, act_in, ACT.Sigmoid).then_inc(scores_ready, 1)

            def store_gates():
                for g in range(GROUPS):
                    cols = slice(g * 512, (g + 1) * 512)
                    act.wait_ge(gates_turned, g + 1)
                    nc.scalar.activation(turned_gates[:, cols], ps_g[0:E, :], ACT.Copy).then_inc(gates_out, 1)
                    act.wait_ge(gates_out, g + 1)
                    act.dma_start(gates_dram[:, cols], turned_gates[:, cols]).then_inc(gates_stored[g], 16)

            def step(n, c, g):
                if alive(n, 0):
                    act.wait_ge(a_done, n + 1)
                    wait(act, h_ready, n - 2)
                    nc.scalar.activation(s[c % 3][:, :], ps_a[c % 3][:, :], ACT.Silu).then_inc(s_ready, 1)
                if isinstance(n, int) and n == 2:
                    store_gates()
                for lag in ((2, 1) if isinstance(n, int) and n == 2 else (1,)):
                    if alive(n, lag) and not (isinstance(n, int) and n == 1):
                        high(n, c, g, lag)

            def high(n, c, g, lag):
                k, group = of(c, g, lag)
                if k == 0:
                    act.wait_ge(h_ready, n - lag + 1)
                else:
                    act.wait_ge(g_ready, group * PAIRS + k)
                wait(act, down_done, n - lag - 2)
                nc.scalar.activation(h_parts[k % 3][0][:, :], h[k % 3][:, :], ACT.Copy).then_inc(high_ready, 1)

            rotate_blocks(act, step, 1)

        @block.gpsimd
        def _(pool):
            def step(n, c, g):
                if c == 0:
                    return
                pair = c - 1
                pool.wait_ge(gate_loaded[pair % SLOTS], (g * (PAIRS // SLOTS) + pair // SLOTS + 1) * 32)
                pool.wait_ge(h_ready, n + 1)
                nc.gpsimd.tensor_tensor(h[c % 3][:, :], h[c % 3][:, :], gate[pair % SLOTS][:, :], ALU.mult)\
                    .then_inc(g_ready, 1)

            rotate_blocks(pool, step, 0)

        @block.vector
        def _(dve):
            flat = lambda a: a.rearrange("p a b -> p (a b)")
            dve.wait_ge(scores_ready, 1)
            nc.vector.tensor_tensor(L[:, :, :], L[:, :, :], bias.unsqueeze(1).broadcast_to([P, TILES, E]), ALU.add)
            nc.vector.memset(grp[:, :, GRP:12], SENTINEL)
            nc.vector.memset(cand[:, :, E:E + 2], SENTINEL)
            dve.drain()
            nc.vector.tensor_reduce(grp[:, :, 0:GRP], L[:, :, :].rearrange("p t (g e) -> p t g e", e=GRP), X, ALU.max)
            dve.drain()
            for t in range(TILES):
                nc.vector.max(top[:, t, :], grp[:, t, :])
            dve.drain()
            for t in range(TILES):
                nc.vector.match_replace(grp_rest[:, t, :], top[:, t, :], grp[:, t, :], -SENTINEL)
            dve.drain()
            nc.vector.tensor_tensor(grp[:, :, 0:GRP], grp[:, :, 0:GRP], grp_rest[:, :, 0:GRP], ALU.not_equal)
            dve.drain()
            for t in range(TILES):
                nc.vector.tensor_tensor(cand[:, t, 0:E].rearrange("p (g e) -> p g e", e=GRP),
                                        L[:, t, :].rearrange("p (g e) -> p g e", e=GRP),
                                        grp[:, t, 0:GRP].unsqueeze(2).broadcast_to([P, GRP, GRP]), ALU.mult)
            dve.drain()
            for t in range(TILES):
                nc.vector.max(top[:, t, :], cand[:, t, :])
            dve.drain()
            for t in range(TILES):
                nc.vector.match_replace(rest[:, t, :], top[:, t, :], cand[:, t, :], -SENTINEL)
            nc.vector.reduce_sum(den[:, :], top[:, :, 2:8], X)
            dve.drain()
            nc.vector.tensor_tensor(rest[:, :, 0:E], rest[:, :, 0:E], cand[:, :, 0:E], ALU.not_equal)
            nc.vector.tensor_scalar(den[:, :], den[:, :], 1.0e-8, None, ALU.add)
            dve.drain()
            nc.vector.tensor_tensor(rest[:, :, 0:E], rest[:, :, 0:E], cand[:, :, 0:E], ALU.mult)
            nc.vector.reciprocal(den[:, :], den[:, :])
            dve.drain()
            nc.vector.tensor_tensor(G[:, :, :], rest[:, :, 0:E],
                                    den[:, :].unsqueeze(2).broadcast_to([P, TILES, E]), ALU.mult)\
                .then_inc(gates_ready, 1)

            def step(n, c, g):
                if alive(n, 0):
                    dve.wait_ge(s_ready, n + 1)
                    dve.wait_ge(b_done, n + 1)
                    wait(dve, low_ready, n - 2)
                    nc.vector.tensor_tensor(h[c % 3][:, :], s[c % 3][:, :], ps_b[c % 3][:, :], ALU.mult)\
                        .then_inc(h_ready, 1)
                if alive(n, 1):
                    k, _ = of(c, g, 1)
                    dve.wait_ge(high_ready, n)
                    nc.vector.tensor_tensor(h_parts[k % 3][1][:, :], h[k % 3][:, :], h_parts[k % 3][0][:, :],
                                            ALU.subtract).then_inc(low_ready, 1)
                if ends_group(n) and c == 2:
                    dve.wait_ge(down_done, n - 2)
                    nc.vector.tensor_copy(y[:, :], ps_y[:, :]).then_inc(y_out, 1)
                if ends_group(n) and c == 4:
                    dve.wait_ge(y_turned, g)
                    rows = x[:, bass.ds((g - 1) * GROUP, GROUP), :].rearrange("p a b -> p (a b)")
                    nc.vector.tensor_tensor(rows, rows, ps_g[:, :], ALU.add).then_inc(added, 1)

            rotate_blocks(dve, step, 5)



def arrive(nc, sem, value):
    with nc.Block() as block:
        @block.sync
        def _(sp):
            sp.wait_ge(sem, value)


def build(nc, A, out):
    with ExitStack() as top:
        m = Memory(nc, top)
        x = m.sb("x", [P, TILES, D])
        zT = m.sb("zT", [P, TILES * P])
        ident = m.sb("ident", [P, P])
        headmask = m.sb("headmask", [P, HEADS])
        rank = m.sb("rank", [P, 8])
        groupmask = m.sb("groupmask", [ROWS, HG])
        ones = m.sb("ones", [1, P])
        zero = m.sb("zero", [P, 1])
        eps = m.sb("eps", [P, 3])
        logits = {E: m.sb(f"logits{E}", [P, TILES, E]) for E in (4, 8)}
        ctxT = m.sb("ctxT", [P, B * KEYS])
        ctx2T = m.sb("ctx2T", [P, B, 2, KEYS])
        ctx_nat = m.sb("ctx_nat", [KEYS, B, D])
        small2 = {n: m.sb("L2" + n, sh) for n, sh in (
            ("wq", [P, D]), ("wk", [P, D]), ("wv", [P, D]), ("wo", [P, D]), ("bq", [P, 1]), ("bk", [P, 1]),
            ("bv", [P, D]), ("bo", [P, D]))}
        two_way = {n: m.sb("L3" + n, sh) for n, sh in (
            ("w_cq", [P, 1]), ("w_c", [P, 1]), ("w_q", [P, 1]), ("b_cq", [P, 1]), ("b_c", [P, 1]), ("b_q", [P, 1]),
            ("wl", [P, 4, D]), ("b_l", [P, D]))}
        gate2 = m.sb("gate2", [P, 8])
        gate3 = m.sb("gate3", [P, 64])
        bias3 = m.sb("bias3", [P, 64])
        x_loaded = [m.sem(f"x_loaded{g}") for g in range(GROUPS)]
        ident_loaded, first_loaded, soon_loaded, later_loaded = (m.sem(n) for n in (
            "ident_loaded", "first_loaded", "soon_loaded", "later_loaded"))
        stored = m.sem("stored")
        gates_dram = nc.dram_tensor("gates_by_expert", (64, B * S), F32).ap()
        root_ln, root_rms = (1.0, eps[:, 0:1]), (1.0, eps[:, 1:2])
        root_both = (1.0 + EPS_RMS, eps[:, 2:3])

        early = ExitStack()
        me = Memory(nc, early)
        self_w = {n: me.sb("L0f" + n, sh) for n, sh in (
            ("wqkv", [P, 3 * D]), ("wo", [P, D]), ("qn", [ROWS, 1]), ("kn", [ROWS, 1]), ("n1", [P, 1]), ("n2", [P, 1]),
            ("gate", [P, 4]), ("e0_up", [P, 1, 256]), ("e0_down", [P, 2, D]), ("e1_w1", [P, 1, 256]),
            ("e1_w2", [P, 1, 256]), ("e1_down", [P, 2, D]), ("e2_l1", [P, 1, 256]), ("e2_l2", [P, 2, 256]),
            ("e2_l3", [P, 2, 256]), ("e2_l4", [P, 2, D]), ("e3_down", [P, 1, D]), ("e3_up", [P, 1, 256]),
            ("e3_out", [P, 2, D]))}
        wide1 = {n: me.sb("L1" + n, sh) for n, sh in (
            ("wq", [P, 1024]), ("wk", [P, 1024]), ("wv", [P, 1024]), ("wo", [P, 8, D]), ("bq", [P, 8]), ("bk", [P, 8]),
            ("bv", [P, 8]), ("bo", [P, D]))}
        gate1 = me.sb("gate1", [P, 8])
        neg1 = me.sb("neg1", [P, TILES, KEYS], BF16)
        causal_b = me.sb("causal_b", [P, P], BF16)
        ident_b = me.sb("ident_b", [P, P], BF16)

        firsts = ExitStack()
        mf = Memory(nc, firsts)
        small0 = {n: mf.sb("L0" + n, sh) for n, sh in (
            ("wq", [P, D]), ("wk", [P, D]), ("wv", [P, D]), ("wo", [P, D]), ("bq", [P, 1]), ("bk", [P, 1]),
            ("bv", [P, D]), ("bo", [P, D]))}
        mask0 = mf.sb("mask0", [P, TPB, KEYS])
        mask1 = mf.sb("mask1", [P, TILES, KEYS], U8)
        causal = mf.sb("causal", [P, P])
        ctx_rows = mf.sb("ctx_rows", [P, B * KEYS // P, D])

        whole = lambda tile: tile[tuple(slice(None) for _ in tile.shape)]
        first = [(ctx_rows, A["ctx"].rearrange("(t p) d -> p t d", p=P)),
                 (headmask, A["headmask"]), (mask0, A["mask0"].rearrange("(t p) k -> p t k", p=P))]
        first += [(t, A["L0" + k]) for k, t in small0.items()]
        first += [(groupmask, A["groupmask"]), (causal, A["causal"]), (rank, A["rank"]), (mask1, A["mask1"].rearrange("(t p) k -> p t k", p=P)),
                  (ctx_nat, A["ctx"].rearrange("(b k) d -> k b d", k=KEYS))]
        soon = [(t, A["L0f" + k]) for k, t in self_w.items()] + [(t, A["L1" + k]) for k, t in wide1.items()]
        soon += [(gate1, A["gate1"])]
        later = [(t, A["L2" + k]) for k, t in small2.items()] + [(t, A["L3" + k]) for k, t in two_way.items()]
        later += [(gate2, A["gate2"]), (gate3, A["gate3"]), (bias3, A["bias3"])]

        with nc.Block() as block:
            @block.sync
            def _(sp):
                for g in range(GROUPS):
                    tiles = slice(g * GROUP, (g + 1) * GROUP)
                    sp.dma_start(x[:, tiles, :], A["x"].rearrange("(t p) d -> p t d", p=P)[:, tiles, :])\
                        .then_inc(x_loaded[g], 16)
                    if g == 0:
                        sp.dma_start(ident[:, :], A["ident"]).then_inc(ident_loaded, 16)

            @block.vector
            def _(dve):
                nc.vector.memset(eps[:, 0:1], EPS_LN)
                nc.vector.memset(eps[:, 1:2], EPS_RMS)
                nc.vector.memset(eps[:, 2:3], EPS_LN * EPS_RMS)
                nc.vector.memset(ones[:, :], 1.0)
                nc.vector.memset(zero[:, :], 0.0)

        def load(tiles, loaded):
            def program(sp):
                for tile, src in tiles:
                    sp.dma_start(whole(tile), src).then_inc(loaded, 16)
            return program

        idn, hm = ident[:, :], headmask[:, :]

        def finish():
            with nc.Block() as block:
                @block.sync
                def _(sp):
                    sp.dma_start(out.rearrange("(t p) d -> p t d", p=P), x[:, :, :]).then_inc(stored, 16)
                    sp.wait_ge(stored, 16)

        normalise(nc, "n0_", x, idn, root_ln, zT, arrived=x_loaded, ident_loaded=ident_loaded, then=ACT.Exp,
                  loads=load(first, first_loaded))
        with ExitStack() as stack:
            ms = Memory(nc, stack, "su_")
            ps_c = ms.ps("ps_c")
            turned, masked, copied = ms.sem("turned"), ms.sem("masked"), ms.sem("copied")
            block = stack.enter_context(nc.Block())

            @block.tensor
            def _(pe):
                pe.wait_ge(first_loaded, 16 * len(first))
                for i in range(B * KEYS // P):
                    last = nc.tensor.transpose(ps_c[:, i * P:(i + 1) * P], ctx_rows[:, i, :], idn)
                last.then_inc(turned, 1)

            @block.scalar
            def _(act):
                act.wait_ge(turned, 1)
                for i in range(2):
                    nc.scalar.activation(ctx2T[:, :, i, :], ps_c[:, :].rearrange("p (b k) -> p b k", k=KEYS), ACT.Copy)
                act.drain()
                nc.scalar.activation(ctxT[:, :].rearrange("p (b k) -> p b k", k=KEYS), ctx2T[:, :, 0, :], ACT.Copy)

            @block.vector
            def _(dve):
                dve.wait_ge(first_loaded, 16 * len(first))
                nc.vector.tensor_scalar(mask0[:, :, :], mask0[:, :, :], -1.0e9, None, ALU.mult)
                nc.vector.tensor_copy(ident_b[:, :], ident[:, :])
                nc.vector.tensor_scalar(causal_b[:, :], causal[:, :], BIG, -BIG, ALU.mult, ALU.add)
                nc.vector.tensor_scalar(neg1[:, :, :], mask1[:, :, :], BIG, -BIG, ALU.mult, ALU.add)

        with ExitStack() as stack:
            ml = Memory(nc, stack, "a0_")
            qT_all, kT_all, v2_all = ml.sb("qT", [P, TILES * P]), ml.sb("kT", [P, B * KEYS]), ml.sb("v2", [P, B, D])
            project_small(nc, "p0_", small0, zT, ctx2T, idn, qT_all, kT_all, v2_all)
            attend_small(nc, "t0_", x, small0, qT_all, kT_all, v2_all, idn, hm, HD ** -0.5, neg=mask0,
                         loads=load(soon, soon_loaded))
        firsts.close()
        with ExitStack() as stack:
            ml = Memory(nc, stack, "f0_")
            x2 = ml.sb("x2", [P, TILES, D])
            arrive(nc, soon_loaded, 16 * len(soon))
            normalise(nc, "n1_", x, idn, root_both, zT, second=root_ln, out_natural=x2,
                      channel_scale=self_w["n1"][:, 0:1])
            with ExitStack() as inner:
                mi = Memory(nc, inner, "s0_")
                q_all, k_all = (mi.sb(n, [ROWS, TILES, HEADS // HG, P], F32R) for n in ("q", "k"))
                v_all = mi.sb("v", [P, TILES, D])
                project_self(nc, "q0_", self_w, zT, idn, q_all, k_all, v_all, eps[:, 1:2])
                attend_self(nc, "u0_", x2, self_w, q_all, k_all, v_all, idn, groupmask[:, :], causal_b[:, :],
                            ident_b[:, :])
            normalise(nc, "n3_", x2, idn, root_rms, zT, center=False, channel_scale=self_w["n2"][:, 0:1],
                      gate_w=self_w["gate"], logits=logits[4], then=ACT.Exp)
            experts_mixed(nc, "e0_", x, x2, self_w, zT, logits[4], rank)
        clear_spent(nc)
        normalise(nc, "n4_", x, idn, root_ln, zT, then=ACT.Exp)
        with ExitStack() as stack:
            ml = Memory(nc, stack, "a1_")
            kT_all, vT_all = ml.sb("kT", [P, 8, B * KEYS]), ml.sb("vT", [P, 8, B * KEYS])
            project_wide(nc, "p1_", wide1, ctxT, kT_all, vT_all)
            attend_wide(nc, "t1_", x, wide1, zT, kT_all, vT_all, idn, neg1, ident_b[:, :],
                        loads=load(later, later_loaded))
        with ExitStack() as stack:
            mw = Memory(nc, stack, "w1_")
            weights = StreamedExperts(nc, mw, zero[:, 0:1], 8, 4, A["L1w1"], A["L1w3"], A["L1w2"])
            z = [mw.sb(n, [P, TILES * P], F32R) for n in ("z_high", "z_low")]
            normalise(nc, "n5_", x, idn, root_ln, zT, gate_w=gate1, logits=logits[8], then=ACT.Exp, parts=z,
                      loads=weights.first_loads, meanwhile=weights.first_splits)
            experts_gated(nc, "e1_", x, z, logits[8], rank, weights, idn, gates_dram, zT)
        early.close()
        clear_spent(nc)
        normalise(nc, "n6_", x, idn, root_ln, zT, then=ACT.Exp)
        with ExitStack() as stack:
            ml = Memory(nc, stack, "a2_")
            qT_all, kT_all, v2_all = ml.sb("qT", [P, TILES * P]), ml.sb("kT", [P, B * KEYS]), ml.sb("v2", [P, B, D])
            project_small(nc, "p2_", small2, zT, ctx2T, idn, qT_all, kT_all, v2_all)
            attend_small(nc, "t2_", x, small2, qT_all, kT_all, v2_all, idn, hm, HD ** -0.5)
        many = ManyExperts(nc, m, 66 * 64, A["L3eg"], A["L3eu"], A["L3ed"])
        with ExitStack() as stack:
            mw = Memory(nc, stack, "w2_")
            weights = StreamedExperts(nc, mw, zero[:, 0:1], 8, 2, A["L2w1"], A["L2w3"], A["L2w2"])
            z = [mw.sb(n, [P, TILES * P], F32R) for n in ("z_high", "z_low")]
            normalise(nc, "n7_", x, idn, root_ln, zT, gate_w=gate2, logits=logits[8], then=ACT.Exp, parts=z,
                      loads=weights.first_loads, meanwhile=weights.first_splits)
            experts_gated(nc, "e2_", x, z, logits[8], rank, weights, idn, gates_dram, zT,
                          lambda sp: many.load_piece(sp, 0))
        clear_spent(nc)
        many.make_room(m)
        normalise(nc, "n8_", x, idn, root_ln, zT, then=ACT.Exp, before=lambda act: many.make_high(act, 0))
        attend_two_way(nc, "t3_", x, two_way, zT, ctxT, ctx_nat, idn, ones[:, :], many)
        z = [m.sb(n, [P, TILES * P], F32R) for n in ("z_high", "z_low")]
        logits[64] = m.sb("logits64", [P, TILES, 64])
        normalise(nc, "n9_", x, idn, root_ln, zT, gate_w=gate3, logits=logits[64], then=ACT.Sigmoid, parts=z)
        experts_many(nc, "e3_", x, z, logits[64], bias3[:, :], many, idn,
                     gates_dram, zT)
        finish()


def lay_out(i):
    import numpy as np

    c = lambda a: np.ascontiguousarray(a)
    rows = lambda v: c(np.broadcast_to(v.reshape(1, -1), (P, v.size)))
    col = lambda v: c(v.reshape(-1, 1))
    split = lambda a: c(a.reshape(-1, P, a.shape[-1]).transpose(1, 0, 2))
    f = {k: np.asarray(v) for k, v in i.items()}
    a = {"x": f["x"].reshape(-1, D), "ctx": f["ctx_1024"].reshape(-1, D),
         "mask0": f["mask_1x1xSxS2_fk1"].reshape(S, KEYS),
         "mask1": f["mask_BxSxS2_bk1"].reshape(B * S, KEYS),
         "ident": np.eye(P, dtype=np.float32),
         "headmask": np.repeat(np.eye(HEADS, dtype=np.float32), HD, axis=0),
         "groupmask": np.tile(np.repeat(np.eye(HG, dtype=np.float32), HD, axis=0), (3, 1)),
         "rank": np.tile(np.arange(8, 0, -1, dtype=np.float32), (P, 1)),
         "causal": np.tril(np.ones((P, P), np.float32))}
    for n, b in (("q", "q"), ("k", "k")):
        a["L0w" + n], a["L0b" + b] = f["L0_xattn_w" + n], col(f["L0_xattn_b" + b])
        a["L2w" + n], a["L2b" + b] = c(f["L2_xattn_W" + n].T), col(f["L2_xattn_b" + b])
    for n in "vo":
        a["L0w" + n], a["L0b" + n] = f["L0_xattn_w" + n], rows(f["L0_xattn_b" + n])
        a["L2w" + n], a["L2b" + n] = c(f["L2_xattn_W" + n].T), rows(f["L2_xattn_b" + n])
    g = lambda n: f["L0_ffn_" + n]
    a["L0fwqkv"] = c(np.concatenate([g("wq").T, g("wk").T, g("wv").T], axis=1))
    a["L0fwo"] = c(g("wo").T)
    a["L0fqn"], a["L0fkn"] = col(np.tile(g("qn_w"), ROWS // HD)), col(np.tile(g("kn_w"), ROWS // HD))
    a["L0fn1"], a["L0fn2"] = col(g("n1_w")), col(g("n2_w"))
    a["L0fgate"] = c(g("gate_w").T)
    for n in ("e0_up", "e0_down", "e1_w1", "e1_w2", "e1_down", "e2_l1", "e2_l2", "e2_l3", "e2_l4", "e3_down",
              "e3_up", "e3_out"):
        a["L0f" + n] = split(g(n).T)
    for n in "qkv":
        a["L1w" + n] = c(f["L1_xattn_w" + n].transpose(1, 0, 2).reshape(D, 1024))
        a["L1b" + n] = c(f["L1_xattn_b" + n].reshape(8, P).T)
    a["L1wo"], a["L1bo"] = split(f["L1_xattn_wo"]), rows(f["L1_xattn_bo"])
    a["gate1"], a["gate2"] = f["L1_ffn_gate_w"], c(f["L2_ffn_Wg"].T)
    down = lambda w: c(w.reshape(8, -1, P, D).transpose(0, 2, 1, 3).reshape(8, P, -1))
    a["L1w1"], a["L1w3"], a["L1w2"] = f["L1_ffn_w1"], f["L1_ffn_w3"], down(f["L1_ffn_w2"])
    a["L2w1"], a["L2w3"] = c(f["L2_ffn_W1"].transpose(0, 2, 1)), c(f["L2_ffn_W2"].transpose(0, 2, 1))
    a["L2w2"] = down(f["L2_ffn_W3"].transpose(0, 2, 1))
    for n in ("w_cq", "w_c", "w_q"):
        a["L3" + n] = col(f["L3_xattn_" + n])
    for n in ("b_cq", "b_c", "b_q"):
        a["L3" + n] = c(np.broadcast_to(f["L3_xattn_" + n].reshape(1, 1), (P, 1)))
    a["L3wl"], a["L3b_l"] = split(f["L3_xattn_W_l"].T), rows(f["L3_xattn_b_l"])
    a["gate3"], a["bias3"] = c(f["L3_ffn_gate_w"].T), rows(f["L3_ffn_gate_bias"])
    for n in ("g", "u"):
        a["L3e" + n] = c(np.concatenate([f[f"L3_ffn_e{n}_w"].transpose(2, 0, 1).reshape(D, -1),
                                         f[f"L3_ffn_s{n}_w"].T], axis=1))
    down = np.concatenate([f["L3_ffn_ed_w"].transpose(0, 2, 1).reshape(-1, D), f["L3_ffn_sd_w"].T])
    a["L3ed"] = split(down).reshape(P, -1)
    return a


def kernel(**inputs):
    import numpy as np
    import concourse.bacc as bacc
    from concourse.bass_utils import run_bass_kernel_spmd

    nc = bacc.Bacc("TRN2", target_bir_lowering=False, num_devices=1)
    arrays = {f"in_{n}": np.ascontiguousarray(a) for n, a in lay_out(inputs).items()}
    aps = {n[3:]: nc.dram_tensor(n, a.shape, mybir.dt.from_np(a.dtype), kind="ExternalInput").ap()
           for n, a in arrays.items()}
    out = nc.dram_tensor("out", (B * S, D), F32, kind="ExternalOutput").ap()
    build(nc, aps, out)
    r = run_bass_kernel_spmd(nc, [arrays], core_ids=[0])
    return r.results[0]["out"].reshape(B, S, D)
```
